# Optimizing a Trainium2 kernel written in Bass

```python
import numpy as np
import jax
import jax.numpy as jnp

def _softmax(x, axis=-1):
    return jax.nn.softmax(x, axis=axis)

def _gelu(x):
    return jax.nn.gelu(x, approximate=True)

def _silu(x):
    return jax.nn.silu(x)

def _sigmoid(x):
    return jax.nn.sigmoid(x)

def _layernorm(x, axis=-1, eps=1e-05):
    m = jnp.mean(x, axis=axis, keepdims=True)
    v = jnp.var(x, axis=axis, keepdims=True)
    return (x - m) / jnp.sqrt(v + eps)

def _scatter_add(tgt, idx, src, axis=0):
    return tgt.at[idx].add(src)

def _segment_sum(src, seg, n):
    return jax.ops.segment_sum(src, seg, n)
kernel_name = 'mk_sandwich_d2_jaxref_r8_ce7cf3'

def setup_inputs(seed: int=0):
    np.random.seed(seed)
    _w = jnp.asarray

    def _L0_attn_setup():
        import jax, jax.numpy as jnp
        import numpy as np
        B, S, D = (1, 256, 256)
        H, KV = (16, 4)
        NB, NV = (8, 8)
        W = 32 // NB
        QKD = W * NB
        key = jax.random.key(seed)
        ks = jax.random.split(key, 5)
        s = 0.02
        return {'hidden_states': jax.random.normal(ks[0], (B, S, D), jnp.float32), 'Wq': jax.random.normal(ks[1], (H * NB, D), jnp.float32) * s, 'Wk': jax.random.normal(ks[2], (KV * NB, D), jnp.float32) * s, 'Wv': jax.random.normal(ks[3], (KV * NV, D), jnp.float32) * s, 'Wo': jax.random.normal(ks[4], (D, H * NV), jnp.float32) * s, 'v_emb0': jnp.full((H * NV,), -1e-05, jnp.float32), 'v_emb1': jnp.full((H * NV,), 1e-05, jnp.float32), 'tau': jnp.ones((), jnp.float32)}
    _L0_attn_in = _L0_attn_setup()

    def _L0_ffn_setup():
        import jax, jax.numpy as jnp
        import numpy as np
        E4M3_MAX = 448.0

        def _quant_e4m3(t):
            amax = jnp.max(jnp.abs(t)).astype(jnp.float32)
            scale = jnp.maximum(amax / E4M3_MAX, 1e-12)
            fp8 = (t.astype(jnp.float32) / scale).astype(jnp.float8_e4m3fn)
            return (fp8, scale)

        def _scaled_mm(a_fp8, b_fp8, sa, sb):
            acc = jnp.matmul(a_fp8.astype(jnp.float32), b_fp8.astype(jnp.float32))
            return (acc * (sa * sb)).astype(jnp.bfloat16)
        key = jax.random.key(seed)
        k1, k2 = jax.random.split(key)
        x = jax.random.normal(k1, (4, 256, 256), dtype=jnp.bfloat16)
        weight = (jax.random.normal(k2, (256, 256), dtype=jnp.bfloat16) * 0.02).astype(jnp.bfloat16)
        return {'x': x, 'weight': weight}
    _L0_ffn_in = _L0_ffn_setup()

    def _L1_attn_setup():
        import jax, jax.numpy as jnp
        import numpy as np
        B, L, DM, H, N = (4, 512, 256, 32, 128)
        HD = DM // H
        key = jax.random.key(seed)
        ks = jax.random.split(key, 6)
        x = jax.random.normal(ks[0], (B, L, DM), dtype=jnp.float32)
        Wx = jax.random.normal(ks[1], (DM, 2 * N + H), dtype=jnp.float32) * 0.02
        Wg = jax.random.normal(ks[2], (DM, DM), dtype=jnp.float32) * 0.02
        bg = jnp.zeros((DM,), dtype=jnp.float32)
        Wo = jax.random.normal(ks[3], (DM, DM), dtype=jnp.float32) * 0.02
        A = -1.0 + 0.1 * jax.random.normal(ks[4], (H, N), dtype=jnp.float32)
        Dp = jnp.ones((H,), dtype=jnp.float32)
        return {'x': x, 'Wx': Wx, 'Wg': Wg, 'bg': bg, 'Wo': Wo, 'A': A, 'Dp': Dp}
    _L1_attn_in = _L1_attn_setup()

    def _L1_ffn_setup():
        import jax, jax.numpy as jnp
        import numpy as np
        B_, S, D = (2, 256, 256)
        F_ = 1024
        R = 16
        H = 16
        HD = D // H
        MOD_SCALE = 0.1
        EPS = 1e-06

        def _rmsnorm(x, w):
            v = jnp.mean(x * x, axis=-1, keepdims=True)
            return x * jax.lax.rsqrt(v + EPS) * w

        def _attention(x, Wq, Wk, Wv, Wo):
            b, s, d = x.shape
            q = (x @ Wq.T).reshape(b, s, H, HD)
            k = (x @ Wk.T).reshape(b, s, H, HD)
            v = (x @ Wv.T).reshape(b, s, H, HD)
            scores = jnp.einsum('bqhd,bkhd->bhqk', q, k) / np.sqrt(HD).astype(np.float32)
            causal = jnp.tril(jnp.ones((s, s), bool))
            scores = jnp.where(causal, scores, jnp.finfo(scores.dtype).min)
            probs = jax.nn.softmax(scores, axis=-1)
            out = jnp.einsum('bhqk,bkhd->bqhd', probs, v).reshape(b, s, d)
            return out @ Wo.T
        key = jax.random.key(seed)
        ks = jax.random.split(key, 12)
        sd = 0.02
        return {'hidden_states': jax.random.normal(ks[0], (B_, S, D), jnp.float32), 'ln1_w': jnp.ones((D,), jnp.float32), 'ln2_w': jnp.ones((D,), jnp.float32), 'Wq': jax.random.normal(ks[1], (D, D), jnp.float32) * sd, 'Wk': jax.random.normal(ks[2], (D, D), jnp.float32) * sd, 'Wv': jax.random.normal(ks[3], (D, D), jnp.float32) * sd, 'Wo': jax.random.normal(ks[4], (D, D), jnp.float32) * sd, 'A': jax.random.normal(ks[5], (D, R), jnp.float32) * (0.01 / np.sqrt(D)), 'B': jax.random.normal(ks[6], (R, F_), jnp.float32) * (0.01 / np.sqrt(R)), 'W_in_base': jax.random.normal(ks[7], (F_, D), jnp.float32) * sd, 'W_up_base': jax.random.normal(ks[8], (F_, D), jnp.float32) * sd, 'W_down': jax.random.normal(ks[9], (D, F_), jnp.float32) * sd}
    _L1_ffn_in = _L1_ffn_setup()
    _d = {'L0_attn_hidden_states': _L0_attn_in['hidden_states'], 'L0_attn_Wq': _L0_attn_in['Wq'], 'L0_attn_Wk': _L0_attn_in['Wk'], 'L0_attn_Wv': _L0_attn_in['Wv'], 'L0_attn_Wo': _L0_attn_in['Wo'], 'L0_attn_v_emb0': _L0_attn_in['v_emb0'], 'L0_attn_v_emb1': _L0_attn_in['v_emb1'], 'L0_attn_tau': _L0_attn_in['tau'], 'L0_ffn_weight': _L0_ffn_in['weight'], 'L1_attn_Wx': _L1_attn_in['Wx'], 'L1_attn_Wg': _L1_attn_in['Wg'], 'L1_attn_bg': _L1_attn_in['bg'], 'L1_attn_Wo': _L1_attn_in['Wo'], 'L1_attn_A': _L1_attn_in['A'], 'L1_attn_Dp': _L1_attn_in['Dp'], 'L1_ffn_ln1_w': _L1_ffn_in['ln1_w'], 'L1_ffn_ln2_w': _L1_ffn_in['ln2_w'], 'L1_ffn_Wq': _L1_ffn_in['Wq'], 'L1_ffn_Wk': _L1_ffn_in['Wk'], 'L1_ffn_Wv': _L1_ffn_in['Wv'], 'L1_ffn_Wo': _L1_ffn_in['Wo'], 'L1_ffn_A': _L1_ffn_in['A'], 'L1_ffn_B': _L1_ffn_in['B'], 'L1_ffn_W_in_base': _L1_ffn_in['W_in_base'], 'L1_ffn_W_up_base': _L1_ffn_in['W_up_base'], 'L1_ffn_W_down': _L1_ffn_in['W_down']}
    _x0 = _d['L0_attn_hidden_states']
    _d['L0_attn_hidden_states'] = jax.random.normal(jax.random.fold_in(jax.random.key(seed), 1), (4, 1024, 256), dtype=_x0.dtype)
    del _x0
    return _d

def reference(L0_attn_hidden_states, L0_attn_Wq, L0_attn_Wk, L0_attn_Wv, L0_attn_Wo, L0_attn_v_emb0, L0_attn_v_emb1, L0_attn_tau, L0_ffn_weight, L1_attn_Wx, L1_attn_Wg, L1_attn_bg, L1_attn_Wo, L1_attn_A, L1_attn_Dp, L1_ffn_ln1_w, L1_ffn_ln2_w, L1_ffn_Wq, L1_ffn_Wk, L1_ffn_Wv, L1_ffn_Wo, L1_ffn_A, L1_ffn_B, L1_ffn_W_in_base, L1_ffn_W_up_base, L1_ffn_W_down):

    def _L0_attn_ref(hidden_states, Wq, Wk, Wv, Wo, v_emb0, v_emb1, tau):
        import jax, jax.numpy as jnp
        import numpy as np
        B, S, D = (1, 256, 256)
        H, KV = (16, 4)
        NB, NV = (8, 8)
        W = 32 // NB
        QKD = W * NB
        bsz, seq_len, _ = hidden_states.shape
        n_rep = H // KV
        q = jnp.tanh(hidden_states @ Wq.T / tau).reshape(bsz, seq_len, H, NB).transpose(0, 2, 1, 3)
        k = jnp.tanh(hidden_states @ Wk.T / tau).reshape(bsz, seq_len, KV, NB).transpose(0, 2, 1, 3)
        v = jax.nn.sigmoid(hidden_states @ Wv.T / tau).reshape(bsz, seq_len, KV, NV).transpose(0, 2, 1, 3)
        pad = ((0, 0), (0, 0), (W - 1, 0), (0, 0))
        qp = jnp.pad(q, pad)
        kp = jnp.pad(k, pad)
        idx = jnp.arange(seq_len)[:, None] + jnp.arange(W)[None, :]
        qw = qp[:, :, idx, :].reshape(bsz, H, seq_len, QKD)
        kw = kp[:, :, idx, :].reshape(bsz, KV, seq_len, QKD)
        vs = jnp.concatenate([v[:, :, 1:, :], jnp.zeros_like(v[:, :, :1, :])], axis=2)
        kw = jnp.repeat(kw, n_rep, axis=1)
        vs = jnp.repeat(vs, n_rep, axis=1)
        r = jnp.arange(seq_len, dtype=hidden_states.dtype)
        bias = r[None, :] / (r[:, None] + 1)
        mask = jnp.tril(jnp.ones((seq_len, seq_len), bool), -1)
        bias = jnp.where(mask, bias, -jnp.inf) / tau
        scale = 1.0 / np.sqrt(QKD) / tau
        scores = jnp.einsum('bhqd,bhkd->bhqk', qw, kw) * scale + bias
        m = jnp.max(scores, axis=-1, keepdims=True)
        m = jnp.where(jnp.isfinite(m), m, 0.0)
        e = jnp.exp(scores - m)
        denom = jnp.sum(e, axis=-1, keepdims=True)
        p = jnp.where(denom > 0, e / jnp.where(denom > 0, denom, 1.0), 0.0)
        out = jnp.einsum('bhqk,bhkd->bhqd', p, vs)
        out = out.transpose(0, 2, 1, 3).reshape(bsz, seq_len, H * NV)
        out = out * v_emb1 + (1.0 - out) * v_emb0
        return out @ Wo.T

    def _L0_ffn_ref(x, weight):
        import jax, jax.numpy as jnp
        import numpy as np
        E4M3_MAX = 448.0

        def _quant_e4m3(t):
            amax = jnp.max(jnp.abs(t)).astype(jnp.float32)
            scale = jnp.maximum(amax / E4M3_MAX, 1e-12)
            fp8 = (t.astype(jnp.float32) / scale).astype(jnp.float8_e4m3fn)
            return (fp8, scale)

        def _scaled_mm(a_fp8, b_fp8, sa, sb):
            acc = jnp.matmul(a_fp8.astype(jnp.float32), b_fp8.astype(jnp.float32))
            return (acc * (sa * sb)).astype(jnp.bfloat16)
        w_fp8, w_scale = _quant_e4m3(weight)
        x2d = x.reshape(-1, x.shape[-1])
        x_fp8, x_scale = _quant_e4m3(x2d)
        out2d = _scaled_mm(x_fp8, w_fp8.T, x_scale, w_scale)
        return out2d.reshape(*x.shape[:-1], out2d.shape[-1])

    def _L1_attn_ref(x, Wx, Wg, bg, Wo, A, Dp):
        import jax, jax.numpy as jnp
        import numpy as np
        B, L, DM, H, N = (4, 512, 256, 32, 128)
        HD = DM // H
        b, l, dm = x.shape
        h, n = A.shape
        hd = dm // h
        ssm_params = x @ Wx
        B_ssm = ssm_params[..., :n]
        C_ssm = ssm_params[..., n:2 * n]
        delta_bias = ssm_params[..., 2 * n:]
        gate = jax.nn.sigmoid(x @ Wg + bg)
        delta = jax.nn.softplus(delta_bias[..., :, None] + B_ssm[..., None, :])
        d_seq = jnp.moveaxis(delta, 1, 0)
        h0 = jnp.zeros((b, h, n), dtype=x.dtype)

        def step(hst, d_t):
            hst = jnp.exp(d_t * A) * hst + d_t * d_t
            return (hst, hst)
        _, hs = jax.lax.scan(step, h0, d_seq)
        hs = jnp.moveaxis(hs, 0, 1)
        y = jnp.einsum('blhn,bln->blh', hs, C_ssm)
        xg = x.reshape(b, l, h, hd)
        yh = y[..., None] + xg * Dp[None, None, :, None]
        y_full = yh.reshape(b, l, dm) * gate
        return y_full @ Wo

    def _L1_ffn_ref(hidden_states, ln1_w, ln2_w, Wq, Wk, Wv, Wo, A, B, W_in_base, W_up_base, W_down):
        import jax, jax.numpy as jnp
        import numpy as np
        B_, S, D = (2, 256, 256)
        F_ = 1024
        R = 16
        H = 16
        HD = D // H
        MOD_SCALE = 0.1
        EPS = 1e-06

        def _rmsnorm(x, w):
            v = jnp.mean(x * x, axis=-1, keepdims=True)
            return x * jax.lax.rsqrt(v + EPS) * w

        def _attention(x, Wq, Wk, Wv, Wo):
            b, s, d = x.shape
            q = (x @ Wq.T).reshape(b, s, H, HD)
            k = (x @ Wk.T).reshape(b, s, H, HD)
            v = (x @ Wv.T).reshape(b, s, H, HD)
            scores = jnp.einsum('bqhd,bkhd->bhqk', q, k) / np.sqrt(HD).astype(np.float32)
            causal = jnp.tril(jnp.ones((s, s), bool))
            scores = jnp.where(causal, scores, jnp.finfo(scores.dtype).min)
            probs = jax.nn.softmax(scores, axis=-1)
            out = jnp.einsum('bhqk,bkhd->bqhd', probs, v).reshape(b, s, d)
            return out @ Wo.T
        residual = hidden_states
        x = _rmsnorm(hidden_states, ln1_w)
        attn = _attention(x, Wq, Wk, Wv, Wo)
        mod = MOD_SCALE * jnp.tanh(attn @ A)
        h = _rmsnorm(residual, ln2_w)
        gate_pre = h @ W_in_base.T + mod * (h @ A) @ B
        gate = jax.nn.silu(gate_pre)
        up = h @ W_up_base.T
        mlp_out = gate * up @ W_down.T
        return residual + mlp_out
    x = L0_attn_hidden_states
    x = x + _layernorm(_L0_attn_ref(_layernorm(x, axis=-1), L0_attn_Wq, L0_attn_Wk, L0_attn_Wv, L0_attn_Wo, L0_attn_v_emb0, L0_attn_v_emb1, L0_attn_tau), axis=-1)
    x = x + _layernorm(_L0_ffn_ref(_layernorm(x, axis=-1), L0_ffn_weight), axis=-1)
    x = x + _layernorm(_L1_attn_ref(_layernorm(x, axis=-1), L1_attn_Wx, L1_attn_Wg, L1_attn_bg, L1_attn_Wo, L1_attn_A, L1_attn_Dp), axis=-1)
    x = x + _layernorm(_L1_ffn_ref(_layernorm(x, axis=-1), L1_ffn_ln1_w, L1_ffn_ln2_w, L1_ffn_Wq, L1_ffn_Wk, L1_ffn_Wv, L1_ffn_Wo, L1_ffn_A, L1_ffn_B, L1_ffn_W_in_base, L1_ffn_W_up_base, L1_ffn_W_down), axis=-1)
    return x

_drawn_inputs = setup_inputs


def setup_inputs(seed=0):
    import zlib

    import numpy as np

    out = dict(_drawn_inputs(seed))
    spreads = {'L0_attn_v_emb0': (-9.999999747378752e-06, 0.6),
     'L0_attn_v_emb1': (9.999999747378752e-06, 0.6),
     'L1_attn_bg': (0.0, 0.288),
     'L1_attn_Dp': (1.0, 0.2),
     'L1_ffn_ln1_w': (1.0, 0.6),
     'L1_ffn_ln2_w': (1.0, 0.6)}
    factors = {'L0_attn_Wq': 200.0,
     'L0_attn_Wk': 200.0,
     'L0_attn_Wv': 200.0,
     'L0_attn_Wo': 33.262,
     'L1_ffn_Wq': 200.0,
     'L1_ffn_Wk': 200.0,
     'L1_ffn_Wv': 200.0,
     'L1_ffn_Wo': 200.0,
     'L1_ffn_A': 200.0,
     'L1_ffn_B': 200.0,
     'L1_ffn_W_in_base': 4.349,
     'L1_ffn_W_up_base': 4.309,
     'L1_ffn_W_down': 4.306}
    for name, (base, spread) in spreads.items():
        noise = np.random.default_rng([zlib.crc32(name.encode()), seed]).standard_normal(out[name].shape)
        drawn = base * np.exp(spread * noise) if base else spread * noise
        out[name] = jnp.asarray(drawn.astype(out[name].dtype))
    for name, factor in factors.items():
        out[name] = (out[name] * factor).astype(out[name].dtype)
    return out
```

```python
from contextlib import ExitStack

import concourse.bass as bass
import numpy as np
from concourse import mybir

F32 = mybir.dt.float32
F16 = mybir.dt.float16
BF16 = mybir.dt.bfloat16
I32 = mybir.dt.int32
ALU = mybir.AluOpType
ACT = mybir.ActivationFunctionType
AX_X = mybir.AxisListType.X
RMAX = bass.bass_isa.ReduceOp.max
ds = bass.ds

P = 128
BATCH, S, D = 4, 1024, 256
KD = D // P
TILES = BATCH * S // P
TPB = S // P
CH = 512
TPC = CH // P
CPB = S // CH
G = 4
HG = 4
EPS = 1e-5
RMS_EPS = 1e-6
MASKED = -3e38
TAPS, NB = 4, 8
AQ, AK = 128, 32
PADT = S + TAPS
HD = 16
N, SH, SHD = 128, 32, 8
F, R = 1024, 16
FT = F // P
E4M3_MAX = 448.0
SAT = 40.0


class Core:

    def __init__(self, nc, ctx):
        self.nc, self.ctx, self.sems = nc, ctx, []

    def sem(self, name):
        self.sems.append(self.nc.alloc_semaphore(name=name))
        return self.sems[-1]

    def end_phase(self):
        self.nc.clear_and_free_semaphores(self.sems)
        self.sems = []
        self.nc.all_engine_barrier()


def sbuf(nc, ctx, name, shape, dt=F32):
    return ctx.enter_context(nc.sbuf_tensor(name, shape, dt))


def psum(nc, ctx, name, shape, dt=F32):
    return ctx.enter_context(nc.psum_tensor(name, shape, dt))


def wait_alone(eng, sem, value, tick):
    eng.wait_ge(sem, value)
    eng.sem_inc(tick, 1)


def row_stats(dve, tiles, sums, stats, summed, count, ready, tick):
    for j, tile in enumerate(tiles):
        last = dve.bn_stats(sums[:, j, :], tile)
    last.then_inc(summed, 1)
    wait_alone(dve, summed, count, tick)
    for j in range(len(tiles)):
        last = dve.bn_aggr(stats[:, j, :], sums[:, j, :])
    last.then_inc(ready, 1)


def rows_rstd(pool, variance_ok, nth, rstd, variance, eps, power, added, count, ready, tick):
    wait_alone(pool, variance_ok, nth, tick)
    pool.tensor_scalar(rstd, variance, eps, None, ALU.add).then_inc(added, 1)
    pool.wait_ge(added, count)
    pool.tensor_tensor(rstd, rstd, power[:, :], ALU.pow).then_inc(ready, 1)


def phase_load(c, a):
    nc = c.nc
    loaded, made = c.sem("loaded"), c.sem("made")
    with nc.Block() as block:

        @block.sync
        def _(sp):
            for b in range(BATCH):
                sp.dma_start(c.x[:, b * TPB * D:(b + 1) * TPB * D].rearrange("p (n d) -> p n d", d=D),
                             a["x"][b].rearrange("(n p) d -> p n d", p=P)).then_inc(loaded, 16)
            sp.dma_start(c.ident[:, :], a["ident"]).then_inc(loaded, 16)
            sp.dma_start(c.masksf[:, :, :], a["masks"].rearrange("m p q -> p m q")).then_inc(loaded, 16)
            sp.wait_ge(loaded, 16 * (BATCH + 2))

        @block.vector
        def _(dve):
            dve.wait_ge(loaded, 16 * (BATCH + 2))
            dve.memset(c.power[:, :], -0.5)
            dve.tensor_copy(c.identb[:, :], c.ident[:, :])
            dve.tensor_copy(c.masks[:, :, :], c.masksf[:, :, :])


def phase_qkv_first(c, a, d):
    nc = c.nc
    with ExitStack() as ctx:
        wq = sbuf(nc, ctx, "p1_wq", [P, KD, AQ])
        wk = sbuf(nc, ctx, "p1_wk", [P, KD, AK])
        wv = sbuf(nc, ctx, "p1_wv", [P, KD, AK])
        sums = sbuf(nc, ctx, "p1_sums", [P, CPB, TPC, 6])
        stats = sbuf(nc, ctx, "p1_stats", [P, CPB, TPC, 2])
        rstd = sbuf(nc, ctx, "p1_rstd", [P, CPB, TPC])
        xn = sbuf(nc, ctx, "p1_xn", [P, CPB, TPC * D])
        xT = sbuf(nc, ctx, "p1_xT", [P, CPB, KD, CH])
        qf = sbuf(nc, ctx, "p1_qf", [P, CPB, CH])
        kf = sbuf(nc, ctx, "p1_kf", [AK, CPB, CH])
        vf = sbuf(nc, ctx, "p1_vf", [P, CPB, TPC, AK])
        qp = sbuf(nc, ctx, "p1_qp", [P, CPB, 2, CH], F16)
        kp = sbuf(nc, ctx, "p1_kp", [AK, CPB, 2, CH], F16)
        vx = sbuf(nc, ctx, "p1_vx", [P, CPB, TPC, G, NB + 1])
        zeros = sbuf(nc, ctx, "p1_zeros", [P, 2, BATCH, TAPS], F16)
        last_v = sbuf(nc, ctx, "p1_last_v", [16, NB + 1])
        psT = [psum(nc, ctx, f"p1_psT{i}", [P, KD, CH]) for i in range(CPB)]
        psQ = psum(nc, ctx, "p1_psQ", [P, CH])
        psK = psum(nc, ctx, "p1_psK", [AK, CH])
        psV = psum(nc, ctx, "p1_psV", [P, TPC, AK])
        w_in, itau = c.sem("p1_w_in"), c.sem("p1_itau")
        const_ok = c.sem("p1_const_ok")
        summed, stats_ok, rstd_ok, xn_ok = (c.sem("p1_" + n) for n in ("summed", "stats_ok", "rstd_ok", "xn_ok"))
        added = c.sem("p1_added")
        tick, tick_pool = c.sem("p1_tick"), c.sem("p1_tick_pool")
        turned, xT_ok, proj_ok = (c.sem("p1_" + n) for n in ("turned", "xT_ok", "proj_ok"))
        tanh_ok, split_ok, parts_ok, stored = (c.sem("p1_" + n) for n in ("tanh_ok", "split_ok", "parts_ok", "stored"))

        with nc.Block() as block:

            @block.sync
            def _(sp):
                for w, src in ((wq, a["wq1"]), (wk, a["wk1"]), (wv, a["wv1"])):
                    sp.dma_start(w[:, :, :], src.rearrange("(k p) n -> p k n", p=P)).then_inc(w_in, 16)
                sp.dma_start(c.tau[:, :], a["tau"].partition_broadcast(P)).then_inc(w_in, 16)
                sp.wait_ge(const_ok, 1)
                sp.dma_start(d["q1"][:, :, :, 0:TAPS].rearrange("e b r t -> r e b t"), zeros[:, :, :, :]).then_inc(stored, 16)
                sp.dma_start(d["k1"][:, :, :, 0:TAPS].rearrange("e b r t -> r e b t"), zeros[0:AK, :, :, :]).then_inc(stored, 16)
                sp.dma_start(d["v1"][:, P - 1:P, TPB:TPB + 1, :].rearrange("n p k d -> (n p k) d"),
                             last_v[:, :]).then_inc(stored, 16)
                sp.wait_ge(stored, 48)
                with sp.Fori(0, BATCH) as b:
                    for ch in range(CPB):
                        sp.wait_ge(parts_ok, b * CPB + ch + 1)
                        t0 = TAPS - 1 + ch * CH
                        for e in range(2):
                            sp.dma_start(d["q1"][e, ds(b, 1), :, t0:t0 + CH].rearrange("b r t -> (b r) t"),
                                         qp[:, ch, e, :]).then_inc(stored, 16)
                            sp.dma_start(d["k1"][e, ds(b, 1), :, t0:t0 + CH].rearrange("b r t -> (b r) t"),
                                         kp[:, ch, e, :]).then_inc(stored, 16)
                        v1b = d["v1"][ds(b * G, G)]
                        for g in range(G):
                            sp.dma_start(v1b[g, 0:P - 1, ch * TPC + 1:ch * TPC + TPC + 1, :], vx[1:P, ch, :, g, :]).then_inc(stored, 16)
                            sp.dma_start(v1b[g, P - 1:P, ch * TPC:ch * TPC + TPC, :], vx[0:1, ch, :, g, :]).then_inc(stored, 16)
                sp.wait_ge(stored, 48 + 16 * 12 * BATCH * CPB)

            @block.vector
            def _(dve):
                dve.memset(zeros[:, :, :, :], 0.0)
                dve.memset(last_v[:, :], 1.0)
                dve.memset(vx[:, :, :, :, :], 1.0).then_inc(const_ok, 1)
                dve.wait_ge(w_in, 64)
                dve.reciprocal(c.itau[:, 0:1], c.tau[:, :]).then_inc(itau, 1)
                dve.wait_ge(itau, 1)
                dve.tensor_scalar(c.itau[:, 1:2], c.itau[:, 0:1], 0.5, None, ALU.mult).then_inc(itau, 1)
                dve.tensor_scalar(c.itau[:, 2:3], c.itau[:, 0:1], (TAPS * NB) ** -0.5, None, ALU.mult)
                with dve.Fori(0, BATCH) as b:
                    for ch in range(CPB):
                        n = b * CPB + ch
                        at = (b * TPB + ch * TPC) * D
                        row_stats(dve, [c.x[:, ds(at + j * D, D)] for j in range(TPC)], sums[:, ch], stats[:, ch], summed, n + 1, stats_ok, tick)
                        dve.wait_ge(rstd_ok, n + 1)
                        dve.wait_ge(turned, n + 1)
                        for j in range(TPC):
                            last = dve.tensor_scalar(xn[:, ch, j * D:(j + 1) * D], c.x[:, ds(at + j * D, D)],
                                                     stats[:, ch, j, 0:1], rstd[:, ch, j:j + 1], ALU.subtract, ALU.mult)
                        last.then_inc(xn_ok, 1)
                        dve.wait_ge(tanh_ok, n + 2)
                        dve.wait_ge(stored, 48 + 192 * n)
                        dve.tensor_copy(qp[:, ch, 0, :], qf[:, ch, :])
                        dve.tensor_copy(kp[:, ch, 0, :], kf[:, ch, :]).then_inc(split_ok, 1)
                        for g in range(G):
                            dve.tensor_scalar(vx[:, ch, :, g, 0:NB], vf[:, ch, :, g * NB:(g + 1) * NB], 0.5, 0.5, ALU.mult, ALU.add)
                        dve.wait_ge(split_ok, n + 1)
                        dve.tensor_tensor(qp[:, ch, 1, :], qf[:, ch, :], qp[:, ch, 0, :], ALU.subtract)
                        dve.tensor_tensor(kp[:, ch, 1, :], kf[:, ch, :], kp[:, ch, 0, :], ALU.subtract).then_inc(parts_ok, 1)

            @block.gpsimd
            def _(pool):
                with pool.Fori(0, BATCH) as b:
                    for ch in range(CPB):
                        rows_rstd(pool, stats_ok, b * CPB + ch + 1, rstd[:, ch, :], stats[:, ch, :, 1], EPS, c.power, added, b * CPB + ch + 1, rstd_ok, tick_pool)

            @block.tensor
            def _(pe):
                pe.sem_inc(turned, 2)
                pe.wait_ge(w_in, 64)
                with pe.Fori(0, BATCH) as b:
                    for ch in range(CPB):
                        n = b * CPB + ch
                        pe.wait_ge(xn_ok, n + 1)
                        for j in range(TPC):
                            for k in range(KD):
                                last = pe.transpose(psT[ch][:, k, j * P:(j + 1) * P], xn[:, ch, j * D + k * P:j * D + (k + 1) * P], c.ident[:, :])
                        last.then_inc(turned, 1)
                        pe.wait_ge(xT_ok, n + 1)
                        pe.wait_ge(tanh_ok, n + 1)
                        for k in range(KD):
                            pe.matmul(psQ[:, :], wq[:, k, :], xT[:, ch, k, :], start=k == 0, stop=k == KD - 1)
                        for k in range(KD):
                            pe.matmul(psK[:, :], wk[:, k, :], xT[:, ch, k, :], start=k == 0, stop=k == KD - 1)
                        for j in range(TPC):
                            for k in range(KD):
                                last = pe.matmul(psV[:, j, :], xT[:, ch, k, j * P:(j + 1) * P], wv[:, k, :], start=k == 0, stop=k == KD - 1)
                        last.then_inc(proj_ok, 1)

            @block.scalar
            def _(act):
                act.preload_act_table_set("exp_and_others")
                act.sem_inc(tanh_ok, 1)
                act.wait_ge(itau, 2)
                with act.Fori(0, BATCH) as b:
                    for ch in range(CPB):
                        n = b * CPB + ch
                        act.wait_ge(turned, n + 3)
                        act.activation(xT[:, ch, :, :], psT[ch][:, :, :], ACT.Copy).then_inc(xT_ok, 1)
                        act.wait_ge(proj_ok, n + 1)
                        act.activation(qf[:, ch, :], psQ[:, :], ACT.Tanh, scale=c.itau[:, 0:1])
                        act.activation(kf[:, ch, :], psK[:, :], ACT.Tanh, scale=c.itau[0:AK, 0:1])
                        act.activation(vf[:, ch, :, :], psV[:, :, :], ACT.Tanh, scale=c.itau[:, 1:2]).then_inc(tanh_ok, 1)


def max_tiles():
    halves = []
    for tiles in (range(0, TPC), range(TPC, TPB)):
        out = []
        for qt in tiles:
            for half in range(qt // TPC + 1):
                keys = min(CH, (qt + 1) * P - half * CH)
                heads = {1: 4, 2: 2}.get(keys // P, 1)
                for h in range(0, HG, heads):
                    out.append((qt, half, h, heads, half * CH, keys, half == qt // TPC))
        halves.append(out)
    return halves


MAX_TILES = max_tiles()
MAX_COUNT = len(MAX_TILES[0]) + len(MAX_TILES[1])
UNITS = [(qc, kt, max(0, kt - qc * TPC) * P) for qc in range(CPB) for kt in range((qc + 1) * TPC)]
NU = len(UNITS)


def group_order(g, maxima):
    width = np.cumsum([CH - q0 for _, _, q0 in UNITS])
    order, taken = [], 0
    for u in range(NU):
        upto = min(MAX_COUNT, -(-MAX_COUNT * int(width[u]) // int(width[NU - 2]))) if maxima else 0
        some, taken = [("max", m) for m in range(taken, upto)], upto
        if u + 1 < NU:
            scores = [("scores", 2 * (u + 1) + pair) for pair in range(2)]
        else:
            scores = [("next", pair) for pair in range(2)] if maxima else []
        half = -(-len(some) // 2)
        order += scores[0:1] + some[0:1] + scores[1:2] + some[1:half] + [("values", u)] + some[half:]
        if u == 0 and g > 0:
            order += [("turn", -1), ("divide", -1)]
        if maxima and u == 5:
            order.append(("finish", 0))
        if maxima and u == 6:
            order += [("turn_max", 0), ("split", 0)]
        if maxima and u == NU - 2:
            order.append(("finish", 1))
        if u == TPC - 1:
            order.append(("evict", 0))
        if u == TPC:
            order += [("turn", 0), ("divide", 0)]
    order.append(("evict", 1))
    if maxima:
        order += [("turn_max", 1), ("split", 1)]
    return order + ([("turn", 1), ("divide", 1)] if g == G - 1 else [])


def first_order():
    done = len(MAX_TILES[0])
    return ([("max", m) for m in range(done)] + [("finish", 0), ("turn_max", 0), ("split", 0)]
            + [("max", m) for m in range(done, MAX_COUNT)] + [("finish", 1), ("turn_max", 1), ("split", 1)]
            + [("next", 0), ("next", 1)])


def turns_before(b, g):
    return 2 + 4 * G * b + (4 * g - 1 if g else 0)


def phase_attention(c, name, dt, q_loads, k_loads, v_load, m_scr, consts, shared_keys, dim, bias_rows,
                    m_parts, scale, clip, mask_k, mask_q, out_row):
    nc = c.nc
    MR = 96 + bias_rows
    ROWS = MR + m_parts
    M = dim + 1
    KH = 1 if shared_keys else HG
    with ExitStack() as ctx:
        Q = [sbuf(nc, ctx, f"{name}_Q{g}", [P, HG, S], dt) for g in range(G)]
        K = [sbuf(nc, ctx, f"{name}_K{g}", [P, KH, S], dt) for g in range(G)]
        V = [sbuf(nc, ctx, f"{name}_V{g}", [P, TPB, KH, M]) for g in range(G)]
        E = [[sbuf(nc, ctx, f"{name}_E{i}{j}", [P, 2, CH]) for j in range(2)] for i in range(2)]
        OT = sbuf(nc, ctx, name + "_OT", [P, CH])
        den = sbuf(nc, ctx, name + "_den", [P, 2, TPC, HG])
        mx = sbuf(nc, ctx, name + "_mx", [P, 2, HG, TPB])
        mall = sbuf(nc, ctx, name + "_mall", [P, HG, TPC])
        nm = sbuf(nc, ctx, name + "_nm", [P, 2, HG, TPC])
        res = sbuf(nc, ctx, name + "_res", [HG * TPC, 2, P])
        mp = sbuf(nc, ctx, name + "_mp", [HG * TPC, 2, m_parts, P], dt)
        clear = sbuf(nc, ctx, name + "_clear", [P, CH], BF16)
        psM = [psum(nc, ctx, f"{name}_psM{i}", [P, CH]) for i in range(2)]
        psS = [psum(nc, ctx, f"{name}_psS{i}", [P, 2, CH]) for i in range(2)]
        psO = psum(nc, ctx, name + "_psO", [P, CH])
        psX = psum(nc, ctx, name + "_psX", [P, CH])
        const_in, clear_ok = c.sem(name + "_const_in"), c.sem(name + "_clear_ok")
        stack_in = [c.sem(f"{name}_stack_in{g}") for g in range(G)]
        m_out = [c.sem(f"{name}_m_out{i}") for i in range(2)]
        m_in = [[c.sem(f"{name}_m_in{g}{i}") for i in range(2)] for g in range(G)]
        max_ready, max_taken = c.sem(name + "_max_ready"), c.sem(name + "_max_taken")
        m_all, nm_ok, split_ok, mp_ok = (c.sem(f"{name}_{n}") for n in ("m_all", "nm_ok", "split_ok", "mp_ok"))
        x_ready, x_taken = c.sem(name + "_x_ready"), c.sem(name + "_x_taken")
        s_ready, e_ready, pv_done, o_copied = (c.sem(f"{name}_{n}") for n in ("s_ready", "e_ready", "pv_done", "o_copied"))
        den_ok = c.sem(name + "_den_ok")
        LOADS = len(q_loads(0, 0)) + len(k_loads(0, 0)) + 1

        with nc.Block() as block:

            @block.sync
            def _(sp):
                for dst, src in consts(Q, K):
                    sp.dma_start(dst, src).then_inc(const_in, 16)

                def load(b, g):
                    for rows, src in q_loads(b, g):
                        sp.dma_start(Q[g][rows[0]:rows[1], :, :], src).then_inc(stack_in[g], 16)
                    for rows, src in k_loads(b, g):
                        sp.dma_start(K[g][rows[0]:rows[1], :, :], src).then_inc(stack_in[g], 16)
                    sp.dma_start(V[g][:, :, :, :], v_load(b, g)).then_inc(stack_in[g], 16)

                def maxima(b, g, n):
                    for i in range(2):
                        sp.wait_ge(mp_ok, 2 * n + i + 1)
                        sp.dma_start(m_scr[g, i].rearrange("e r q -> r e q"), mp[:, i, :, :]).then_inc(m_out[i], 16)
                        sp.wait_ge(m_out[i], 16 * (n + 2))
                        sp.dma_start(Q[g][MR:ROWS, :, i * CH:(i + 1) * CH],
                                     m_scr[g, i].rearrange("e (h j) q -> e h (j q)", h=HG)).then_inc(m_in[g][i], 16)

                for i in range(2):
                    sp.sem_inc(m_out[i], 16)
                for g in range(G):
                    load(0, g)
                maxima(0, 0, 0)

                def batch(b, last):
                    for g in range(G):
                        n = b * G + g
                        if not (last and g == G - 1):
                            maxima(b + (g == G - 1), (g + 1) % G, n + 1)
                        if not last:
                            sp.wait_ge(pv_done, 2 + (n + 1) * NU)
                            load(b + 1, g)

                with sp.Fori(0, BATCH - 1) as b:
                    batch(b, False)
                batch(BATCH - 1, True)

            @block.tensor
            def _(pe):
                pe.sem_inc(pv_done, 2)
                pe.wait_ge(clear_ok, 1)
                pe.matmul(psO[:, :], clear[:, 0:P], clear[:, :], start=True, stop=True)
                pe.wait_ge(const_in, 16 * len(consts(Q, K)))

                def scores(n, b, g, u, pair):
                    qc, kt, q0 = UNITS[u]
                    if kt == 0 and pair == 0:
                        pe.wait_ge(m_in[g][qc], 16 * (b + 1))
                    pe.wait_ge(e_ready, 2 * (n * NU + u) + pair + 1)
                    for h in range(2):
                        head = 2 * pair + h
                        diag = kt >= qc * TPC
                        last = pe.matmul(psS[pair][:, h, q0:CH], K[g][0:ROWS, 0 if shared_keys else head, kt * P:(kt + 1) * P],
                                         Q[g][0:ROWS, head, qc * CH + q0:(qc + 1) * CH], start=True, stop=not diag)
                        if diag:
                            last = pe.matmul(psS[pair][:, h, q0:q0 + P], c.identb[:, :], mask_k, start=False, stop=True)
                    last.then_inc(s_ready, 1)

                def slot(n, b, g, nx, nb, order, uses):
                    nxt = (g + 1) % G
                    for what, i in order:
                        if what == "scores":
                            scores(n, b, g, i // 2, i % 2)
                        elif what == "next":
                            scores(nx, nb, nxt, 0, i)
                        elif what == "max":
                            qt, half, h0, heads, k0, keys, diag = (MAX_TILES[0] + MAX_TILES[1])[i]
                            if i == 0:
                                pe.wait_ge(stack_in[nxt], 16 * LOADS * (nb + 1))
                            pe.wait_ge(max_taken, nx * MAX_COUNT + i + 1)
                            bank = psM[i % 2]
                            for h in range(heads):
                                last = pe.matmul(bank[:, h * keys:(h + 1) * keys], Q[nxt][0:MR, h0 + h, qt * P:(qt + 1) * P],
                                                 K[nxt][0:MR, 0 if shared_keys else h0 + h, k0:k0 + keys], start=True, stop=not diag)
                                if diag:
                                    last = pe.matmul(bank[:, (h + 1) * keys - P:(h + 1) * keys], c.identb[:, :], mask_q, start=False, stop=True)
                            last.then_inc(max_ready, 1)
                        elif what == "turn_max":
                            pe.wait_ge(nm_ok, 2 * nx + i + 1)
                            pe.wait_ge(x_taken, uses + 1)
                            uses = uses + 1
                            pe.transpose(psX[0:HG * TPC, 0:P], nm[:, i, :, :].rearrange("p h t -> p (h t)"), c.ident[:, :]).then_inc(x_ready, 1)
                        elif what == "values":
                            qc, kt, q0 = UNITS[i]
                            if kt == 0:
                                pe.wait_ge(o_copied, 2 * n + qc + 1)
                            pe.wait_ge(e_ready, 2 * (n * NU + i + 1) + 2)
                            for h in range(HG):
                                last = pe.matmul(psO[32 * h:32 * h + M, q0:CH], V[g][:, kt, 0 if shared_keys else h, :],
                                                 E[i % 2][h // 2][:, h % 2, q0:CH], start=kt == 0, stop=kt == (qc + 1) * TPC - 1)
                            last.then_inc(pv_done, 1)
                        elif what == "turn":
                            pe.wait_ge(o_copied, 2 * n + i + 2 if i >= 0 else 2 * n + 1)
                            pe.wait_ge(x_taken, uses + 1)
                            uses = uses + 1
                            for j in range(TPC):
                                last = pe.transpose(psX[:, j * P:(j + 1) * P], OT[:, j * P:(j + 1) * P], c.ident[:, :])
                            last.then_inc(x_ready, 1)

                slot(0, 0, G - 1, 0, 0, first_order(), 0)

                def batch(b, last):
                    for g in range(G):
                        n = b * G + g
                        slot(n, b, g, n + 1, b + (g == G - 1), group_order(g, not (last and g == G - 1)), turns_before(b, g))

                with pe.Fori(0, BATCH - 1) as b:
                    batch(b, False)
                batch(BATCH - 1, True)

            @block.scalar
            def _(act):
                act.preload_act_table_set("exp_and_others")
                act.sem_inc(e_ready, 2)

                def batch(b):
                    for g in range(G):
                        for u, (qc, kt, q0) in enumerate(UNITS):
                            k = (b * G + g) * NU + u
                            act.wait_ge(pv_done, k + 1)
                            for pair in range(2):
                                act.wait_ge(s_ready, 2 * k + pair + 1)
                                act.activation(E[u % 2][pair][:, :, q0:CH], psS[pair][:, :, q0:CH], ACT.Exp,
                                               scale=scale).then_inc(e_ready, 1)

                with act.Fori(0, BATCH) as b:
                    batch(b)

            @block.vector
            def _(dve):
                dve.memset(mx[:, 1, :, 0:TPC], MASKED)
                dve.memset(clear[:, :], 0.0).then_inc(clear_ok, 1)
                dve.wait_ge(clear_ok, 1)
                dve.sem_inc(max_taken, 2)
                dve.sem_inc(x_taken, 1)
                dve.sem_inc(o_copied, 1)

                def slot(n, b, g, nx, order, xs):
                    for what, i in order:
                        if what == "max":
                            qt, half, h0, heads, k0, keys, diag = (MAX_TILES[0] + MAX_TILES[1])[i]
                            dve.wait_ge(max_ready, nx * MAX_COUNT + i + 1)
                            dve.tensor_reduce(out=mx[:, half, h0:h0 + heads, qt],
                                              in_=psM[i % 2][:, 0:heads * keys].rearrange("p (h k) -> p h k", h=heads),
                                              axis=AX_X, op=ALU.max).then_inc(max_taken, 1)
                        elif what == "finish":
                            done = len(MAX_TILES[0]) if i == 0 else MAX_COUNT
                            dve.wait_ge(max_taken, 2 + nx * MAX_COUNT + done)
                            dve.tensor_tensor(mall[:, :, :], mx[:, 0, :, i * TPC:(i + 1) * TPC],
                                              mx[:, 1, :, i * TPC:(i + 1) * TPC], ALU.max).then_inc(m_all, 1)
                            dve.wait_ge(m_all, 2 * nx + i + 1)
                            dve.tensor_scalar(nm[:, i, :, :], mall[:, :, :], clip, -1.0, ALU.max, ALU.mult).then_inc(nm_ok, 1)
                        elif what == "split":
                            xs = xs + 1
                            dve.wait_ge(x_ready, xs)
                            dve.wait_ge(m_out[i], 16 * (nx + 1))
                            src = psX[0:HG * TPC, 0:P]
                            for e in range(m_parts):
                                w = 2 * m_parts - 1
                                dve.tensor_copy(mp[:, i, e, :], src).then_inc(split_ok, 1)
                                if e + 1 < m_parts:
                                    dve.wait_ge(split_ok, (2 * nx + i) * w + 2 * e + 1)
                                    dve.tensor_tensor(res[:, e % 2, :], src, mp[:, i, e, :], ALU.subtract).then_inc(split_ok, 1)
                                    dve.wait_ge(split_ok, (2 * nx + i) * w + 2 * e + 2)
                                    src = res[:, e % 2, :]
                            dve.wait_ge(split_ok, (2 * nx + i + 1) * w)
                            dve.sem_inc(mp_ok, 1)
                            dve.sem_inc(x_taken, 1)
                        elif what == "evict":
                            dve.wait_ge(pv_done, 2 + n * NU + (TPC if i == 0 else NU))
                            dve.tensor_copy(OT[:, :], psO[:, :]).then_inc(o_copied, 1)
                        elif what == "divide":
                            xs = xs + 1
                            dve.wait_ge(x_ready, xs)
                            turned = psX[:, :].rearrange("p (j h e) -> p j h e", j=TPC, h=HG)
                            dve.tensor_scalar(den[:, 0, :, :], turned[:, :, :, M - 1], 1e-30, None, ALU.max).then_inc(den_ok, 1)
                            dve.wait_ge(den_ok, 2 * (2 * n + i) + 1)
                            dve.reciprocal(den[:, 1, :, :], den[:, 0, :, :]).then_inc(den_ok, 1)
                            dve.wait_ge(den_ok, 2 * (2 * n + i) + 2)
                            at, og = (i, g) if i >= 0 else (1, g - 1)
                            out = c.attn[:, ds((b * TPB + at * TPC) * out_row, TPC * out_row)].rearrange("p (j w) -> p j w", j=TPC)
                            out = out[:, :, og * HG * dim:(og + 1) * HG * dim].rearrange("p j (h e) -> p j h e", h=HG)
                            dve.tensor_tensor(out, turned[:, :, :, 0:dim],
                                              den[:, 1, :, :].unsqueeze(3).broadcast_to([P, TPC, HG, dim]), ALU.mult).then_inc(x_taken, 1)

                slot(0, 0, 0, 0, first_order(), 0)

                def batch(b, last):
                    for g in range(G):
                        n = b * G + g
                        slot(n, b, g, n + 1, group_order(g, not (last and g == G - 1)), turns_before(b, g))

                with dve.Fori(0, BATCH - 1) as b:
                    batch(b, False)
                batch(BATCH - 1, True)


def phase_out_first(c, a):
    nc = c.nc
    with ExitStack() as ctx:
        wo = sbuf(nc, ctx, "p3_wo", [P, D])
        emb = sbuf(nc, ctx, "p3_emb", [P, 3])
        at = sbuf(nc, ctx, "p3_at", [P, CPB, TPC * AQ])
        aT = sbuf(nc, ctx, "p3_aT", [P, CPB, CH])
        sums = sbuf(nc, ctx, "p3_sums", [P, 2, TPC, 6])
        stats = sbuf(nc, ctx, "p3_stats", [P, 2, TPC, 2])
        rstd = sbuf(nc, ctx, "p3_rstd", [P, 2, TPC])
        normed = sbuf(nc, ctx, "p3_normed", [P, TPC * D])
        amax = sbuf(nc, ctx, "p3_amax", [P, BATCH * CPB])
        rmax = sbuf(nc, ctx, "p3_rmax", [P, 2])
        psA = [psum(nc, ctx, f"p3_psA{i}", [P, CH]) for i in range(CPB)]
        psO = [psum(nc, ctx, f"p3_psO{i}", [P, TPC * D]) for i in range(CPB)]
        w_in, emb_ok, at_ok, turned, aT_ok, out_ok = (c.sem("p3_" + n) for n in ("w_in", "emb_ok", "at_ok", "turned", "aT_ok", "out_ok"))
        summed, stats_ok, rstd_ok, chain = (c.sem("p3_" + n) for n in ("summed", "stats_ok", "rstd_ok", "chain"))
        added = c.sem("p3_added")
        tick, tick_pool = c.sem("p3_tick"), c.sem("p3_tick_pool")
        norm_ok, amax_ok, max_ok, all_max = (c.sem("p3_" + n) for n in ("norm_ok", "amax_ok", "max_ok", "all_max"))

        with nc.Block() as block:

            @block.sync
            def _(sp):
                sp.dma_start(wo[:, :], a["wo1"]).then_inc(w_in, 16)
                sp.dma_start(emb[:, 0:1], a["emb0"]).then_inc(w_in, 16)
                sp.dma_start(emb[:, 1:2], a["emb1"]).then_inc(w_in, 16)
                sp.wait_ge(w_in, 48)

            @block.gpsimd
            def _(pool):
                with pool.Fori(0, BATCH) as b:
                    for ch in range(CPB):
                        n = b * CPB + ch
                        pool.wait_ge(turned, n + 1)
                        pool.tensor_copy(at[:, ch, :], c.attn[:, ds((b * TPB + ch * TPC) * AQ, TPC * AQ)]).then_inc(at_ok, 1)
                        for k in range(2):
                            rows_rstd(pool, stats_ok, 2 * n + k + 1, rstd[:, k, :], stats[:, k, :, 1], EPS, c.power, added, 2 * n + k + 1, rstd_ok, tick_pool)
                pool.wait_ge(max_ok, 1)
                pool.partition_all_reduce(rmax[:, 1:2], rmax[:, 0:1], P, RMAX).then_inc(all_max, 1)

            @block.tensor
            def _(pe):
                pe.sem_inc(turned, 2)
                pe.wait_ge(w_in, 48)
                with pe.Fori(0, BATCH) as b:
                    for ch in range(CPB):
                        n = b * CPB + ch
                        pe.wait_ge(at_ok, n + 1)
                        for j in range(TPC):
                            last = pe.transpose(psA[ch][:, j * P:(j + 1) * P], at[:, ch, j * AQ:(j + 1) * AQ], c.ident[:, :])
                        last.then_inc(turned, 1)
                        pe.wait_ge(aT_ok, n + 1)
                        pe.wait_ge(chain, 2 * n + 1)
                        for j in range(TPC):
                            last = pe.matmul(psO[ch][:, j * D:(j + 1) * D], aT[:, ch, j * P:(j + 1) * P], wo[:, :], start=True, stop=True)
                        last.then_inc(out_ok, 1)

            @block.scalar
            def _(act):
                act.wait_ge(emb_ok, 1)
                with act.Fori(0, BATCH) as b:
                    for ch in range(CPB):
                        n = b * CPB + ch
                        act.wait_ge(turned, n + 3)
                        act.activation(aT[:, ch, :], psA[ch][:, :], ACT.Identity, scale=emb[:, 2:3], bias=emb[:, 0:1]).then_inc(aT_ok, 1)

            @block.vector
            def _(dve):
                dve.wait_ge(w_in, 48)
                dve.tensor_tensor(emb[:, 2:3], emb[:, 1:2], emb[:, 0:1], ALU.subtract).then_inc(emb_ok, 1)
                dve.sem_inc(chain, 3)
                with dve.Fori(0, BATCH) as b:
                    for ch in range(CPB):
                        n = b * CPB + ch
                        at0 = (b * TPB + ch * TPC) * D
                        rows = c.x[:, ds(at0, TPC * D)]
                        tiles = [c.x[:, ds(at0 + j * D, D)] for j in range(TPC)]
                        dve.wait_ge(out_ok, n + 1)
                        row_stats(dve, [psO[ch][:, j * D:(j + 1) * D] for j in range(TPC)], sums[:, 0], stats[:, 0], summed, 2 * n + 1, stats_ok, tick)
                        dve.wait_ge(rstd_ok, 2 * n + 1)
                        for j in range(TPC):
                            last = dve.tensor_scalar(normed[:, j * D:(j + 1) * D], psO[ch][:, j * D:(j + 1) * D],
                                                     stats[:, 0, j, 0:1], rstd[:, 0, j:j + 1], ALU.subtract, ALU.mult)
                        last.then_inc(chain, 1)
                        dve.wait_ge(chain, 3 + 2 * n + 1)
                        dve.tensor_tensor(rows, rows, normed[:, :], ALU.add).then_inc(chain, 1)
                        wait_alone(dve, chain, 3 + 2 * n + 2, tick)
                        row_stats(dve, tiles, sums[:, 1], stats[:, 1], summed, 2 * n + 2, stats_ok, tick)
                        dve.wait_ge(rstd_ok, 2 * n + 2)
                        for j in range(TPC):
                            last = dve.tensor_scalar(c.norm[:, ds(at0 + j * D, D)], tiles[j],
                                                     stats[:, 1, j, 0:1], rstd[:, 1, j:j + 1], ALU.subtract, ALU.mult)
                        last.then_inc(norm_ok, 1)
                        dve.wait_ge(norm_ok, n + 1)
                        dve.tensor_reduce(out=amax[:, ds(n, 1)], in_=c.norm[:, ds(at0, TPC * D)], axis=AX_X, op=ALU.max,
                                          apply_absolute_value=True).then_inc(amax_ok, 1)
                dve.wait_ge(amax_ok, BATCH * CPB)
                dve.tensor_reduce(out=rmax[:, 0:1], in_=amax[:, :], axis=AX_X, op=ALU.max).then_inc(max_ok, 1)
                dve.wait_ge(all_max, 1)
                dve.tensor_scalar(c.xscale[:, 0:1], rmax[:, 1:2], 1.0 / E4M3_MAX, 1e-12, ALU.mult, ALU.max).then_inc(max_ok, 1)
                dve.wait_ge(max_ok, 2)
                dve.reciprocal(c.xscale[:, 1:2], c.xscale[:, 0:1])


def to_e4m3(dve, v, bits, out, step_ok, count):
    dve.tensor_scalar(bits.bitcast(I32), v.bitcast(I32), 0x7F800000, None, ALU.bitwise_and).then_inc(step_ok, 1)
    dve.wait_ge(step_ok, count + 1)
    dve.tensor_scalar(bits, bits, 2.0 ** -6, 1.5 * 2.0 ** 20, ALU.max, ALU.mult).then_inc(step_ok, 1)
    dve.wait_ge(step_ok, count + 2)
    dve.tensor_tensor(v, v, bits, ALU.add).then_inc(step_ok, 1)
    dve.wait_ge(step_ok, count + 3)
    dve.tensor_tensor(out, v, bits, ALU.subtract).then_inc(step_ok, 1)
    dve.wait_ge(step_ok, count + 4)


def phase_fp8_and_ssm_inputs(c, a, m):
    nc = c.nc
    with ExitStack() as ctx:
        wf = sbuf(nc, ctx, "p4_wf", [P, KD * D], BF16)
        wbits = sbuf(nc, ctx, "p4_wbits", [P, KD * D])
        wv = sbuf(nc, ctx, "p4_wv", [P, KD * D])
        w8 = sbuf(nc, ctx, "p4_w8", [P, KD, D], BF16)
        wmax = sbuf(nc, ctx, "p4_wmax", [P, 4])
        wx = sbuf(nc, ctx, "p4_wx", [P, KD, 2 * N + SH])
        wg = sbuf(nc, ctx, "p4_wg", [P, KD, D])
        bg = sbuf(nc, ctx, "p4_bg", [P, 2, KD])
        v = sbuf(nc, ctx, "p4_v", [P, TPC * D])
        bits = sbuf(nc, ctx, "p4_bits", [P, TPC * D])
        q8 = sbuf(nc, ctx, "p4_q8", [P, TPC * D], BF16)
        qT = sbuf(nc, ctx, "p4_qT", [P, KD, CH], BF16)
        o16 = sbuf(nc, ctx, "p4_o16", [P, TPC * D], BF16)
        sums = sbuf(nc, ctx, "p4_sums", [P, 2, TPC, 6])
        stats = sbuf(nc, ctx, "p4_stats", [P, 2, TPC, 2])
        rstd = sbuf(nc, ctx, "p4_rstd", [P, 2, TPC])
        normed = sbuf(nc, ctx, "p4_normed", [P, TPC * D])
        mv16 = sbuf(nc, ctx, "p4_mv16", [P, TPC, 2], BF16)
        sd16 = sbuf(nc, ctx, "p4_sd16", [P, 2, TPC], BF16)
        shift = sbuf(nc, ctx, "p4_shift", [P, 2, TPC])
        half = sbuf(nc, ctx, "p4_half", [P, TPC])
        c16 = sbuf(nc, ctx, "p4_c16", [P, TPC * D], BF16)
        n16 = sbuf(nc, ctx, "p4_n16", [P, TPC * D], BF16)
        bres = sbuf(nc, ctx, "p4_bres", [P, CH])
        dres = sbuf(nc, ctx, "p4_dres", [SH, CH])
        gt = sbuf(nc, ctx, "p4_gt", [P, KD, CH])
        psQ = psum(nc, ctx, "p4_psQ", [P, KD, CH], BF16)
        psO = psum(nc, ctx, "p4_psO", [P, TPC * D])
        psT = psum(nc, ctx, "p4_psT", [P, KD, CH])
        psB = psum(nc, ctx, "p4_psB", [P, CH])
        psC = psum(nc, ctx, "p4_psC", [P, CH])
        psD = psum(nc, ctx, "p4_psD", [SH, CH])
        w_in, wstep, w8_ok, wmax_ok = (c.sem("p4_" + n) for n in ("w_in", "wstep", "w8_ok", "wmax_ok"))
        step_ok, q8_ok, q_turned, qT_ok, out_ok, o16_ok = (c.sem("p4_" + n) for n in ("step_ok", "q8_ok", "q_turned", "qT_ok", "out_ok", "o16_ok"))
        summed, stats_ok, rstd_ok, chain = (c.sem("p4_" + n) for n in ("summed", "stats_ok", "rstd_ok", "chain"))
        added = c.sem("p4_added")
        tick, tick_pool = c.sem("p4_tick"), c.sem("p4_tick_pool")
        mv16_ok, sd_ok, step16 = (c.sem("p4_" + n) for n in ("mv16_ok", "sd_ok", "step16"))
        turned, xT_ok, proj_ok, gate_ok, upper_ok, taken, split_ok = (c.sem("p4_" + n) for n in ("turned", "xT_ok", "proj_ok", "gate_ok", "upper_ok", "taken", "split_ok"))

        with nc.Block() as block:

            @block.sync
            def _(sp):
                sp.dma_start(wf[:, :].rearrange("p (k n) -> p k n", k=KD), a["wf"].rearrange("(k p) n -> p k n", p=P)).then_inc(w_in, 16)
                sp.dma_start(wx[:, :, :], a["wx"].rearrange("(k p) n -> p k n", p=P)).then_inc(w_in, 16)
                sp.dma_start(wg[:, :, :], a["wg"].rearrange("(k p) n -> p k n", p=P)).then_inc(w_in, 16)
                sp.dma_start(bg[:, 0, :], a["bg"]).then_inc(w_in, 16)
                sp.wait_ge(w_in, 64)

            @block.gpsimd
            def _(pool):
                pool.wait_ge(wmax_ok, 1)
                pool.partition_all_reduce(wmax[:, 1:2], wmax[:, 0:1], P, RMAX).then_inc(wmax_ok, 1)
                with pool.Fori(0, BATCH) as b:
                    for ch in range(CPB):
                        n = b * CPB + ch
                        wait_alone(pool, mv16_ok, n + 1, tick_pool)
                        pool.tensor_scalar(sd16[:, 0, :], mv16[:, :, 1], EPS, None, ALU.add).then_inc(sd_ok, 1)
                        pool.wait_ge(sd_ok, 2 * n + 1)
                        pool.tensor_tensor(sd16[:, 1, :], sd16[:, 0, :], half[:, :], ALU.pow).then_inc(sd_ok, 1)
                        rows_rstd(pool, stats_ok, 2 * n + 2, rstd[:, 1, :], stats[:, 1, :, 1], EPS, c.power, added, n + 1, rstd_ok, tick_pool)

            @block.tensor
            def _(pe):
                pe.wait_ge(w8_ok, 1)
                with pe.Fori(0, BATCH) as b:
                    for ch in range(CPB):
                        n = b * CPB + ch
                        pe.wait_ge(q8_ok, n + 1)
                        for j in range(TPC):
                            for k in range(KD):
                                last = pe.transpose(psQ[:, k, j * P:(j + 1) * P], q8[:, j * D + k * P:j * D + (k + 1) * P], c.identb[:, :])
                        last.then_inc(q_turned, 1)
                        pe.wait_ge(qT_ok, n + 1)
                        for j in range(TPC):
                            for k in range(KD):
                                last = pe.matmul(psO[:, j * D:(j + 1) * D], qT[:, k, j * P:(j + 1) * P], w8[:, k, :], start=k == 0, stop=k == KD - 1)
                        last.then_inc(out_ok, 1)
                        pe.wait_ge(chain, 2 * n + 2)
                        for j in range(TPC):
                            for k in range(KD):
                                last = pe.transpose(psT[:, k, j * P:(j + 1) * P], normed[:, j * D + k * P:j * D + (k + 1) * P], c.ident[:, :])
                        last.then_inc(turned, 1)
                        pe.wait_ge(xT_ok, n + 1)
                        xT = [m["xT"][:, ds((b * CPB + ch) * KD * CH + k * CH, CH)] for k in range(KD)]
                        pe.wait_ge(taken, n + 1)
                        for ps, lo, hi in ((psB, 0, N), (psC, N, 2 * N), (psD, 2 * N, 2 * N + SH)):
                            for k in range(KD):
                                last = pe.matmul(ps[:, :], wx[:, k, lo:hi], xT[k], start=k == 0, stop=k == KD - 1)
                        last.then_inc(proj_ok, 1)
                        for f in range(KD):
                            for k in range(KD):
                                last = pe.matmul(psT[:, f, :], wg[:, k, f * P:(f + 1) * P], xT[k], start=k == 0, stop=k == KD - 1)
                        last.then_inc(proj_ok, 1)

            @block.scalar
            def _(act):
                act.preload_act_table_set("exp_and_others")
                act.wait_ge(w8_ok, 1)
                with act.Fori(0, BATCH) as b:
                    for ch in range(CPB):
                        n = b * CPB + ch
                        act.wait_ge(q_turned, n + 1)
                        act.activation(qT[:, :, :], psQ[:, :, :], ACT.Copy).then_inc(qT_ok, 1)
                        act.wait_ge(out_ok, n + 1)
                        act.activation(o16[:, :], psO[:, :], ACT.Copy, scale=wmax[:, 3:4]).then_inc(o16_ok, 1)
                        act.wait_ge(turned, n + 1)
                        act.activation(m["xT"][:, ds(n * KD * CH, KD * CH)], psT[:, :, :].rearrange("p k t -> p (k t)"), ACT.Copy).then_inc(xT_ok, 1)
                        act.wait_ge(proj_ok, 2 * n + 1)
                        act.activation(m["Bp"][0][:, ds(n * CH, CH)], psB[:, :], ACT.Copy)
                        act.activation(m["dp"][0:SH, ds(n * CH, CH)], psD[:, :], ACT.Copy).then_inc(upper_ok, 1)
                        act.activation(m["CT"][:, ds(n * CH, CH)], psC[:, :], ACT.Copy)
                        act.wait_ge(proj_ok, 2 * n + 2)
                        for f in range(KD):
                            last = act.activation(gt[:, f, :], psT[:, f, :], ACT.Tanh, scale=0.5, bias=bg[:, 1, f:f + 1])
                        last.then_inc(gate_ok, 1)

            @block.vector
            def _(dve):
                dve.wait_ge(w_in, 64)
                dve.memset(half[:, :], 0.5)
                dve.tensor_scalar(bg[:, 1, :], bg[:, 0, :], 0.5, None, ALU.mult)
                dve.tensor_reduce(out=wmax[:, 0:1], in_=wf[:, :], axis=AX_X, op=ALU.max, apply_absolute_value=True).then_inc(wmax_ok, 1)
                dve.wait_ge(wmax_ok, 2)
                dve.tensor_scalar(wmax[:, 2:3], wmax[:, 1:2], 1.0 / E4M3_MAX, 1e-12, ALU.mult, ALU.max).then_inc(wstep, 1)
                dve.wait_ge(wstep, 1)
                dve.tensor_tensor(wmax[:, 3:4], c.xscale[:, 0:1], wmax[:, 2:3], ALU.mult)
                dve.reciprocal(wmax[:, 0:1], wmax[:, 2:3]).then_inc(wstep, 1)
                dve.wait_ge(wstep, 2)
                dve.tensor_scalar(wv[:, :], wf[:, :], wmax[:, 0:1], None, ALU.mult).then_inc(wstep, 1)
                dve.wait_ge(wstep, 3)
                to_e4m3(dve, wv[:, :], wbits[:, :], w8[:, :, :].rearrange("p k n -> p (k n)"), wstep, 3)
                dve.sem_inc(w8_ok, 1)
                dve.sem_inc(taken, 1)
                with dve.Fori(0, BATCH) as b:
                    for ch in range(CPB):
                        n = b * CPB + ch
                        at0 = (b * TPB + ch * TPC) * D
                        rows = c.x[:, ds(at0, TPC * D)]
                        tiles = [c.x[:, ds(at0 + j * D, D)] for j in range(TPC)]
                        dve.tensor_scalar(v[:, :], c.norm[:, ds(at0, TPC * D)], c.xscale[:, 1:2], None, ALU.mult).then_inc(step_ok, 1)
                        dve.wait_ge(step_ok, 5 * n + 1)
                        to_e4m3(dve, v[:, :], bits[:, :], q8[:, :], step_ok, 5 * n + 1)
                        dve.sem_inc(q8_ok, 1)
                        dve.wait_ge(o16_ok, n + 1)
                        row_stats(dve, [o16[:, j * D:(j + 1) * D] for j in range(TPC)], sums[:, 0], stats[:, 0], summed, 2 * n + 1, stats_ok, tick)
                        dve.wait_ge(stats_ok, 2 * n + 1)
                        dve.tensor_copy(mv16[:, :, :], stats[:, 0]).then_inc(mv16_ok, 1)
                        dve.wait_ge(mv16_ok, n + 1)
                        dve.tensor_copy(shift[:, 0, :], mv16[:, :, 0])
                        dve.wait_ge(sd_ok, 2 * n + 2)
                        dve.reciprocal(shift[:, 1, :], sd16[:, 1, :]).then_inc(step16, 1)
                        dve.wait_ge(step16, 3 * n + 1)
                        for j in range(TPC):
                            last = dve.tensor_scalar(c16[:, j * D:(j + 1) * D], o16[:, j * D:(j + 1) * D], shift[:, 0, j:j + 1], None, ALU.subtract)
                        last.then_inc(step16, 1)
                        dve.wait_ge(step16, 3 * n + 2)
                        for j in range(TPC):
                            last = dve.tensor_scalar(n16[:, j * D:(j + 1) * D], c16[:, j * D:(j + 1) * D], shift[:, 1, j:j + 1], None, ALU.mult)
                        last.then_inc(step16, 1)
                        dve.wait_ge(step16, 3 * n + 3)
                        dve.tensor_tensor(rows, rows, n16[:, :], ALU.add).then_inc(chain, 1)
                        wait_alone(dve, chain, 2 * n + 1, tick)
                        row_stats(dve, tiles, sums[:, 1], stats[:, 1], summed, 2 * n + 2, stats_ok, tick)
                        dve.wait_ge(rstd_ok, n + 1)
                        for j in range(TPC):
                            last = dve.tensor_scalar(normed[:, j * D:(j + 1) * D], tiles[j],
                                                     stats[:, 1, j, 0:1], rstd[:, 1, j:j + 1], ALU.subtract, ALU.mult)
                        last.then_inc(chain, 1)
                        dve.wait_ge(upper_ok, n + 1)
                        cols = ds(n * CH, CH)
                        dve.tensor_tensor(bres[:, :], psB[:, :], m["Bp"][0][:, cols], ALU.subtract)
                        dve.tensor_tensor(dres[:, :], psD[:, :], m["dp"][0:SH, cols], ALU.subtract).then_inc(split_ok, 1)
                        dve.wait_ge(split_ok, 2 * n + 1)
                        dve.tensor_copy(m["Bp"][1][:, cols], bres[:, :])
                        dve.tensor_copy(m["dp"][SH:2 * SH, cols], dres[:, :])
                        dve.tensor_copy(m["dm"][:, :], dres[:, :]).then_inc(split_ok, 1)
                        dve.wait_ge(split_ok, 2 * n + 2)
                        dve.tensor_tensor(m["Bp"][2][:, cols], bres[:, :], m["Bp"][1][:, cols], ALU.subtract)
                        dve.tensor_tensor(m["dp"][2 * SH:3 * SH, cols], dres[:, :], m["dm"][:, :], ALU.subtract)
                        dve.wait_ge(gate_ok, n + 1)
                        dve.tensor_scalar(c.norm[:, ds(n * KD * CH, KD * CH)], gt[:, :, :].rearrange("p k t -> p (k t)"), 0.5, 0.5, ALU.mult, ALU.add).then_inc(taken, 1)


def ring(*turns):
    slots = [s for n in turns for s in range(n)]
    assert len(slots) == SH
    return slots, [next(k for k in range(1, SH + 1) if k == max(turns) or slots[q - k] == slots[q]) for q in range(SH)]


def phase_ssm(c, a, m):
    nc = c.nc
    FREE = 5
    Z, Z_BACK = ring(*[3] * 10, 2)
    U, U_BACK = ring(*[5] * 4, *[4] * 3)
    RQ = 2

    def head_of(q):
        return (q // 16) * 16 + 4 * (q % 4) + (q // 4) % 4

    def ahead(b, q, k, last):
        if q + k < SH:
            return b * SH + q + k, b, q + k
        return None if last else (b * SH + q + k, b + 1, q + k - SH)

    with ExitStack() as ctx:
        AT = sbuf(nc, ctx, "p5_AT", [P, SH])
        skip = sbuf(nc, ctx, "p5_skip", [P, KD])
        pick = sbuf(nc, ctx, "p5_pick", [3 * SH, 2, SH])
        sel = sbuf(nc, ctx, "p5_sel", [3 * SH, SH], BF16)
        ones = sbuf(nc, ctx, "p5_ones", [P, 4, 4 * SHD])
        u = [sbuf(nc, ctx, f"p5_u{i}", [P, S]) for i in range(5)]
        st = [sbuf(nc, ctx, f"p5_st{i}", [P, S]) for i in range(5)]
        sq = [sbuf(nc, ctx, f"p5_sq{i}", [P, S]) for i in range(RQ)]
        psZ = [psum(nc, ctx, f"p5_psZ{i}", [P, CPB, CH]) for i in range(3)]
        psY = psum(nc, ctx, "p5_psY", [P, CPB, CH])
        w_in, const_ok = c.sem("p5_w_in"), c.sem("p5_const_ok")
        z_ok, exp_ok, ln_ok, d_ok, sq_ok, a_ok = (c.sem("p5_" + n) for n in ("z_ok", "exp_ok", "ln_ok", "d_ok", "sq_ok", "a_ok"))
        scan_ok, prod_ok, read_ok, y_taken, skip_ok = (c.sem("p5_" + n) for n in ("scan_ok", "prod_ok", "read_ok", "y_taken", "skip_ok"))

        with nc.Block() as block:

            @block.sync
            def _(sp):
                sp.dma_start(AT[:, :], a["ssmA"]).then_inc(w_in, 16)
                sp.dma_start(skip[:, :], a["skip"]).then_inc(w_in, 16)
                sp.wait_ge(w_in, 32)

            @block.tensor
            def _(pe):
                pe.sem_inc(read_ok, FREE)
                pe.wait_ge(const_ok, 3)

                def logits(i, b, q):
                    pe.wait_ge(d_ok, FREE + i - Z_BACK[q] + 1)
                    pick_head = sel[:, head_of(q):head_of(q) + 1].broadcast_to([3 * SH, P])
                    for ch in range(CPB):
                        cols = ds(b * S + ch * CH, CH)
                        for e in range(3):
                            pe.matmul(psZ[Z[q]][:, ch, :], c.identb[:, :], m["Bp"][e][:, cols], start=e == 0, stop=False)
                        last = pe.matmul(psZ[Z[q]][:, ch, :], pick_head, m["dp"][:, cols], start=False, stop=True)
                    last.then_inc(z_ok, 1)

                def read(b, q):
                    r = (q // 4) % 4
                    if q % 16 == 1:
                        pe.wait_ge(y_taken, 2 * b + q // 16 + 1)
                    pe.wait_ge(prod_ok, b * SH + q + 1)
                    for ch in range(CPB):
                        for p in (q - 1, q):
                            j = p % 4
                            last = pe.matmul(psY[32 * j:32 * j + 32, ch, :], ones[:, r, :], st[U[p]][:, ch * CH:(ch + 1) * CH],
                                             start=r == 0, stop=r == 3)
                    last.then_inc(read_ok, 2)

                def batch(b, last_batch):
                    for q in range(SH):
                        nxt = ahead(b, q, 4, last_batch)
                        if nxt:
                            logits(*nxt)
                        if q % 2 == 0 and q:
                            read(b, q - 1)
                    read(b, SH - 1)

                for q in range(4):
                    logits(q, 0, q)
                with pe.Fori(0, BATCH - 1) as b:
                    batch(b, False)
                batch(BATCH - 1, True)

            @block.scalar
            def _(act):
                act.preload_act_table_set("natural_log_exp_and_others")
                act.wait_ge(w_in, 32)

                def exps(i, b, q):
                    act.wait_ge(sq_ok, FREE + i - U_BACK[q] + 1)
                    act.wait_ge(z_ok, i + 1)
                    act.activation(u[U[q]][:, :], psZ[Z[q]][:, :, :].rearrange("p c t -> p (c t)"), ACT.Exp).then_inc(exp_ok, 1)

                def logs(i, b, q):
                    act.wait_ge(exp_ok, i + 1)
                    act.activation(u[U[q]][:, :], u[U[q]][:, :], ACT.Ln, bias=1.0).then_inc(ln_ok, 1)

                def decays(i, b, q):
                    act.wait_ge(d_ok, FREE + i + 1)
                    act.wait_ge(read_ok, FREE + i - U_BACK[q] + 1)
                    act.activation(st[U[q]][:, :], u[U[q]][:, :], ACT.Exp, scale=AT[:, head_of(q):head_of(q) + 1]).then_inc(a_ok, 1)

                def batch(b, last):
                    for q in range(SH):
                        for step, k in ((decays, 1), (logs, 3), (exps, 4)):
                            nxt = ahead(b, q, k, last)
                            if nxt:
                                step(*nxt)

                for q in range(3):
                    exps(q, 0, q)
                    logs(q, 0, q)
                exps(3, 0, 3)
                decays(0, 0, 0)
                with act.Fori(0, BATCH - 1) as b:
                    batch(b, False)
                batch(BATCH - 1, True)

            @block.gpsimd
            def _(pool):
                pool.sem_inc(sq_ok, FREE)
                with pool.Fori(0, BATCH) as b:
                    for q in range(SH):
                        i = b * SH + q
                        pool.wait_ge(d_ok, FREE + i + 1)
                        pool.wait_ge(scan_ok, i + 1)
                        pool.tensor_tensor(sq[q % RQ][:, :], u[U[q]][:, :], u[U[q]][:, :], ALU.mult).then_inc(sq_ok, 1)

            @block.vector
            def _(dve):
                dve.memset(ones[:, :, :], 0.0).then_inc(const_ok, 1)
                dve.wait_ge(const_ok, 1)
                for r in range(4):
                    dve.memset(ones[:, r, r * SHD:(r + 1) * SHD], 1.0)
                dve.tensor_tensor(pick[:, 0, :], c.ident[0:3 * SH, 0:SH], c.ident[0:3 * SH, SH:2 * SH], ALU.add).then_inc(const_ok, 1)
                dve.wait_ge(const_ok, 2)
                dve.tensor_tensor(pick[:, 1, :], pick[:, 0, :], c.ident[0:3 * SH, 2 * SH:3 * SH], ALU.add).then_inc(skip_ok, 1)
                dve.wait_ge(skip_ok, 1)
                dve.tensor_copy(sel[:, :], pick[:, 1, :]).then_inc(const_ok, 1)
                dve.sem_inc(d_ok, FREE)
                dve.sem_inc(scan_ok, RQ)
                dve.sem_inc(y_taken, 1)
                dve.wait_ge(w_in, 32)

                def step_sizes(i, b, q):
                    dve.wait_ge(ln_ok, i + 1)
                    dve.scalar_tensor_tensor(out=u[U[q]][:, :], in0=u[U[q]][:, :], scalar=SAT,
                                             in1=psZ[Z[q]][:, :, :].rearrange("p c t -> p (c t)"), op0=ALU.min, op1=ALU.max).then_inc(d_ok, 1)

                def skip_and_gate(b, f):
                    dve.wait_ge(read_ok, FREE + b * SH + (f + 1) * 16)
                    for ch in range(CPB):
                        cols = ds((b * CPB + ch) * KD * CH + f * CH, CH)
                        last = dve.scalar_tensor_tensor(out=m["xT"][:, cols], in0=m["xT"][:, cols], scalar=skip[:, f:f + 1],
                                                        in1=psY[:, ch, :], op0=ALU.mult, op1=ALU.add)
                    last.then_inc(y_taken, 1)
                    dve.wait_ge(y_taken, 1 + 2 * b + f + 1)
                    for ch in range(CPB):
                        cols = ds((b * CPB + ch) * KD * CH + f * CH, CH)
                        dve.tensor_tensor(c.norm[:, cols], m["xT"][:, cols], c.norm[:, cols], ALU.mult)

                def batch(b, last):
                    for q in range(SH):
                        i = b * SH + q
                        dve.wait_ge(a_ok, i + 1)
                        dve.wait_ge(sq_ok, FREE + i + 1)
                        dve.tensor_tensor_scan(st[U[q]][:, :], st[U[q]][:, :], sq[q % RQ][:, :], 0.0, ALU.mult, ALU.add).then_inc(scan_ok, 1)
                        nxt = ahead(b, q, 2, last)
                        if nxt:
                            step_sizes(*nxt)
                        if q == 17:
                            skip_and_gate(b, 0)
                        dve.wait_ge(scan_ok, RQ + i + 1)
                        dve.tensor_tensor(st[U[q]][:, :], st[U[q]][:, :], m["CT"][:, ds(b * S, S)], ALU.mult).then_inc(prod_ok, 1)
                    skip_and_gate(b, 1)

                step_sizes(0, 0, 0)
                step_sizes(1, 0, 1)
                with dve.Fori(0, BATCH - 1) as b:
                    batch(b, False)
                batch(BATCH - 1, True)


def phase_qkv_second(c, a, d):
    nc = c.nc
    with ExitStack() as ctx:
        wo = sbuf(nc, ctx, "p6_wo", [P, KD, D])
        wqk = [sbuf(nc, ctx, f"p6_wqk{i}", [P, KD, D]) for i in range(2)]
        wv = sbuf(nc, ctx, "p6_wv", [P, KD, D])
        ln = sbuf(nc, ctx, "p6_ln", [P, 2, KD])
        ys = sbuf(nc, ctx, "p6_ys", [P, 2, KD, CH])
        sums = sbuf(nc, ctx, "p6_sums", [P, 3, TPC, 6])
        stats = sbuf(nc, ctx, "p6_stats", [P, 3, TPC, 2])
        rstd = sbuf(nc, ctx, "p6_rstd", [P, 3, TPC])
        msq = sbuf(nc, ctx, "p6_msq", [P, 2, TPC])
        normed = sbuf(nc, ctx, "p6_normed", [P, TPC * D])
        base = sbuf(nc, ctx, "p6_base", [P, TPC * D])
        aT = sbuf(nc, ctx, "p6_aT", [P, KD, CH])
        hT = sbuf(nc, ctx, "p6_hT", [P, KD, CH])
        rest = sbuf(nc, ctx, "p6_rest", [P, 2, CH])
        parts = [sbuf(nc, ctx, f"p6_parts{i}", [P, 3, 2, CH], BF16) for i in range(2)]
        vx = sbuf(nc, ctx, "p6_vx", [P, TPC, G * HG, HD + 1])
        psO = psum(nc, ctx, "p6_psO", [P, TPC * D])
        psT = psum(nc, ctx, "p6_psT", [P, KD, CH])
        psP = psum(nc, ctx, "p6_psP", [P, 2, CH])
        psV = psum(nc, ctx, "p6_psV", [P, TPC, D])
        w_in, ones_ok, ys_ok, out_ok = (c.sem("p6_" + n) for n in ("w_in", "ones_ok", "ys_ok", "out_ok"))
        summed, stats_ok, ms_ok, rstd_ok, chain = (c.sem("p6_" + n) for n in ("summed", "stats_ok", "ms_ok", "rstd_ok", "chain"))
        added = c.sem("p6_added")
        tick, tick_pool = c.sem("p6_tick"), c.sem("p6_tick_pool")
        turned, aT_ok, hT_ok, v_ok, proj_ok = (c.sem("p6_" + n) for n in ("turned", "aT_ok", "hT_ok", "v_ok", "proj_ok"))
        upper_ok, rest_ok, mid_ok, low_ok, vx_ok, stored = (c.sem("p6_" + n) for n in ("upper_ok", "rest_ok", "mid_ok", "low_ok", "vx_ok", "stored"))
        STORES = 16 * (1 + 4 + 4 + 4)

        with nc.Block() as block:

            @block.sync
            def _(sp):
                for w, src in ((wo, a["wo3"]), (wqk[0], a["wq2"]), (wqk[1], a["wk2"]), (wv, a["wv2"])):
                    sp.dma_start(w[:, :, :], src.rearrange("(k p) n -> p k n", p=P)).then_inc(w_in, 16)
                sp.dma_start(ln[:, 0, :], a["ln1"]).then_inc(w_in, 16)
                sp.dma_start(ln[:, 1, :], a["ln2"]).then_inc(w_in, 16)
                sp.sem_inc(stored, STORES)
                with sp.Fori(0, BATCH) as b:
                    for ch in range(CPB):
                        n = b * CPB + ch
                        sp.wait_ge(hT_ok, n + 1)
                        sp.dma_start(d["h"][ds(n, 1)].rearrange("n p e -> (n p) e"), hT[:, :, :].rearrange("p k t -> p (k t)")).then_inc(stored, 16)
                        sp.wait_ge(vx_ok, n + 1)
                        bg = ds(b * G, G)
                        for g in range(G):
                            sp.dma_start(d["v2"][bg][g, :, ch * TPC:(ch + 1) * TPC, :, :].rearrange("p j h e -> p j (h e)"),
                                         vx[:, :, g * HG:(g + 1) * HG, :].rearrange("p j h e -> p j (h e)")).then_inc(stored, 16)
                        for i in range(2):
                            sp.wait_ge(low_ok, 2 * n + i + 2)
                            for g in range(G):
                                rows = slice(64 * (g % 2), 64 * (g % 2) + 64)
                                sp.dma_start(d["qk2"][i][bg][g, :, :, ch * CH:(ch + 1) * CH].rearrange("e r t -> r e t"),
                                             parts[i][rows, :, g // 2, :]).then_inc(stored, 16)
                sp.wait_ge(stored, STORES * (BATCH * CPB + 1))

            @block.gpsimd
            def _(pool):
                pool.sem_inc(low_ok, 1)
                with pool.Fori(0, BATCH) as b:
                    for ch in range(CPB):
                        n = b * CPB + ch
                        pool.wait_ge(out_ok, n + 1)
                        pool.tensor_copy(ys[:, ch, :, :].rearrange("p k t -> p (k t)"), c.norm[:, ds(n * KD * CH, KD * CH)]).then_inc(ys_ok, 1)
                        for k in range(2):
                            rows_rstd(pool, stats_ok, 3 * n + k + 1, rstd[:, k, :], stats[:, k, :, 1], EPS, c.power, added, 3 * n + k + 1, rstd_ok, tick_pool)
                        rows_rstd(pool, ms_ok, 2 * n + 2, rstd[:, 2, :], msq[:, 1, :], RMS_EPS, c.power, added, 3 * n + 3, rstd_ok, tick_pool)
                        for i in range(2):
                            pool.wait_ge(mid_ok, 2 * n + i + 1)
                            pool.tensor_tensor(parts[i][:, 2, :, :], rest[:, :, :], parts[i][:, 1, :, :], ALU.subtract).then_inc(low_ok, 1)

            @block.tensor
            def _(pe):
                pe.sem_inc(out_ok, 2)
                pe.wait_ge(w_in, 96)
                with pe.Fori(0, BATCH) as b:
                    for ch in range(CPB):
                        n = b * CPB + ch
                        pe.wait_ge(ys_ok, n + 1)
                        pe.wait_ge(chain, 4 * n + 1)
                        for j in range(TPC):
                            for k in range(KD):
                                last = pe.matmul(psO[:, j * D:(j + 1) * D], ys[:, ch, k, j * P:(j + 1) * P], wo[:, k, :], start=k == 0, stop=k == KD - 1)
                        last.then_inc(out_ok, 1)
                        pe.wait_ge(chain, 1 + 4 * n + 4)
                        for j in range(TPC):
                            for k in range(KD):
                                last = pe.transpose(psT[:, k, j * P:(j + 1) * P], base[:, j * D + k * P:j * D + (k + 1) * P], c.ident[:, :])
                        last.then_inc(turned, 1)
                        pe.wait_ge(aT_ok, n + 1)
                        for i in range(2):
                            pe.wait_ge(rest_ok, 2 * n + i + 1)
                            for f in range(2):
                                for k in range(KD):
                                    last = pe.matmul(psP[:, f, :], wqk[i][:, k, f * P:(f + 1) * P], aT[:, k, :], start=k == 0, stop=k == KD - 1)
                            last.then_inc(proj_ok, 1)
                            if i == 0:
                                for j in range(TPC):
                                    for k in range(KD):
                                        last = pe.matmul(psV[:, j, :], aT[:, k, j * P:(j + 1) * P], wv[:, k, :], start=k == 0, stop=k == KD - 1)
                                last.then_inc(v_ok, 1)

            @block.scalar
            def _(act):
                act.wait_ge(w_in, 96)
                act.wait_ge(ones_ok, 1)
                with act.Fori(0, BATCH) as b:
                    for ch in range(CPB):
                        n = b * CPB + ch
                        act.wait_ge(turned, n + 1)
                        for k in range(KD):
                            last = act.activation(aT[:, k, :], psT[:, k, :], ACT.Copy, scale=ln[:, 0, k:k + 1])
                        last.then_inc(aT_ok, 1)
                        act.wait_ge(stored, STORES * (n + 1))
                        for k in range(KD):
                            last = act.activation(hT[:, k, :], psT[:, k, :], ACT.Copy, scale=ln[:, 1, k:k + 1])
                        last.then_inc(hT_ok, 1)
                        for i in range(2):
                            act.wait_ge(proj_ok, 2 * n + i + 1)
                            act.activation(parts[i][:, 0, :, :], psP[:, :, :], ACT.Copy).then_inc(upper_ok, 1)
                            if i == 0:
                                act.wait_ge(v_ok, n + 1)
                                act.activation(vx[:, :, :, 0:HD], psV[:, :, :].rearrange("p j (h e) -> p j h e", e=HD), ACT.Copy).then_inc(vx_ok, 1)
                            act.wait_ge(rest_ok, 1 + 2 * n + i + 1)
                            act.activation(parts[i][:, 1, :, :], rest[:, :, :], ACT.Copy).then_inc(mid_ok, 1)

            @block.vector
            def _(dve):
                dve.memset(vx[:, :, :, :], 1.0).then_inc(ones_ok, 1)
                dve.sem_inc(chain, 1)
                dve.sem_inc(rest_ok, 1)
                with dve.Fori(0, BATCH) as b:
                    for ch in range(CPB):
                        n = b * CPB + ch
                        at0 = (b * TPB + ch * TPC) * D
                        rows = c.x[:, ds(at0, TPC * D)]
                        tiles = [c.x[:, ds(at0 + j * D, D)] for j in range(TPC)]
                        kept = [c.norm[:, ds(at0 + j * D, D)] for j in range(TPC)]
                        dve.wait_ge(out_ok, n + 3)
                        row_stats(dve, [psO[:, j * D:(j + 1) * D] for j in range(TPC)], sums[:, 0], stats[:, 0], summed, 3 * n + 1, stats_ok, tick)
                        dve.wait_ge(rstd_ok, 3 * n + 1)
                        for j in range(TPC):
                            last = dve.tensor_scalar(normed[:, j * D:(j + 1) * D], psO[:, j * D:(j + 1) * D],
                                                     stats[:, 0, j, 0:1], rstd[:, 0, j:j + 1], ALU.subtract, ALU.mult)
                        last.then_inc(chain, 1)
                        dve.wait_ge(chain, 1 + 4 * n + 1)
                        dve.tensor_tensor(rows, rows, normed[:, :], ALU.add).then_inc(chain, 1)
                        wait_alone(dve, chain, 1 + 4 * n + 2, tick)
                        row_stats(dve, tiles, sums[:, 1], stats[:, 1], summed, 3 * n + 2, stats_ok, tick)
                        dve.wait_ge(rstd_ok, 3 * n + 2)
                        dve.wait_ge(ys_ok, n + 1)
                        for j in range(TPC):
                            last = dve.tensor_scalar(kept[j], tiles[j], stats[:, 1, j, 0:1], rstd[:, 1, j:j + 1], ALU.subtract, ALU.mult)
                        last.then_inc(chain, 1)
                        wait_alone(dve, chain, 1 + 4 * n + 3, tick)
                        row_stats(dve, kept, sums[:, 2], stats[:, 2], summed, 3 * n + 3, stats_ok, tick)
                        dve.wait_ge(stats_ok, 3 * n + 3)
                        dve.tensor_tensor(msq[:, 0, :], stats[:, 2, :, 0], stats[:, 2, :, 0], ALU.mult).then_inc(ms_ok, 1)
                        dve.wait_ge(ms_ok, 2 * n + 1)
                        dve.tensor_tensor(msq[:, 1, :], msq[:, 0, :], stats[:, 2, :, 1], ALU.add).then_inc(ms_ok, 1)
                        dve.wait_ge(rstd_ok, 3 * n + 3)
                        for j in range(TPC):
                            last = dve.tensor_scalar(base[:, j * D:(j + 1) * D], kept[j], rstd[:, 2, j:j + 1], None, ALU.mult)
                        last.then_inc(chain, 1)
                        for i in range(2):
                            dve.wait_ge(upper_ok, 2 * n + i + 1)
                            dve.wait_ge(low_ok, 2 * n + i + 1)
                            dve.tensor_tensor(rest[:, :, :], psP[:, :, :], parts[i][:, 0, :, :], ALU.subtract).then_inc(rest_ok, 1)


def phase_mlp(c, a, d, out):
    nc = c.nc
    with ExitStack() as ctx:
        wo = sbuf(nc, ctx, "p8_wo", [P, KD, D])
        wa = sbuf(nc, ctx, "p8_wa", [P, KD, R])
        wb = sbuf(nc, ctx, "p8_wb", [R, F])
        wgu = [sbuf(nc, ctx, f"p8_wgu{i}", [P, KD, F]) for i in range(2)]
        wd = sbuf(nc, ctx, "p8_wd", [P, FT, D])
        at = sbuf(nc, ctx, "p8_at", [P, CPB, TPC * D])
        hT = sbuf(nc, ctx, "p8_hT", [P, CPB, KD, CH])
        aT = sbuf(nc, ctx, "p8_aT", [P, KD, CH])
        oT = sbuf(nc, ctx, "p8_oT", [P, KD, CH])
        mod = sbuf(nc, ctx, "p8_mod", [R, CH])
        g = sbuf(nc, ctx, "p8_g", [R, CH])
        gate = sbuf(nc, ctx, "p8_gate", [P, 2, CH])
        mT = sbuf(nc, ctx, "p8_mT", [P, FT, CH])
        sums = sbuf(nc, ctx, "p8_sums", [P, TPC, 6])
        stats = sbuf(nc, ctx, "p8_stats", [P, TPC, 2])
        rstd = sbuf(nc, ctx, "p8_rstd", [P, TPC])
        y = sbuf(nc, ctx, "p8_y", [P, TPC * D])
        normed = sbuf(nc, ctx, "p8_normed", [P, TPC * D])
        psX = [psum(nc, ctx, f"p8_psX{i}", [P, 2, CH]) for i in range(2)]
        psM = [psum(nc, ctx, f"p8_psM{i}", [P, CH]) for i in range(2)]
        psD = psum(nc, ctx, "p8_psD", [P, TPC * D])
        w_in, h_in, h_used = c.sem("p8_w_in"), [c.sem(f"p8_h_in{i}") for i in range(CPB)], c.sem("p8_h_used")
        at_ok, turned, aT_ok, oproj_ok, oT_ok, low_ok, mod_ok, g_ok = (c.sem("p8_" + n) for n in ("at_ok", "turned", "aT_ok", "oproj_ok", "oT_ok", "low_ok", "mod_ok", "g_ok"))
        gu_ok, silu_ok, m_ok, down_ok = (c.sem("p8_" + n) for n in ("gu_ok", "silu_ok", "m_ok", "down_ok"))
        summed, stats_ok, rstd_ok, chain, stored = (c.sem("p8_" + n) for n in ("summed", "stats_ok", "rstd_ok", "chain", "stored"))
        added = c.sem("p8_added")
        tick, tick_pool = c.sem("p8_tick"), c.sem("p8_tick_pool")

        with nc.Block() as block:

            @block.sync
            def _(sp):
                for w, src in ((wo, a["wo4"]), (wa, a["loraA"]), (wgu[0], a["win"]), (wgu[1], a["wup"]), (wd, a["wdown"])):
                    sp.dma_start(w[:, :, :], src.rearrange("(k p) n -> p k n", p=P)).then_inc(w_in, 16)
                sp.dma_start(wb[:, :], a["loraB"]).then_inc(w_in, 16)

                def load(n, ch):
                    sp.dma_start(hT[:, ch, :, :].rearrange("p k t -> p (k t)"), d["h"][ds(n, 1)].rearrange("n p e -> (n p) e")).then_inc(h_in[ch], 16)

                for ch in range(CPB):
                    load(ch, ch)

                def batch(b, last):
                    for ch in range(CPB):
                        n = b * CPB + ch
                        if not last:
                            sp.wait_ge(gu_ok, (n + 1) * FT)
                            load(n + CPB, ch)
                        sp.wait_ge(chain, 3 * n + 4)
                        sp.dma_start(out[ds(b, 1), ch * CH:(ch + 1) * CH, :].rearrange("b (j p) e -> p (b j) e", p=P),
                                     c.x[:, ds(n * TPC * D, TPC * D)].rearrange("p (j e) -> p j e", e=D)).then_inc(stored, 16)

                with sp.Fori(0, BATCH - 1) as b:
                    batch(b, False)
                batch(BATCH - 1, True)
                sp.wait_ge(stored, 16 * BATCH * CPB)

            @block.gpsimd
            def _(pool):
                with pool.Fori(0, BATCH) as b:
                    for ch in range(CPB):
                        n = b * CPB + ch
                        pool.wait_ge(turned, n + 1)
                        pool.tensor_copy(at[:, ch, :], c.attn[:, ds(n * TPC * D, TPC * D)]).then_inc(at_ok, 1)
                        rows_rstd(pool, stats_ok, n + 1, rstd[:, :], stats[:, :, 1], EPS, c.power, added, n + 1, rstd_ok, tick_pool)

            @block.tensor
            def _(pe):
                pe.sem_inc(turned, 2)
                pe.wait_ge(w_in, 96)
                with pe.Fori(0, BATCH) as b:
                    for ch in range(CPB):
                        n = b * CPB + ch
                        pe.wait_ge(at_ok, n + 1)
                        pe.wait_ge(m_ok, FT * n + 1)
                        for j in range(TPC):
                            for k in range(KD):
                                last = pe.transpose(psX[0][:, k, j * P:(j + 1) * P], at[:, ch, j * D + k * P:j * D + (k + 1) * P], c.ident[:, :])
                        last.then_inc(turned, 1)
                        pe.wait_ge(aT_ok, n + 1)
                        for f in range(KD):
                            for k in range(KD):
                                last = pe.matmul(psX[1][:, f, :], wo[:, k, f * P:(f + 1) * P], aT[:, k, :], start=k == 0, stop=k == KD - 1)
                        last.then_inc(oproj_ok, 1)
                        pe.wait_ge(oT_ok, n + 1)
                        pe.wait_ge(h_in[ch], 16 * (b + 1))
                        for ps, src in ((psM[0], oT), (psM[1], hT[:, ch])):
                            for k in range(KD):
                                last = pe.matmul(ps[0:R, :], wa[:, k, :], src[:, k, :], start=k == 0, stop=k == KD - 1)
                        last.then_inc(low_ok, 1)
                        for f in range(FT):
                            if f == 0:
                                pe.wait_ge(g_ok, n + 1)
                            else:
                                pe.wait_ge(m_ok, FT * n + f - 1 + 1)
                            for i in range(2):
                                for k in range(KD):
                                    last = pe.matmul(psX[f % 2][:, i, :], wgu[i][:, k, f * P:(f + 1) * P], hT[:, ch, k, :], start=k == 0, stop=i == 1 and k == KD - 1)
                                if i == 0:
                                    pe.matmul(psX[f % 2][:, 0, :], wb[:, f * P:(f + 1) * P], g[:, :], start=False, stop=True)
                            last.then_inc(gu_ok, 1)
                        pe.wait_ge(m_ok, 1 + FT * (n + 1))
                        pe.wait_ge(chain, 3 * n + 1)
                        for j in range(TPC):
                            for k in range(FT):
                                last = pe.matmul(psD[:, j * D:(j + 1) * D], mT[:, k, j * P:(j + 1) * P], wd[:, k, :], start=k == 0, stop=k == FT - 1)
                        last.then_inc(down_ok, 1)

            @block.scalar
            def _(act):
                act.preload_act_table_set("silu_and_others")
                with act.Fori(0, BATCH) as b:
                    for ch in range(CPB):
                        n = b * CPB + ch
                        act.wait_ge(turned, n + 3)
                        act.activation(aT[:, :, :], psX[0][:, :, :], ACT.Copy).then_inc(aT_ok, 1)
                        act.wait_ge(oproj_ok, n + 1)
                        act.activation(oT[:, :, :], psX[1][:, :, :], ACT.Copy).then_inc(oT_ok, 1)
                        act.wait_ge(low_ok, n + 1)
                        act.activation(mod[:, :], psM[0][0:R, :], ACT.Tanh).then_inc(mod_ok, 1)
                        for f in range(FT):
                            act.wait_ge(gu_ok, FT * n + f + 1)
                            act.activation(gate[:, f % 2, :], psX[f % 2][:, 0, :], ACT.Silu).then_inc(silu_ok, 1)

            @block.vector
            def _(dve):
                dve.sem_inc(chain, 1)
                dve.sem_inc(m_ok, 1)
                with dve.Fori(0, BATCH) as b:
                    for ch in range(CPB):
                        n = b * CPB + ch
                        dve.wait_ge(mod_ok, n + 1)
                        dve.scalar_tensor_tensor(out=g[:, :], in0=mod[:, :], scalar=0.1, in1=psM[1][0:R, :], op0=ALU.mult, op1=ALU.mult).then_inc(g_ok, 1)
                        for f in range(FT):
                            dve.wait_ge(silu_ok, FT * n + f + 1)
                            dve.tensor_tensor(mT[:, f, :], gate[:, f % 2, :], psX[f % 2][:, 1, :], ALU.mult).then_inc(m_ok, 1)
                        rows = c.x[:, ds(n * TPC * D, TPC * D)]
                        dve.wait_ge(down_ok, n + 1)
                        dve.tensor_tensor(y[:, :], psD[:, :], c.norm[:, ds(n * TPC * D, TPC * D)], ALU.add).then_inc(chain, 1)
                        dve.wait_ge(chain, 1 + 3 * n + 1)
                        row_stats(dve, [y[:, j * D:(j + 1) * D] for j in range(TPC)], sums, stats, summed, n + 1, stats_ok, tick)
                        dve.wait_ge(rstd_ok, n + 1)
                        for j in range(TPC):
                            last = dve.tensor_scalar(normed[:, j * D:(j + 1) * D], y[:, j * D:(j + 1) * D],
                                                     stats[:, j, 0:1], rstd[:, j:j + 1], ALU.subtract, ALU.mult)
                        last.then_inc(chain, 1)
                        dve.wait_ge(chain, 1 + 3 * n + 2)
                        dve.tensor_tensor(rows, rows, normed[:, :], ALU.add).then_inc(chain, 1)


def sandwich(nc, a, out):
    with ExitStack() as ctx:
        c = Core(nc, ctx)
        c.x = sbuf(nc, ctx, "x", [P, TILES * D])
        c.norm = sbuf(nc, ctx, "norm", [P, TILES * D])
        c.attn = sbuf(nc, ctx, "attn", [P, TILES * D])
        c.ident = sbuf(nc, ctx, "ident_f32", [P, P])
        c.identb = sbuf(nc, ctx, "ident_bf16", [P, P], BF16)
        c.masks = sbuf(nc, ctx, "masks_bf16", [P, 4, P], BF16)
        c.tau = sbuf(nc, ctx, "tau", [P, 1])
        c.itau = sbuf(nc, ctx, "itau", [P, 3])
        c.power = sbuf(nc, ctx, "power", [P, TPC])
        c.xscale = sbuf(nc, ctx, "xscale", [P, 2])

        def dram(name, shape, dt=F32):
            return nc.dram_tensor(name, shape, dt).ap()

        d = dict(
            q1=dram("q1", [2, BATCH, AQ, PADT], F16), k1=dram("k1", [2, BATCH, AK, PADT], F16),
            v1=dram("v1", [BATCH * G, P, TPB + 1, NB + 1]), m1=dram("m1", [G, 2, 2, HG * TPC, P], F16),
            qk2=[dram(n, [BATCH * G, 3, HD * HG, S], BF16) for n in ("q2", "k2")],
            v2=dram("v2", [BATCH * G, P, TPB, HG, HD + 1]), m2=dram("m2", [G, 2, 3, HG * TPC, P], BF16),
            h=dram("h", [BATCH * CPB, P, KD * CH]))

        with ExitStack() as first:
            c.masksf = sbuf(nc, first, "masks_f32", [P, 4, P])
            phase_load(c, a)
            c.end_phase()
        phase_qkv_first(c, a, d)
        c.end_phase()

        def q1_loads(b, g):
            return [((32 * e + NB * w, 32 * e + NB * w + NB),
                     d["q1"][(0, 1, 0)[e], ds(b, 1), g * 32:(g + 1) * 32, w:w + S].rearrange("b (n h) t -> (b n) h t", h=HG))
                    for e in range(3) for w in range(TAPS)]

        def k1_loads(b, g):
            return [((32 * e + NB * w, 32 * e + NB * w + NB),
                     d["k1"][(0, 0, 1)[e], ds(b, 1), g * NB:(g + 1) * NB, w:w + S].rearrange("b n t -> n b t"))
                    for e in range(3) for w in range(TAPS)]

        def v1_load(b, g):
            return d["v1"][ds(b * G + g, 1), :, 1:, :].rearrange("n p k e -> (n p) k e").unsqueeze(2)

        def consts1(Q, K):
            return [(t[96:98, :, :], a["qbias"]) for t in Q] + [(t[96:100, 0, :], a["kbias"]) for t in K]

        phase_attention(c, "a1", F16, q1_loads, k1_loads, v1_load, d["m1"], consts1, True, NB, 2, 2,
                        c.itau[:, 2:3], -60000.0, c.masks[:, 0, :], c.masks[:, 1, :], AQ)
        c.end_phase()
        phase_out_first(c, a)
        c.end_phase()

        with ExitStack() as mid:
            m = dict(Bp=[sbuf(nc, mid, f"Bp{e}", [P, BATCH * S], BF16) for e in range(3)],
                      dp=sbuf(nc, mid, "dp", [3 * SH, BATCH * S], BF16), dm=sbuf(nc, mid, "dm", [SH, CH], BF16),
                      CT=sbuf(nc, mid, "CT", [P, BATCH * S]), xT=c.attn)
            phase_fp8_and_ssm_inputs(c, a, m)
            c.end_phase()
            phase_ssm(c, a, m)
            c.end_phase()
        phase_qkv_second(c, a, d)
        c.end_phase()

        def q2_loads(b, g):
            return [(rows, d["qk2"][0][ds(b * G + g, 1), 0:e].rearrange("b e (n h) t -> (b e n) h t", h=HG))
                    for rows, e in (((0, 48), 3), ((48, 80), 2), ((80, 96), 1))]

        def k2_loads(b, g):
            return [((16 * i, 16 * i + 16), d["qk2"][1][ds(b * G + g, 1), e].rearrange("b (n h) t -> (b n) h t", h=HG))
                    for i, e in enumerate((0, 0, 0, 1, 1, 2))]

        def v2_load(b, g):
            return d["v2"][ds(b * G + g, 1)].rearrange("n p k h e -> (n p) k h e")

        def consts2(Q, K):
            return [(t[96:99, :, :], a["kones"]) for t in K]

        phase_attention(c, "a2", BF16, q2_loads, k2_loads, v2_load, d["m2"], consts2, False, HD, 0, 3,
                        HD ** -0.5, MASKED, c.masks[:, 2, :], c.masks[:, 3, :], D)
        c.end_phase()
        phase_mlp(c, a, d, out)


def shape_constants():
    r = np.arange(S, dtype=np.float32)
    k, q = np.arange(P)[:, None], np.arange(P)[None, :]
    masks = np.stack([np.where(hidden, np.float32(MASKED), np.float32(0))
                      for hidden in (k >= q, k <= q, k > q, k < q)]).astype(np.float32)
    bias = (S * np.sqrt(TAPS * NB) / (r.astype(np.float64) + 1))
    high = bias.astype(np.float16)
    low = (bias - high).astype(np.float16)
    qbias = np.broadcast_to(np.stack([high, low])[:, None, :], (2, HG, S))
    kbias = np.stack([r / S, r / S, np.ones(S), np.ones(S)]).astype(np.float16)
    return dict(ident=np.eye(P, dtype=np.float32), masks=masks, qbias=np.ascontiguousarray(qbias), kbias=kbias)


def kernel(**inputs):
    import concourse.bacc as bacc
    from concourse.bass_utils import run_bass_kernel_spmd

    i = {k: np.asarray(v) for k, v in inputs.items()}

    def heads_last(w, groups, per):
        return w.reshape(groups, per, -1, w.shape[-1]).transpose(0, 2, 1, 3).reshape(w.shape)

    def column(v):
        return v.reshape(KD, P).T

    arrays = dict(
        x=i["L0_attn_hidden_states"], tau=i["L0_attn_tau"].reshape(1),
        wq1=heads_last(i["L0_attn_Wq"], G, HG).T, wk1=i["L0_attn_Wk"].T, wv1=i["L0_attn_Wv"].T, wo1=i["L0_attn_Wo"].T,
        emb0=i["L0_attn_v_emb0"].reshape(P, 1), emb1=i["L0_attn_v_emb1"].reshape(P, 1),
        wf=i["L0_ffn_weight"].T, wx=i["L1_attn_Wx"], wg=i["L1_attn_Wg"], bg=column(i["L1_attn_bg"]),
        wo3=i["L1_attn_Wo"], ssmA=i["L1_attn_A"].T, skip=column(np.repeat(i["L1_attn_Dp"], SHD)),
        ln1=column(i["L1_ffn_ln1_w"]), ln2=column(i["L1_ffn_ln2_w"]),
        wq2=heads_last(i["L1_ffn_Wq"], G, HG).T, wk2=heads_last(i["L1_ffn_Wk"], G, HG).T,
        wv2=i["L1_ffn_Wv"].T, wo4=i["L1_ffn_Wo"].T, loraA=i["L1_ffn_A"], loraB=i["L1_ffn_B"],
        win=i["L1_ffn_W_in_base"].T, wup=i["L1_ffn_W_up_base"].T, wdown=i["L1_ffn_W_down"].T,
        kones=np.ones((3, HG, S), i["L0_ffn_weight"].dtype), **shape_constants())
    nc = bacc.Bacc("TRN2", target_bir_lowering=False, num_devices=1)
    feed, handles = {}, {}
    for name, v in arrays.items():
        v = np.ascontiguousarray(v)
        feed["in_" + name] = v
        handles[name] = nc.dram_tensor("in_" + name, v.shape, mybir.dt.from_np(v.dtype), kind="ExternalInput").ap()
    out = nc.dram_tensor("out", (BATCH, S, D), F32, kind="ExternalOutput").ap()
    sandwich(nc, handles, out)
    result = run_bass_kernel_spmd(nc, [feed], core_ids=[0])
    return result.results[0]["out"]
```

```python
from contextlib import ExitStack

import concourse.bass as bass
import numpy as np
from concourse import mybir

F32 = mybir.dt.float32
F16 = mybir.dt.float16
BF16 = mybir.dt.bfloat16
I32 = mybir.dt.int32
ALU = mybir.AluOpType
ACT = mybir.ActivationFunctionType
AX_X = mybir.AxisListType.X
RMAX = bass.bass_isa.ReduceOp.max
ds = bass.ds

P = 128
BATCH, S, D = 4, 1024, 256
KD = D // P
TILES = BATCH * S // P
TPB = S // P
CH = 512
TPC = CH // P
CPB = S // CH
G = 4
HG = 4
EPS = 1e-5
RMS_EPS = 1e-6
MASKED = -3e38
TAPS, NB = 4, 8
AQ, AK = 128, 32
PADT = S + TAPS
HD = 16
N, SH, SHD = 128, 32, 8
F, R = 1024, 16
FT = F // P
E4M3_MAX = 448.0
SAT = 40.0


class Core:

    def __init__(self, nc, ctx):
        self.nc, self.ctx, self.sems = nc, ctx, []

    def sem(self, name):
        self.sems.append(self.nc.alloc_semaphore(name=name))
        return self.sems[-1]

    def end_phase(self):
        self.nc.clear_and_free_semaphores(self.sems)
        self.sems = []
        self.nc.all_engine_barrier()


def sbuf(nc, ctx, name, shape, dt=F32):
    return ctx.enter_context(nc.sbuf_tensor(name, shape, dt))


def psum(nc, ctx, name, shape, dt=F32):
    return ctx.enter_context(nc.psum_tensor(name, shape, dt))


def wait_alone(eng, sem, value, tick):
    eng.wait_ge(sem, value)
    eng.sem_inc(tick, 1)


def row_stats(dve, tiles, sums, stats, summed, count, ready, tick):
    for j, tile in enumerate(tiles):
        last = dve.bn_stats(sums[:, j, :], tile)
    last.then_inc(summed, 1)
    wait_alone(dve, summed, count, tick)
    for j in range(len(tiles)):
        last = dve.bn_aggr(stats[:, j, :], sums[:, j, :])
    last.then_inc(ready, 1)


def rows_rstd(pool, variance_ok, nth, rstd, variance, eps, power, added, count, ready, tick):
    wait_alone(pool, variance_ok, nth, tick)
    pool.tensor_scalar(rstd, variance, eps, None, ALU.add).then_inc(added, 1)
    pool.wait_ge(added, count)
    pool.tensor_tensor(rstd, rstd, power[:, :], ALU.pow).then_inc(ready, 1)


def phase_load(c, a):
    nc = c.nc
    loaded, made = c.sem("loaded"), c.sem("made")
    with nc.Block() as block:

        @block.sync
        def _(sp):
            for b in range(BATCH):
                sp.dma_start(c.x[:, b * TPB * D:(b + 1) * TPB * D].rearrange("p (n d) -> p n d", d=D),
                             a["x"][b].rearrange("(n p) d -> p n d", p=P)).then_inc(loaded, 16)
            sp.dma_start(c.ident[:, :], a["ident"]).then_inc(loaded, 16)
            sp.dma_start(c.masksf[:, :, :], a["masks"].rearrange("m p q -> p m q")).then_inc(loaded, 16)
            sp.wait_ge(loaded, 16 * (BATCH + 2))

        @block.vector
        def _(dve):
            dve.wait_ge(loaded, 16 * (BATCH + 2))
            dve.memset(c.power[:, :], -0.5)
            dve.tensor_copy(c.identb[:, :], c.ident[:, :])
            dve.tensor_copy(c.masks[:, :, :], c.masksf[:, :, :])


def phase_qkv_first(c, a, d):
    nc = c.nc
    with ExitStack() as ctx:
        wq = sbuf(nc, ctx, "p1_wq", [P, KD, AQ])
        wk = sbuf(nc, ctx, "p1_wk", [P, KD, AK])
        wv = sbuf(nc, ctx, "p1_wv", [P, KD, AK])
        sums = sbuf(nc, ctx, "p1_sums", [P, CPB, TPC, 6])
        stats = sbuf(nc, ctx, "p1_stats", [P, CPB, TPC, 2])
        rstd = sbuf(nc, ctx, "p1_rstd", [P, CPB, TPC])
        xn = sbuf(nc, ctx, "p1_xn", [P, CPB, TPC * D])
        xT = sbuf(nc, ctx, "p1_xT", [P, CPB, KD, CH])
        qf = sbuf(nc, ctx, "p1_qf", [P, CPB, CH])
        kf = sbuf(nc, ctx, "p1_kf", [AK, CPB, CH])
        vf = sbuf(nc, ctx, "p1_vf", [P, CPB, TPC, AK])
        qp = sbuf(nc, ctx, "p1_qp", [P, CPB, 2, CH], F16)
        kp = sbuf(nc, ctx, "p1_kp", [AK, CPB, 2, CH], F16)
        vx = sbuf(nc, ctx, "p1_vx", [P, CPB, TPC, G, NB + 1])
        zeros = sbuf(nc, ctx, "p1_zeros", [P, 2, BATCH, TAPS], F16)
        last_v = sbuf(nc, ctx, "p1_last_v", [16, NB + 1])
        psT = [psum(nc, ctx, f"p1_psT{i}", [P, KD, CH]) for i in range(CPB)]
        psQ = psum(nc, ctx, "p1_psQ", [P, CH])
        psK = psum(nc, ctx, "p1_psK", [AK, CH])
        psV = psum(nc, ctx, "p1_psV", [P, TPC, AK])
        w_in, itau = c.sem("p1_w_in"), c.sem("p1_itau")
        const_ok = c.sem("p1_const_ok")
        summed, stats_ok, rstd_ok, xn_ok = (c.sem("p1_" + n) for n in ("summed", "stats_ok", "rstd_ok", "xn_ok"))
        added = c.sem("p1_added")
        tick, tick_pool = c.sem("p1_tick"), c.sem("p1_tick_pool")
        turned, xT_ok, proj_ok = (c.sem("p1_" + n) for n in ("turned", "xT_ok", "proj_ok"))
        tanh_ok, split_ok, parts_ok, stored = (c.sem("p1_" + n) for n in ("tanh_ok", "split_ok", "parts_ok", "stored"))

        with nc.Block() as block:

            @block.sync
            def _(sp):
                for w, src in ((wq, a["wq1"]), (wk, a["wk1"]), (wv, a["wv1"])):
                    sp.dma_start(w[:, :, :], src.rearrange("(k p) n -> p k n", p=P)).then_inc(w_in, 16)
                sp.dma_start(c.tau[:, :], a["tau"].partition_broadcast(P)).then_inc(w_in, 16)
                sp.wait_ge(const_ok, 1)
                sp.dma_start(d["q1"][:, :, :, 0:TAPS].rearrange("e b r t -> r e b t"), zeros[:, :, :, :]).then_inc(stored, 16)
                sp.dma_start(d["k1"][:, :, :, 0:TAPS].rearrange("e b r t -> r e b t"), zeros[0:AK, :, :, :]).then_inc(stored, 16)
                sp.dma_start(d["v1"][:, P - 1:P, TPB:TPB + 1, :].rearrange("n p k d -> (n p k) d"),
                             last_v[:, :]).then_inc(stored, 16)
                sp.wait_ge(stored, 48)
                with sp.Fori(0, BATCH) as b:
                    for ch in range(CPB):
                        sp.wait_ge(parts_ok, b * CPB + ch + 1)
                        t0 = TAPS - 1 + ch * CH
                        for e in range(2):
                            sp.dma_start(d["q1"][e, ds(b, 1), :, t0:t0 + CH].rearrange("b r t -> (b r) t"),
                                         qp[:, ch, e, :]).then_inc(stored, 16)
                            sp.dma_start(d["k1"][e, ds(b, 1), :, t0:t0 + CH].rearrange("b r t -> (b r) t"),
                                         kp[:, ch, e, :]).then_inc(stored, 16)
                        v1b = d["v1"][ds(b * G, G)]
                        for g in range(G):
                            sp.dma_start(v1b[g, 0:P - 1, ch * TPC + 1:ch * TPC + TPC + 1, :], vx[1:P, ch, :, g, :]).then_inc(stored, 16)
                            sp.dma_start(v1b[g, P - 1:P, ch * TPC:ch * TPC + TPC, :], vx[0:1, ch, :, g, :]).then_inc(stored, 16)
                sp.wait_ge(stored, 48 + 16 * 12 * BATCH * CPB)

            @block.vector
            def _(dve):
                dve.memset(zeros[:, :, :, :], 0.0)
                dve.memset(last_v[:, :], 1.0)
                dve.memset(vx[:, :, :, :, :], 1.0).then_inc(const_ok, 1)
                dve.wait_ge(w_in, 64)
                dve.reciprocal(c.itau[:, 0:1], c.tau[:, :]).then_inc(itau, 1)
                dve.wait_ge(itau, 1)
                dve.tensor_scalar(c.itau[:, 1:2], c.itau[:, 0:1], 0.5, None, ALU.mult).then_inc(itau, 1)
                dve.tensor_scalar(c.itau[:, 2:3], c.itau[:, 0:1], (TAPS * NB) ** -0.5, None, ALU.mult)

                def normalise(n, ch):
                    tiles = [ds(n * TPC * D + j * D, D) for j in range(TPC)]
                    row_stats(dve, [c.x[:, r] for r in tiles], sums[:, ch], stats[:, ch], summed, n + 1, stats_ok, tick)
                    dve.wait_ge(rstd_ok, n + 1)
                    dve.wait_ge(turned, n + 1)
                    for j, r in enumerate(tiles):
                        last = dve.tensor_scalar(xn[:, ch, j * D:(j + 1) * D], c.x[:, r],
                                                 stats[:, ch, j, 0:1], rstd[:, ch, j:j + 1], ALU.subtract, ALU.mult)
                    last.then_inc(xn_ok, 1)

                def split(n, ch):
                    dve.wait_ge(tanh_ok, n + 2)
                    dve.wait_ge(stored, 48 + 192 * n)
                    dve.tensor_copy(qp[:, ch, 0, :], qf[:, ch, :])
                    dve.tensor_copy(kp[:, ch, 0, :], kf[:, ch, :]).then_inc(split_ok, 1)
                    for g in range(G):
                        dve.tensor_scalar(vx[:, ch, :, g, 0:NB], vf[:, ch, :, g * NB:(g + 1) * NB], 0.5, 0.5, ALU.mult, ALU.add)
                    dve.wait_ge(split_ok, n + 1)
                    dve.tensor_tensor(qp[:, ch, 1, :], qf[:, ch, :], qp[:, ch, 0, :], ALU.subtract)
                    dve.tensor_tensor(kp[:, ch, 1, :], kf[:, ch, :], kp[:, ch, 0, :], ALU.subtract).then_inc(parts_ok, 1)

                def batch(b, last):
                    for ch in range(CPB):
                        n = b * CPB + ch
                        if not (last and ch == CPB - 1):
                            normalise(n + 1, 1 - ch)
                        split(n, ch)

                normalise(0, 0)
                with dve.Fori(0, BATCH - 1) as b:
                    batch(b, False)
                batch(BATCH - 1, True)

            @block.gpsimd
            def _(pool):
                with pool.Fori(0, BATCH) as b:
                    for ch in range(CPB):
                        rows_rstd(pool, stats_ok, b * CPB + ch + 1, rstd[:, ch, :], stats[:, ch, :, 1], EPS, c.power, added, b * CPB + ch + 1, rstd_ok, tick_pool)

            @block.tensor
            def _(pe):
                pe.sem_inc(turned, 2)
                pe.wait_ge(w_in, 64)

                def turn(n, ch):
                    pe.wait_ge(xn_ok, n + 1)
                    for j in range(TPC):
                        for k in range(KD):
                            last = pe.transpose(psT[ch][:, k, j * P:(j + 1) * P], xn[:, ch, j * D + k * P:j * D + (k + 1) * P], c.ident[:, :])
                    last.then_inc(turned, 1)

                def projections(n, ch):
                    pe.wait_ge(xT_ok, n + 1)
                    pe.wait_ge(tanh_ok, n + 1)
                    for k in range(KD):
                        pe.matmul(psQ[:, :], wq[:, k, :], xT[:, ch, k, :], start=k == 0, stop=k == KD - 1)
                    for k in range(KD):
                        pe.matmul(psK[:, :], wk[:, k, :], xT[:, ch, k, :], start=k == 0, stop=k == KD - 1)
                    for j in range(TPC):
                        for k in range(KD):
                            last = pe.matmul(psV[:, j, :], xT[:, ch, k, j * P:(j + 1) * P], wv[:, k, :], start=k == 0, stop=k == KD - 1)
                    last.then_inc(proj_ok, 1)

                def batch(b, last):
                    for ch in range(CPB):
                        n = b * CPB + ch
                        projections(n, ch)
                        if not (last and ch == CPB - 1):
                            turn(n + 1, 1 - ch)

                turn(0, 0)
                with pe.Fori(0, BATCH - 1) as b:
                    batch(b, False)
                batch(BATCH - 1, True)

            @block.scalar
            def _(act):
                act.preload_act_table_set("exp_and_others")
                act.sem_inc(tanh_ok, 1)
                act.wait_ge(itau, 2)

                def keep(n, ch):
                    act.wait_ge(turned, n + 3)
                    act.activation(xT[:, ch, :, :], psT[ch][:, :, :], ACT.Copy).then_inc(xT_ok, 1)

                def tanhs(n, ch):
                    act.wait_ge(proj_ok, n + 1)
                    act.activation(qf[:, ch, :], psQ[:, :], ACT.Tanh, scale=c.itau[:, 0:1])
                    act.activation(kf[:, ch, :], psK[:, :], ACT.Tanh, scale=c.itau[0:AK, 0:1])
                    act.activation(vf[:, ch, :, :], psV[:, :, :], ACT.Tanh, scale=c.itau[:, 1:2]).then_inc(tanh_ok, 1)

                def batch(b, last):
                    for ch in range(CPB):
                        n = b * CPB + ch
                        tanhs(n, ch)
                        if not (last and ch == CPB - 1):
                            keep(n + 1, 1 - ch)

                keep(0, 0)
                with act.Fori(0, BATCH - 1) as b:
                    batch(b, False)
                batch(BATCH - 1, True)


def max_tiles():
    halves = []
    for tiles in (range(0, TPC), range(TPC, TPB)):
        out = []
        for qt in tiles:
            for half in range(qt // TPC + 1):
                keys = min(CH, (qt + 1) * P - half * CH)
                heads = {1: 4, 2: 2}.get(keys // P, 1)
                for h in range(0, HG, heads):
                    out.append((qt, half, h, heads, half * CH, keys, half == qt // TPC))
        halves.append(out)
    return halves


MAX_TILES = max_tiles()
MAX_COUNT = len(MAX_TILES[0]) + len(MAX_TILES[1])
UNITS = [(qc, kt, max(0, kt - qc * TPC) * P) for qc in range(CPB) for kt in range((qc + 1) * TPC)]
NU = len(UNITS)


def group_order(g, maxima):
    width = np.cumsum([CH - q0 for _, _, q0 in UNITS])
    order, taken = [], 0
    for u in range(NU):
        upto = min(MAX_COUNT, -(-MAX_COUNT * int(width[u]) // int(width[NU - 2]))) if maxima else 0
        some, taken = [("max", m) for m in range(taken, upto)], upto
        if u + 1 < NU:
            scores = [("scores", 2 * (u + 1) + pair) for pair in range(2)]
        else:
            scores = [("next", pair) for pair in range(2)] if maxima else []
        half = -(-len(some) // 2)
        order += scores[0:1] + some[0:1] + scores[1:2] + some[1:half] + [("values", u)] + some[half:]
        if u == 0 and g > 0:
            order += [("turn", -1), ("divide", -1)]
        if maxima and u == 5:
            order.append(("finish", 0))
        if maxima and u == 6:
            order += [("turn_max", 0), ("split", 0)]
        if maxima and u == NU - 2:
            order.append(("finish", 1))
        if u == TPC - 1:
            order.append(("evict", 0))
        if u == TPC:
            order += [("turn", 0), ("divide", 0)]
    order.append(("evict", 1))
    if maxima:
        order += [("turn_max", 1), ("split", 1)]
    return order + ([("turn", 1), ("divide", 1)] if g == G - 1 else [])


def first_order():
    done = len(MAX_TILES[0])
    return ([("max", m) for m in range(done)] + [("finish", 0), ("turn_max", 0), ("split", 0)]
            + [("max", m) for m in range(done, MAX_COUNT)] + [("finish", 1), ("turn_max", 1), ("split", 1)]
            + [("next", 0), ("next", 1)])


def turns_before(b, g):
    return 2 + 4 * G * b + (4 * g - 1 if g else 0)


def phase_attention(c, name, dt, q_loads, k_loads, v_load, m_scr, consts, shared_keys, dim, bias_rows,
                    m_parts, scale, clip, mask_k, mask_q, out_row):
    nc = c.nc
    MR = 96 + bias_rows
    ROWS = MR + m_parts
    M = dim + 1
    KH = 1 if shared_keys else HG
    with ExitStack() as ctx:
        Q = [sbuf(nc, ctx, f"{name}_Q{g}", [P, HG, S], dt) for g in range(G)]
        K = [sbuf(nc, ctx, f"{name}_K{g}", [P, KH, S], dt) for g in range(G)]
        V = [sbuf(nc, ctx, f"{name}_V{g}", [P, TPB, KH, M]) for g in range(G)]
        E = [[sbuf(nc, ctx, f"{name}_E{i}{j}", [P, 2, CH]) for j in range(2)] for i in range(2)]
        OT = sbuf(nc, ctx, name + "_OT", [P, CH])
        den = sbuf(nc, ctx, name + "_den", [P, 2, TPC, HG])
        mx = sbuf(nc, ctx, name + "_mx", [P, 2, HG, TPB])
        mall = sbuf(nc, ctx, name + "_mall", [P, HG, TPC])
        nm = sbuf(nc, ctx, name + "_nm", [P, 2, HG, TPC])
        res = sbuf(nc, ctx, name + "_res", [HG * TPC, 2, P])
        mp = sbuf(nc, ctx, name + "_mp", [HG * TPC, 2, m_parts, P], dt)
        clear = sbuf(nc, ctx, name + "_clear", [P, CH], BF16)
        psM = [psum(nc, ctx, f"{name}_psM{i}", [P, CH]) for i in range(2)]
        psS = [psum(nc, ctx, f"{name}_psS{i}", [P, 2, CH]) for i in range(2)]
        psO = psum(nc, ctx, name + "_psO", [P, CH])
        psX = psum(nc, ctx, name + "_psX", [P, CH])
        const_in, clear_ok = c.sem(name + "_const_in"), c.sem(name + "_clear_ok")
        stack_in = [c.sem(f"{name}_stack_in{g}") for g in range(G)]
        m_out = [c.sem(f"{name}_m_out{i}") for i in range(2)]
        m_in = [[c.sem(f"{name}_m_in{g}{i}") for i in range(2)] for g in range(G)]
        max_ready, max_taken = c.sem(name + "_max_ready"), c.sem(name + "_max_taken")
        m_all, nm_ok, split_ok, mp_ok = (c.sem(f"{name}_{n}") for n in ("m_all", "nm_ok", "split_ok", "mp_ok"))
        x_ready, x_taken = c.sem(name + "_x_ready"), c.sem(name + "_x_taken")
        s_ready, e_ready, pv_done, o_copied = (c.sem(f"{name}_{n}") for n in ("s_ready", "e_ready", "pv_done", "o_copied"))
        den_ok = c.sem(name + "_den_ok")
        LOADS = len(q_loads(0, 0)) + len(k_loads(0, 0)) + 1

        with nc.Block() as block:

            @block.sync
            def _(sp):
                for dst, src in consts(Q, K):
                    sp.dma_start(dst, src).then_inc(const_in, 16)

                def load(b, g):
                    for rows, src in q_loads(b, g):
                        sp.dma_start(Q[g][rows[0]:rows[1], :, :], src).then_inc(stack_in[g], 16)
                    for rows, src in k_loads(b, g):
                        sp.dma_start(K[g][rows[0]:rows[1], :, :], src).then_inc(stack_in[g], 16)
                    sp.dma_start(V[g][:, :, :, :], v_load(b, g)).then_inc(stack_in[g], 16)

                def maxima(b, g, n):
                    for i in range(2):
                        sp.wait_ge(mp_ok, 2 * n + i + 1)
                        sp.dma_start(m_scr[g, i].rearrange("e r q -> r e q"), mp[:, i, :, :]).then_inc(m_out[i], 16)
                        sp.wait_ge(m_out[i], 16 * (n + 2))
                        sp.dma_start(Q[g][MR:ROWS, :, i * CH:(i + 1) * CH],
                                     m_scr[g, i].rearrange("e (h j) q -> e h (j q)", h=HG)).then_inc(m_in[g][i], 16)

                for i in range(2):
                    sp.sem_inc(m_out[i], 16)
                load(0, 0)
                load(0, 1)
                maxima(0, 0, 0)
                load(0, 2)
                load(0, 3)

                def batch(b, last):
                    for g in range(G):
                        n = b * G + g
                        if not (last and g == G - 1):
                            maxima(b + (g == G - 1), (g + 1) % G, n + 1)
                        if not last:
                            sp.wait_ge(pv_done, 2 + (n + 1) * NU)
                            load(b + 1, g)

                with sp.Fori(0, BATCH - 1) as b:
                    batch(b, False)
                batch(BATCH - 1, True)

            @block.tensor
            def _(pe):
                pe.sem_inc(pv_done, 2)
                pe.wait_ge(clear_ok, 1)
                pe.matmul(psO[:, :], clear[:, 0:P], clear[:, :], start=True, stop=True)
                pe.wait_ge(const_in, 16 * len(consts(Q, K)))

                def scores(n, b, g, u, pair):
                    qc, kt, q0 = UNITS[u]
                    if kt == 0 and pair == 0:
                        pe.wait_ge(m_in[g][qc], 16 * (b + 1))
                    pe.wait_ge(e_ready, 2 * (n * NU + u) + pair + 1)
                    for h in range(2):
                        head = 2 * pair + h
                        diag = kt >= qc * TPC
                        last = pe.matmul(psS[pair][:, h, q0:CH], K[g][0:ROWS, 0 if shared_keys else head, kt * P:(kt + 1) * P],
                                         Q[g][0:ROWS, head, qc * CH + q0:(qc + 1) * CH], start=True, stop=not diag)
                        if diag:
                            last = pe.matmul(psS[pair][:, h, q0:q0 + P], c.identb[:, :], mask_k, start=False, stop=True)
                    last.then_inc(s_ready, 1)

                def slot(n, b, g, nx, nb, order, uses):
                    nxt = (g + 1) % G
                    for what, i in order:
                        if what == "scores":
                            scores(n, b, g, i // 2, i % 2)
                        elif what == "next":
                            scores(nx, nb, nxt, 0, i)
                        elif what == "max":
                            qt, half, h0, heads, k0, keys, diag = (MAX_TILES[0] + MAX_TILES[1])[i]
                            if i == 0:
                                pe.wait_ge(stack_in[nxt], 16 * LOADS * (nb + 1))
                            pe.wait_ge(max_taken, nx * MAX_COUNT + i + 1)
                            bank = psM[i % 2]
                            for h in range(heads):
                                last = pe.matmul(bank[:, h * keys:(h + 1) * keys], Q[nxt][0:MR, h0 + h, qt * P:(qt + 1) * P],
                                                 K[nxt][0:MR, 0 if shared_keys else h0 + h, k0:k0 + keys], start=True, stop=not diag)
                                if diag:
                                    last = pe.matmul(bank[:, (h + 1) * keys - P:(h + 1) * keys], c.identb[:, :], mask_q, start=False, stop=True)
                            last.then_inc(max_ready, 1)
                        elif what == "turn_max":
                            pe.wait_ge(nm_ok, 2 * nx + i + 1)
                            pe.wait_ge(x_taken, uses + 1)
                            uses = uses + 1
                            pe.transpose(psX[0:HG * TPC, 0:P], nm[:, i, :, :].rearrange("p h t -> p (h t)"), c.ident[:, :]).then_inc(x_ready, 1)
                        elif what == "values":
                            qc, kt, q0 = UNITS[i]
                            if kt == 0:
                                pe.wait_ge(o_copied, 2 * n + qc + 1)
                            pe.wait_ge(e_ready, 2 * (n * NU + i + 1) + 2)
                            for h in range(HG):
                                last = pe.matmul(psO[32 * h:32 * h + M, q0:CH], V[g][:, kt, 0 if shared_keys else h, :],
                                                 E[i % 2][h // 2][:, h % 2, q0:CH], start=kt == 0, stop=kt == (qc + 1) * TPC - 1)
                            last.then_inc(pv_done, 1)
                        elif what == "turn":
                            pe.wait_ge(o_copied, 2 * n + i + 2 if i >= 0 else 2 * n + 1)
                            pe.wait_ge(x_taken, uses + 1)
                            uses = uses + 1
                            for j in range(TPC):
                                last = pe.transpose(psX[:, j * P:(j + 1) * P], OT[:, j * P:(j + 1) * P], c.ident[:, :])
                            last.then_inc(x_ready, 1)

                slot(0, 0, G - 1, 0, 0, first_order(), 0)

                def batch(b, last):
                    for g in range(G):
                        n = b * G + g
                        slot(n, b, g, n + 1, b + (g == G - 1), group_order(g, not (last and g == G - 1)), turns_before(b, g))

                with pe.Fori(0, BATCH - 1) as b:
                    batch(b, False)
                batch(BATCH - 1, True)

            @block.scalar
            def _(act):
                act.preload_act_table_set("exp_and_others")
                act.sem_inc(e_ready, 2)

                def batch(b):
                    for g in range(G):
                        for u, (qc, kt, q0) in enumerate(UNITS):
                            k = (b * G + g) * NU + u
                            act.wait_ge(pv_done, k + 1)
                            for pair in range(2):
                                act.wait_ge(s_ready, 2 * k + pair + 1)
                                act.activation(E[u % 2][pair][:, :, q0:CH], psS[pair][:, :, q0:CH], ACT.Exp,
                                               scale=scale).then_inc(e_ready, 1)

                with act.Fori(0, BATCH) as b:
                    batch(b)

            @block.vector
            def _(dve):
                dve.memset(mx[:, 1, :, 0:TPC], MASKED)
                dve.memset(clear[:, :], 0.0).then_inc(clear_ok, 1)
                dve.wait_ge(clear_ok, 1)
                dve.sem_inc(max_taken, 2)
                dve.sem_inc(x_taken, 1)
                dve.sem_inc(o_copied, 1)

                def slot(n, b, g, nx, order, xs):
                    for what, i in order:
                        if what == "max":
                            qt, half, h0, heads, k0, keys, diag = (MAX_TILES[0] + MAX_TILES[1])[i]
                            dve.wait_ge(max_ready, nx * MAX_COUNT + i + 1)
                            dve.tensor_reduce(out=mx[:, half, h0:h0 + heads, qt],
                                              in_=psM[i % 2][:, 0:heads * keys].rearrange("p (h k) -> p h k", h=heads),
                                              axis=AX_X, op=ALU.max).then_inc(max_taken, 1)
                        elif what == "finish":
                            done = len(MAX_TILES[0]) if i == 0 else MAX_COUNT
                            dve.wait_ge(max_taken, 2 + nx * MAX_COUNT + done)
                            dve.tensor_tensor(mall[:, :, :], mx[:, 0, :, i * TPC:(i + 1) * TPC],
                                              mx[:, 1, :, i * TPC:(i + 1) * TPC], ALU.max).then_inc(m_all, 1)
                            dve.wait_ge(m_all, 2 * nx + i + 1)
                            dve.tensor_scalar(nm[:, i, :, :], mall[:, :, :], clip, -1.0, ALU.max, ALU.mult).then_inc(nm_ok, 1)
                        elif what == "split":
                            xs = xs + 1
                            dve.wait_ge(x_ready, xs)
                            dve.wait_ge(m_out[i], 16 * (nx + 1))
                            src = psX[0:HG * TPC, 0:P]
                            for e in range(m_parts):
                                w = 2 * m_parts - 1
                                dve.tensor_copy(mp[:, i, e, :], src).then_inc(split_ok, 1)
                                if e + 1 < m_parts:
                                    dve.wait_ge(split_ok, (2 * nx + i) * w + 2 * e + 1)
                                    dve.tensor_tensor(res[:, e % 2, :], src, mp[:, i, e, :], ALU.subtract).then_inc(split_ok, 1)
                                    dve.wait_ge(split_ok, (2 * nx + i) * w + 2 * e + 2)
                                    src = res[:, e % 2, :]
                            dve.wait_ge(split_ok, (2 * nx + i + 1) * w)
                            dve.sem_inc(mp_ok, 1)
                            dve.sem_inc(x_taken, 1)
                        elif what == "evict":
                            dve.wait_ge(pv_done, 2 + n * NU + (TPC if i == 0 else NU))
                            dve.tensor_copy(OT[:, :], psO[:, :]).then_inc(o_copied, 1)
                        elif what == "divide":
                            xs = xs + 1
                            dve.wait_ge(x_ready, xs)
                            turned = psX[:, :].rearrange("p (j h e) -> p j h e", j=TPC, h=HG)
                            dve.tensor_scalar(den[:, 0, :, :], turned[:, :, :, M - 1], 1e-30, None, ALU.max).then_inc(den_ok, 1)
                            dve.wait_ge(den_ok, 2 * (2 * n + i) + 1)
                            dve.reciprocal(den[:, 1, :, :], den[:, 0, :, :]).then_inc(den_ok, 1)
                            dve.wait_ge(den_ok, 2 * (2 * n + i) + 2)
                            at, og = (i, g) if i >= 0 else (1, g - 1)
                            out = c.attn[:, ds((b * TPB + at * TPC) * out_row, TPC * out_row)].rearrange("p (j w) -> p j w", j=TPC)
                            out = out[:, :, og * HG * dim:(og + 1) * HG * dim].rearrange("p j (h e) -> p j h e", h=HG)
                            dve.tensor_tensor(out, turned[:, :, :, 0:dim],
                                              den[:, 1, :, :].unsqueeze(3).broadcast_to([P, TPC, HG, dim]), ALU.mult).then_inc(x_taken, 1)

                slot(0, 0, 0, 0, first_order(), 0)

                def batch(b, last):
                    for g in range(G):
                        n = b * G + g
                        slot(n, b, g, n + 1, group_order(g, not (last and g == G - 1)), turns_before(b, g))

                with dve.Fori(0, BATCH - 1) as b:
                    batch(b, False)
                batch(BATCH - 1, True)


def phase_out_first(c, a):
    nc = c.nc
    with ExitStack() as ctx:
        wo = sbuf(nc, ctx, "p3_wo", [P, D])
        emb = sbuf(nc, ctx, "p3_emb", [P, 3])
        at = sbuf(nc, ctx, "p3_at", [P, CPB, TPC * AQ])
        aT = sbuf(nc, ctx, "p3_aT", [P, CPB, CH])
        sums = sbuf(nc, ctx, "p3_sums", [P, 2, TPC, 6])
        stats = sbuf(nc, ctx, "p3_stats", [P, 2, TPC, 2])
        rstd = sbuf(nc, ctx, "p3_rstd", [P, 2, TPC])
        normed = sbuf(nc, ctx, "p3_normed", [P, TPC * D])
        amax = sbuf(nc, ctx, "p3_amax", [P, BATCH * CPB])
        rmax = sbuf(nc, ctx, "p3_rmax", [P, 2])
        psA = [psum(nc, ctx, f"p3_psA{i}", [P, CH]) for i in range(CPB)]
        psO = [psum(nc, ctx, f"p3_psO{i}", [P, TPC * D]) for i in range(CPB)]
        w_in, emb_ok, at_ok, turned, aT_ok, out_ok = (c.sem("p3_" + n) for n in ("w_in", "emb_ok", "at_ok", "turned", "aT_ok", "out_ok"))
        summed, stats_ok, rstd_ok, chain = (c.sem("p3_" + n) for n in ("summed", "stats_ok", "rstd_ok", "chain"))
        added = c.sem("p3_added")
        tick, tick_pool = c.sem("p3_tick"), c.sem("p3_tick_pool")
        norm_ok, amax_ok, max_ok, all_max = (c.sem("p3_" + n) for n in ("norm_ok", "amax_ok", "max_ok", "all_max"))

        with nc.Block() as block:

            @block.sync
            def _(sp):
                sp.dma_start(wo[:, :], a["wo1"]).then_inc(w_in, 16)
                sp.dma_start(emb[:, 0:1], a["emb0"]).then_inc(w_in, 16)
                sp.dma_start(emb[:, 1:2], a["emb1"]).then_inc(w_in, 16)
                sp.wait_ge(w_in, 48)

            @block.gpsimd
            def _(pool):

                def copy(n, ch):
                    pool.wait_ge(turned, n + 1)
                    pool.tensor_copy(at[:, ch, :], c.attn[:, ds(n * TPC * AQ, TPC * AQ)]).then_inc(at_ok, 1)

                def rstd_of(k, count):
                    rows_rstd(pool, stats_ok, count, rstd[:, k, :], stats[:, k, :, 1], EPS, c.power, added, count, rstd_ok, tick_pool)

                def batch(b, last):
                    for ch in range(CPB):
                        n = b * CPB + ch
                        more = not (last and ch == CPB - 1)
                        if not last:
                            copy(n + 2, ch)
                        if more:
                            rstd_of(0, 2 * n + 2)
                        rstd_of(1, 2 * n + 2 + more)

                copy(0, 0)
                copy(1, 1)
                rstd_of(0, 1)
                with pool.Fori(0, BATCH - 1) as b:
                    batch(b, False)
                batch(BATCH - 1, True)
                pool.wait_ge(max_ok, 1)
                pool.partition_all_reduce(rmax[:, 1:2], rmax[:, 0:1], P, RMAX).then_inc(all_max, 1)

            @block.tensor
            def _(pe):
                pe.sem_inc(turned, 2)
                pe.wait_ge(w_in, 48)
                with pe.Fori(0, BATCH) as b:
                    for ch in range(CPB):
                        n = b * CPB + ch
                        pe.wait_ge(at_ok, n + 1)
                        for j in range(TPC):
                            last = pe.transpose(psA[ch][:, j * P:(j + 1) * P], at[:, ch, j * AQ:(j + 1) * AQ], c.ident[:, :])
                        last.then_inc(turned, 1)
                        pe.wait_ge(aT_ok, n + 1)
                        pe.wait_ge(chain, 2 * n + 1)
                        for j in range(TPC):
                            last = pe.matmul(psO[ch][:, j * D:(j + 1) * D], aT[:, ch, j * P:(j + 1) * P], wo[:, :], start=True, stop=True)
                        last.then_inc(out_ok, 1)

            @block.scalar
            def _(act):
                act.wait_ge(emb_ok, 1)
                with act.Fori(0, BATCH) as b:
                    for ch in range(CPB):
                        n = b * CPB + ch
                        act.wait_ge(turned, n + 3)
                        act.activation(aT[:, ch, :], psA[ch][:, :], ACT.Identity, scale=emb[:, 2:3], bias=emb[:, 0:1]).then_inc(aT_ok, 1)

            @block.vector
            def _(dve):
                dve.wait_ge(w_in, 48)
                dve.tensor_tensor(emb[:, 2:3], emb[:, 1:2], emb[:, 0:1], ALU.subtract).then_inc(emb_ok, 1)
                dve.sem_inc(chain, 3)

                def projected_stats(n, ch, count):
                    dve.wait_ge(out_ok, n + 1)
                    row_stats(dve, [psO[ch][:, j * D:(j + 1) * D] for j in range(TPC)], sums[:, 0], stats[:, 0], summed, count, stats_ok, tick)

                def update(n, ch, count):
                    rows = c.x[:, ds(n * TPC * D, TPC * D)]
                    dve.wait_ge(rstd_ok, count)
                    for j in range(TPC):
                        last = dve.tensor_scalar(normed[:, j * D:(j + 1) * D], psO[ch][:, j * D:(j + 1) * D],
                                                 stats[:, 0, j, 0:1], rstd[:, 0, j:j + 1], ALU.subtract, ALU.mult)
                    last.then_inc(chain, 1)
                    dve.wait_ge(chain, 3 + 2 * n + 1)
                    dve.tensor_tensor(rows, rows, normed[:, :], ALU.add).then_inc(chain, 1)

                def magnitude(n):
                    dve.wait_ge(norm_ok, n + 1)
                    dve.tensor_reduce(out=amax[:, ds(n, 1)], in_=c.norm[:, ds(n * TPC * D, TPC * D)], axis=AX_X, op=ALU.max,
                                      apply_absolute_value=True).then_inc(amax_ok, 1)

                def batch(b, last):
                    for ch in range(CPB):
                        n = b * CPB + ch
                        more = not (last and ch == CPB - 1)
                        tiles = [ds(n * TPC * D + j * D, D) for j in range(TPC)]
                        if more:
                            projected_stats(n + 1, 1 - ch, 2 * n + 2)
                        wait_alone(dve, chain, 3 + 2 * n + 2, tick)
                        row_stats(dve, [c.x[:, r] for r in tiles], sums[:, 1], stats[:, 1], summed, 2 * n + 2 + more, stats_ok, tick)
                        if more:
                            update(n + 1, 1 - ch, 2 * n + 2)
                        dve.wait_ge(rstd_ok, 2 * n + 2 + more)
                        for j, r in enumerate(tiles):
                            done = dve.tensor_scalar(c.norm[:, r], c.x[:, r],
                                                     stats[:, 1, j, 0:1], rstd[:, 1, j:j + 1], ALU.subtract, ALU.mult)
                        done.then_inc(norm_ok, 1)
                        magnitude(n)

                projected_stats(0, 0, 1)
                update(0, 0, 1)
                with dve.Fori(0, BATCH - 1) as b:
                    batch(b, False)
                batch(BATCH - 1, True)
                dve.wait_ge(amax_ok, BATCH * CPB)
                dve.tensor_reduce(out=rmax[:, 0:1], in_=amax[:, :], axis=AX_X, op=ALU.max).then_inc(max_ok, 1)
                dve.wait_ge(all_max, 1)
                dve.tensor_scalar(c.xscale[:, 0:1], rmax[:, 1:2], 1.0 / E4M3_MAX, 1e-12, ALU.mult, ALU.max).then_inc(max_ok, 1)
                dve.wait_ge(max_ok, 2)
                dve.reciprocal(c.xscale[:, 1:2], c.xscale[:, 0:1])


def to_e4m3(dve, v, bits, out, step_ok, count):
    dve.tensor_scalar(bits.bitcast(I32), v.bitcast(I32), 0x7F800000, None, ALU.bitwise_and).then_inc(step_ok, 1)
    dve.wait_ge(step_ok, count + 1)
    dve.tensor_scalar(bits, bits, 2.0 ** -6, 1.5 * 2.0 ** 20, ALU.max, ALU.mult).then_inc(step_ok, 1)
    dve.wait_ge(step_ok, count + 2)
    dve.tensor_tensor(v, v, bits, ALU.add).then_inc(step_ok, 1)
    dve.wait_ge(step_ok, count + 3)
    dve.tensor_tensor(out, v, bits, ALU.subtract).then_inc(step_ok, 1)
    dve.wait_ge(step_ok, count + 4)


def phase_fp8_and_ssm_inputs(c, a, m):
    nc = c.nc
    with ExitStack() as ctx:
        wf = sbuf(nc, ctx, "p4_wf", [P, KD * D], BF16)
        wbits = sbuf(nc, ctx, "p4_wbits", [P, KD * D])
        wv = sbuf(nc, ctx, "p4_wv", [P, KD * D])
        w8 = sbuf(nc, ctx, "p4_w8", [P, KD, D], BF16)
        wmax = sbuf(nc, ctx, "p4_wmax", [P, 4])
        wx = sbuf(nc, ctx, "p4_wx", [P, KD, 2 * N + SH])
        wg = sbuf(nc, ctx, "p4_wg", [P, KD, D])
        bg = sbuf(nc, ctx, "p4_bg", [P, 2, KD])
        v = sbuf(nc, ctx, "p4_v", [P, TPC * D])
        bits = sbuf(nc, ctx, "p4_bits", [P, TPC * D])
        q8 = sbuf(nc, ctx, "p4_q8", [P, TPC * D], BF16)
        qT = sbuf(nc, ctx, "p4_qT", [P, KD, CH], BF16)
        o16 = sbuf(nc, ctx, "p4_o16", [P, TPC * D], BF16)
        sums = sbuf(nc, ctx, "p4_sums", [P, 2, TPC, 6])
        stats = sbuf(nc, ctx, "p4_stats", [P, 2, TPC, 2])
        rstd = sbuf(nc, ctx, "p4_rstd", [P, 2, TPC])
        normed = sbuf(nc, ctx, "p4_normed", [P, TPC * D])
        mv16 = sbuf(nc, ctx, "p4_mv16", [P, TPC, 2], BF16)
        sd16 = sbuf(nc, ctx, "p4_sd16", [P, 2, TPC], BF16)
        shift = sbuf(nc, ctx, "p4_shift", [P, 2, TPC])
        half = sbuf(nc, ctx, "p4_half", [P, TPC])
        c16 = sbuf(nc, ctx, "p4_c16", [P, TPC * D], BF16)
        n16 = sbuf(nc, ctx, "p4_n16", [P, TPC * D], BF16)
        bres = sbuf(nc, ctx, "p4_bres", [P, CH])
        dres = sbuf(nc, ctx, "p4_dres", [SH, CH])
        gt = sbuf(nc, ctx, "p4_gt", [P, KD, CH])
        psQ = psum(nc, ctx, "p4_psQ", [P, KD, CH], BF16)
        psO = psum(nc, ctx, "p4_psO", [P, TPC * D])
        psT = psum(nc, ctx, "p4_psT", [P, KD, CH])
        psB = psum(nc, ctx, "p4_psB", [P, CH])
        psC = psum(nc, ctx, "p4_psC", [P, CH])
        psD = psum(nc, ctx, "p4_psD", [SH, CH])
        w_in, wstep, w8_ok, wmax_ok = (c.sem("p4_" + n) for n in ("w_in", "wstep", "w8_ok", "wmax_ok"))
        step_ok, q8_ok, q_turned, qT_ok, out_ok, o16_ok = (c.sem("p4_" + n) for n in ("step_ok", "q8_ok", "q_turned", "qT_ok", "out_ok", "o16_ok"))
        summed, stats_ok, rstd_ok, chain = (c.sem("p4_" + n) for n in ("summed", "stats_ok", "rstd_ok", "chain"))
        added = c.sem("p4_added")
        tick, tick_pool = c.sem("p4_tick"), c.sem("p4_tick_pool")
        mv16_ok, sd_ok, step16 = (c.sem("p4_" + n) for n in ("mv16_ok", "sd_ok", "step16"))
        turned, xT_ok, proj_ok, gate_ok, upper_ok, taken, split_ok = (c.sem("p4_" + n) for n in ("turned", "xT_ok", "proj_ok", "gate_ok", "upper_ok", "taken", "split_ok"))

        with nc.Block() as block:

            @block.sync
            def _(sp):
                sp.dma_start(wf[:, :].rearrange("p (k n) -> p k n", k=KD), a["wf"].rearrange("(k p) n -> p k n", p=P)).then_inc(w_in, 16)
                sp.dma_start(wx[:, :, :], a["wx"].rearrange("(k p) n -> p k n", p=P)).then_inc(w_in, 16)
                sp.dma_start(wg[:, :, :], a["wg"].rearrange("(k p) n -> p k n", p=P)).then_inc(w_in, 16)
                sp.dma_start(bg[:, 0, :], a["bg"]).then_inc(w_in, 16)
                sp.wait_ge(w_in, 64)

            @block.gpsimd
            def _(pool):
                pool.wait_ge(wmax_ok, 1)
                pool.partition_all_reduce(wmax[:, 1:2], wmax[:, 0:1], P, RMAX).then_inc(wmax_ok, 1)
                with pool.Fori(0, BATCH) as b:
                    for ch in range(CPB):
                        n = b * CPB + ch
                        wait_alone(pool, mv16_ok, n + 1, tick_pool)
                        pool.tensor_scalar(sd16[:, 0, :], mv16[:, :, 1], EPS, None, ALU.add).then_inc(sd_ok, 1)
                        pool.wait_ge(sd_ok, 2 * n + 1)
                        pool.tensor_tensor(sd16[:, 1, :], sd16[:, 0, :], half[:, :], ALU.pow).then_inc(sd_ok, 1)
                        rows_rstd(pool, stats_ok, 2 * n + 2, rstd[:, 1, :], stats[:, 1, :, 1], EPS, c.power, added, n + 1, rstd_ok, tick_pool)

            @block.tensor
            def _(pe):
                pe.sem_inc(turned, 1)
                pe.wait_ge(w8_ok, 1)

                def turn_quantised(n):
                    pe.wait_ge(q8_ok, n + 1)
                    for j in range(TPC):
                        for k in range(KD):
                            last = pe.transpose(psQ[:, k, j * P:(j + 1) * P], q8[:, j * D + k * P:j * D + (k + 1) * P], c.identb[:, :])
                    last.then_inc(q_turned, 1)

                def linear(n, first):
                    pe.wait_ge(qT_ok, n + 1)
                    if not first:
                        pe.wait_ge(o16_ok, n)
                    for j in range(TPC):
                        for k in range(KD):
                            last = pe.matmul(psO[:, j * D:(j + 1) * D], qT[:, k, j * P:(j + 1) * P], w8[:, k, :], start=k == 0, stop=k == KD - 1)
                    last.then_inc(out_ok, 1)

                def turn(n):
                    pe.wait_ge(gate_ok, n + 1)
                    pe.wait_ge(chain, 2 * n + 2)
                    for j in range(TPC):
                        for k in range(KD):
                            last = pe.transpose(psT[:, k, j * P:(j + 1) * P], normed[:, j * D + k * P:j * D + (k + 1) * P], c.ident[:, :])
                    last.then_inc(turned, 1)

                def projections(n):
                    pe.wait_ge(xT_ok, n + 1)
                    xT = [m["xT"][:, ds(n * KD * CH + k * CH, CH)] for k in range(KD)]
                    pe.wait_ge(taken, n + 1)
                    for ps, lo, hi in ((psB, 0, N), (psC, N, 2 * N), (psD, 2 * N, 2 * N + SH)):
                        for k in range(KD):
                            last = pe.matmul(ps[:, :], wx[:, k, lo:hi], xT[k], start=k == 0, stop=k == KD - 1)
                    last.then_inc(proj_ok, 1)
                    for f in range(KD):
                        for k in range(KD):
                            last = pe.matmul(psT[:, f, :], wg[:, k, f * P:(f + 1) * P], xT[k], start=k == 0, stop=k == KD - 1)
                    last.then_inc(proj_ok, 1)

                def batch(b, last):
                    for ch in range(CPB):
                        n = b * CPB + ch
                        turn(n)
                        if not last:
                            turn_quantised(n + 2)
                        projections(n)
                        if not last:
                            linear(n + 2, False)

                for n in range(2):
                    turn_quantised(n)
                    linear(n, n == 0)
                with pe.Fori(0, BATCH - 1) as b:
                    batch(b, False)
                batch(BATCH - 1, True)

            @block.scalar
            def _(act):
                act.preload_act_table_set("exp_and_others")
                act.wait_ge(w8_ok, 1)
                act.sem_inc(gate_ok, 1)

                def keep_quantised(n):
                    act.wait_ge(q_turned, n + 1)
                    act.activation(qT[:, :, :], psQ[:, :, :], ACT.Copy).then_inc(qT_ok, 1)

                def scale_rows(n, first):
                    act.wait_ge(out_ok, n + 1)
                    if not first:
                        act.wait_ge(step16, 3 * n - 1)
                    act.activation(o16[:, :], psO[:, :], ACT.Copy, scale=wmax[:, 3:4]).then_inc(o16_ok, 1)

                def batch(b, last):
                    for ch in range(CPB):
                        n = b * CPB + ch
                        act.wait_ge(turned, n + 2)
                        act.activation(m["xT"][:, ds(n * KD * CH, KD * CH)], psT[:, :, :].rearrange("p k t -> p (k t)"), ACT.Copy).then_inc(xT_ok, 1)
                        if not last:
                            keep_quantised(n + 2)
                        act.wait_ge(proj_ok, 2 * n + 1)
                        act.activation(m["Bp"][0][:, ds(n * CH, CH)], psB[:, :], ACT.Copy)
                        act.activation(m["dp"][0:SH, ds(n * CH, CH)], psD[:, :], ACT.Copy).then_inc(upper_ok, 1)
                        act.activation(m["CT"][:, ds(n * CH, CH)], psC[:, :], ACT.Copy)
                        act.wait_ge(proj_ok, 2 * n + 2)
                        for f in range(KD):
                            gated = act.activation(gt[:, f, :], psT[:, f, :], ACT.Tanh, scale=0.5, bias=bg[:, 1, f:f + 1])
                        gated.then_inc(gate_ok, 1)
                        if not last:
                            scale_rows(n + 2, False)

                for n in range(2):
                    keep_quantised(n)
                    scale_rows(n, n == 0)
                with act.Fori(0, BATCH - 1) as b:
                    batch(b, False)
                batch(BATCH - 1, True)

            @block.vector
            def _(dve):
                dve.wait_ge(w_in, 64)
                dve.memset(half[:, :], 0.5)
                dve.tensor_scalar(bg[:, 1, :], bg[:, 0, :], 0.5, None, ALU.mult)
                dve.tensor_reduce(out=wmax[:, 0:1], in_=wf[:, :], axis=AX_X, op=ALU.max, apply_absolute_value=True).then_inc(wmax_ok, 1)
                dve.wait_ge(wmax_ok, 2)
                dve.tensor_scalar(wmax[:, 2:3], wmax[:, 1:2], 1.0 / E4M3_MAX, 1e-12, ALU.mult, ALU.max).then_inc(wstep, 1)
                dve.wait_ge(wstep, 1)
                dve.tensor_tensor(wmax[:, 3:4], c.xscale[:, 0:1], wmax[:, 2:3], ALU.mult)
                dve.reciprocal(wmax[:, 0:1], wmax[:, 2:3]).then_inc(wstep, 1)
                dve.wait_ge(wstep, 2)
                dve.tensor_scalar(wv[:, :], wf[:, :], wmax[:, 0:1], None, ALU.mult).then_inc(wstep, 1)
                dve.wait_ge(wstep, 3)
                to_e4m3(dve, wv[:, :], wbits[:, :], w8[:, :, :].rearrange("p k n -> p (k n)"), wstep, 3)
                dve.sem_inc(w8_ok, 1)
                dve.sem_inc(taken, 1)

                def quantise(n, first):
                    dve.tensor_scalar(v[:, :], c.norm[:, ds(n * TPC * D, TPC * D)], c.xscale[:, 1:2], None, ALU.mult).then_inc(step_ok, 1)
                    dve.wait_ge(step_ok, 5 * n + 1)
                    if not first:
                        wait_alone(dve, q_turned, n, tick)
                    to_e4m3(dve, v[:, :], bits[:, :], q8[:, :], step_ok, 5 * n + 1)
                    dve.sem_inc(q8_ok, 1)

                def update(n):
                    rows = c.x[:, ds(n * TPC * D, TPC * D)]
                    dve.wait_ge(o16_ok, n + 1)
                    row_stats(dve, [o16[:, j * D:(j + 1) * D] for j in range(TPC)], sums[:, 0], stats[:, 0], summed, 2 * n + 1, stats_ok, tick)
                    dve.wait_ge(stats_ok, 2 * n + 1)
                    dve.tensor_copy(mv16[:, :, :], stats[:, 0]).then_inc(mv16_ok, 1)
                    dve.wait_ge(mv16_ok, n + 1)
                    dve.tensor_copy(shift[:, 0, :], mv16[:, :, 0])
                    dve.wait_ge(sd_ok, 2 * n + 2)
                    dve.reciprocal(shift[:, 1, :], sd16[:, 1, :]).then_inc(step16, 1)
                    dve.wait_ge(step16, 3 * n + 1)
                    for j in range(TPC):
                        last = dve.tensor_scalar(c16[:, j * D:(j + 1) * D], o16[:, j * D:(j + 1) * D], shift[:, 0, j:j + 1], None, ALU.subtract)
                    last.then_inc(step16, 1)
                    dve.wait_ge(step16, 3 * n + 2)
                    for j in range(TPC):
                        last = dve.tensor_scalar(n16[:, j * D:(j + 1) * D], c16[:, j * D:(j + 1) * D], shift[:, 1, j:j + 1], None, ALU.mult)
                    last.then_inc(step16, 1)
                    dve.wait_ge(step16, 3 * n + 3)
                    dve.tensor_tensor(rows, rows, n16[:, :], ALU.add).then_inc(chain, 1)

                def normalise(n, meanwhile):
                    tiles = [c.x[:, ds(n * TPC * D + j * D, D)] for j in range(TPC)]
                    wait_alone(dve, chain, 2 * n + 1, tick)
                    row_stats(dve, tiles, sums[:, 1], stats[:, 1], summed, 2 * n + 2, stats_ok, tick)
                    meanwhile()
                    dve.wait_ge(rstd_ok, n + 1)
                    dve.wait_ge(turned, n + 1)
                    for j in range(TPC):
                        last = dve.tensor_scalar(normed[:, j * D:(j + 1) * D], tiles[j],
                                                 stats[:, 1, j, 0:1], rstd[:, 1, j:j + 1], ALU.subtract, ALU.mult)
                    last.then_inc(chain, 1)

                def split(n):
                    dve.wait_ge(upper_ok, n + 1)
                    cols = ds(n * CH, CH)
                    dve.tensor_tensor(bres[:, :], psB[:, :], m["Bp"][0][:, cols], ALU.subtract)
                    dve.tensor_tensor(dres[:, :], psD[:, :], m["dp"][0:SH, cols], ALU.subtract).then_inc(split_ok, 1)
                    dve.wait_ge(split_ok, 2 * n + 1)
                    dve.tensor_copy(m["Bp"][1][:, cols], bres[:, :])
                    dve.tensor_copy(m["dp"][SH:2 * SH, cols], dres[:, :])
                    dve.tensor_copy(m["dm"][:, :], dres[:, :]).then_inc(split_ok, 1)
                    dve.wait_ge(split_ok, 2 * n + 2)
                    dve.tensor_tensor(m["Bp"][2][:, cols], bres[:, :], m["Bp"][1][:, cols], ALU.subtract)
                    dve.tensor_tensor(m["dp"][2 * SH:3 * SH, cols], dres[:, :], m["dm"][:, :], ALU.subtract)

                def gates(n):
                    dve.wait_ge(gate_ok, n + 2)
                    dve.tensor_scalar(c.norm[:, ds(n * KD * CH, KD * CH)], gt[:, :, :].rearrange("p k t -> p (k t)"), 0.5, 0.5, ALU.mult, ALU.add).then_inc(taken, 1)

                def batch(b, last):
                    for ch in range(CPB):
                        n = b * CPB + ch
                        more = not (last and ch == CPB - 1)
                        if not last:
                            quantise(n + 2, False)
                        if more:
                            update(n + 1)
                            normalise(n + 1, lambda: split(n))
                        else:
                            split(n)
                        gates(n)

                for n in range(2):
                    quantise(n, n == 0)
                update(0)
                normalise(0, lambda: None)
                with dve.Fori(0, BATCH - 1) as b:
                    batch(b, False)
                batch(BATCH - 1, True)


def ring(*turns):
    slots = [s for n in turns for s in range(n)]
    assert len(slots) == SH
    return slots, [next(k for k in range(1, SH + 1) if k == max(turns) or slots[q - k] == slots[q]) for q in range(SH)]


def phase_ssm(c, a, m):
    nc = c.nc
    FREE = 5
    Z, Z_BACK = ring(*[3] * 10, 2)
    U, U_BACK = ring(*[5] * 4, *[4] * 3)
    RQ = 2
    SHARE = 4

    def head_of(q):
        return (q // 16) * 16 + 4 * (q % 4) + (q // 4) % 4

    def ahead(b, q, k, last):
        if q + k < SH:
            return b * SH + q + k, b, q + k
        return None if last else (b * SH + q + k, b + 1, q + k - SH)

    with ExitStack() as ctx:
        AT = sbuf(nc, ctx, "p5_AT", [P, SH])
        skip = sbuf(nc, ctx, "p5_skip", [P, KD])
        pick = sbuf(nc, ctx, "p5_pick", [3 * SH, 2, SH])
        sel = sbuf(nc, ctx, "p5_sel", [3 * SH, SH], BF16)
        ones = sbuf(nc, ctx, "p5_ones", [P, 4, 4 * SHD])
        u = [sbuf(nc, ctx, f"p5_u{i}", [P, S]) for i in range(5)]
        st = [sbuf(nc, ctx, f"p5_st{i}", [P, S]) for i in range(5)]
        sq = [sbuf(nc, ctx, f"p5_sq{i}", [P, S]) for i in range(RQ)]
        psZ = [psum(nc, ctx, f"p5_psZ{i}", [P, CPB, CH]) for i in range(3)]
        psY = psum(nc, ctx, "p5_psY", [P, CPB, CH])
        w_in, const_ok, tick = c.sem("p5_w_in"), c.sem("p5_const_ok"), c.sem("p5_tick")
        z_ok, exp_ok, ln_ok, d_ok, sq_ok, a_ok = (c.sem("p5_" + n) for n in ("z_ok", "exp_ok", "ln_ok", "d_ok", "sq_ok", "a_ok"))
        scan_ok, prod_ok, pool_prod_ok, read_ok, y_taken, skip_ok = (c.sem("p5_" + n) for n in ("scan_ok", "prod_ok", "pool_prod_ok", "read_ok", "y_taken", "skip_ok"))

        with nc.Block() as block:

            @block.sync
            def _(sp):
                sp.dma_start(AT[:, :], a["ssmA"]).then_inc(w_in, 16)
                sp.dma_start(skip[:, :], a["skip"]).then_inc(w_in, 16)
                sp.wait_ge(w_in, 32)

            @block.tensor
            def _(pe):
                pe.sem_inc(read_ok, FREE)
                pe.wait_ge(const_ok, 3)

                def logits(i, b, q):
                    pe.wait_ge(d_ok, FREE + i - Z_BACK[q] + 1)
                    pick_head = sel[:, head_of(q):head_of(q) + 1].broadcast_to([3 * SH, P])
                    for ch in range(CPB):
                        cols = ds(b * S + ch * CH, CH)
                        for e in range(3):
                            pe.matmul(psZ[Z[q]][:, ch, :], c.identb[:, :], m["Bp"][e][:, cols], start=e == 0, stop=False)
                        last = pe.matmul(psZ[Z[q]][:, ch, :], pick_head, m["dp"][:, cols], start=False, stop=True)
                    last.then_inc(z_ok, 1)

                def read(b, q):
                    r = (q // 4) % 4
                    if q % 16 == 1:
                        pe.wait_ge(y_taken, 2 * b + q // 16 + 1)
                    pe.wait_ge(prod_ok, b * (SH - SH // SHARE) + q + 1 - (q + 1) // SHARE)
                    if (q + 1) % SHARE == 0:
                        pe.wait_ge(pool_prod_ok, b * (SH // SHARE) + (q + 1) // SHARE)
                    for ch in range(CPB):
                        for p in (q - 1, q):
                            j = p % 4
                            last = pe.matmul(psY[32 * j:32 * j + 32, ch, :], ones[:, r, :], st[U[p]][:, ch * CH:(ch + 1) * CH],
                                             start=r == 0, stop=r == 3)
                    last.then_inc(read_ok, 2)

                def batch(b, last_batch):
                    for q in range(SH):
                        nxt = ahead(b, q, 4, last_batch)
                        if nxt:
                            logits(*nxt)
                        if q % 2 == 0 and q:
                            read(b, q - 1)
                    read(b, SH - 1)

                for q in range(4):
                    logits(q, 0, q)
                with pe.Fori(0, BATCH - 1) as b:
                    batch(b, False)
                batch(BATCH - 1, True)

            @block.scalar
            def _(act):
                act.preload_act_table_set("natural_log_exp_and_others")
                act.wait_ge(w_in, 32)

                def exps(i, b, q):
                    act.wait_ge(sq_ok, FREE + i - U_BACK[q] + 1)
                    act.wait_ge(z_ok, i + 1)
                    act.activation(u[U[q]][:, :], psZ[Z[q]][:, :, :].rearrange("p c t -> p (c t)"), ACT.Exp).then_inc(exp_ok, 1)

                def logs(i, b, q):
                    act.wait_ge(exp_ok, i + 1)
                    act.activation(u[U[q]][:, :], u[U[q]][:, :], ACT.Ln, bias=1.0).then_inc(ln_ok, 1)

                def decays(i, b, q):
                    act.wait_ge(d_ok, FREE + i + 1)
                    act.wait_ge(read_ok, FREE + i - U_BACK[q] + 1)
                    act.activation(st[U[q]][:, :], u[U[q]][:, :], ACT.Exp, scale=AT[:, head_of(q):head_of(q) + 1]).then_inc(a_ok, 1)

                def batch(b, last):
                    for q in range(SH):
                        for step, k in ((decays, 1), (logs, 3), (exps, 4)):
                            nxt = ahead(b, q, k, last)
                            if nxt:
                                step(*nxt)

                for q in range(3):
                    exps(q, 0, q)
                    logs(q, 0, q)
                exps(3, 0, 3)
                decays(0, 0, 0)
                with act.Fori(0, BATCH - 1) as b:
                    batch(b, False)
                batch(BATCH - 1, True)

            @block.gpsimd
            def _(pool):
                pool.sem_inc(sq_ok, FREE)

                def product(b, q):
                    wait_alone(pool, scan_ok, RQ + b * SH + q + 1, tick)
                    pool.tensor_tensor(st[U[q]][:, :], st[U[q]][:, :], m["CT"][:, ds(b * S, S)], ALU.mult).then_inc(pool_prod_ok, 1)

                with pool.Fori(0, BATCH) as b:
                    for q in range(SH):
                        i = b * SH + q
                        pool.wait_ge(d_ok, FREE + i + 1)
                        pool.wait_ge(scan_ok, i + 1)
                        pool.tensor_tensor(sq[q % RQ][:, :], u[U[q]][:, :], u[U[q]][:, :], ALU.mult).then_inc(sq_ok, 1)
                        if q % SHARE == 0 and q > 0:
                            product(b, q - 1)
                    product(b, SH - 1)

            @block.vector
            def _(dve):
                dve.memset(ones[:, :, :], 0.0).then_inc(const_ok, 1)
                dve.wait_ge(const_ok, 1)
                for r in range(4):
                    dve.memset(ones[:, r, r * SHD:(r + 1) * SHD], 1.0)
                dve.tensor_tensor(pick[:, 0, :], c.ident[0:3 * SH, 0:SH], c.ident[0:3 * SH, SH:2 * SH], ALU.add).then_inc(const_ok, 1)
                dve.wait_ge(const_ok, 2)
                dve.tensor_tensor(pick[:, 1, :], pick[:, 0, :], c.ident[0:3 * SH, 2 * SH:3 * SH], ALU.add).then_inc(skip_ok, 1)
                dve.wait_ge(skip_ok, 1)
                dve.tensor_copy(sel[:, :], pick[:, 1, :]).then_inc(const_ok, 1)
                dve.sem_inc(d_ok, FREE)
                dve.sem_inc(scan_ok, RQ)
                dve.sem_inc(y_taken, 1)
                dve.wait_ge(w_in, 32)

                def step_sizes(i, b, q):
                    dve.wait_ge(ln_ok, i + 1)
                    dve.scalar_tensor_tensor(out=u[U[q]][:, :], in0=u[U[q]][:, :], scalar=SAT,
                                             in1=psZ[Z[q]][:, :, :].rearrange("p c t -> p (c t)"), op0=ALU.min, op1=ALU.max).then_inc(d_ok, 1)

                def skip_and_gate(b, f):
                    dve.wait_ge(read_ok, FREE + b * SH + (f + 1) * 16)
                    for ch in range(CPB):
                        cols = ds((b * CPB + ch) * KD * CH + f * CH, CH)
                        last = dve.scalar_tensor_tensor(out=m["xT"][:, cols], in0=m["xT"][:, cols], scalar=skip[:, f:f + 1],
                                                        in1=psY[:, ch, :], op0=ALU.mult, op1=ALU.add)
                    last.then_inc(y_taken, 1)
                    dve.wait_ge(y_taken, 1 + 2 * b + f + 1)
                    for ch in range(CPB):
                        cols = ds((b * CPB + ch) * KD * CH + f * CH, CH)
                        dve.tensor_tensor(c.norm[:, cols], m["xT"][:, cols], c.norm[:, cols], ALU.mult)

                def batch(b, last):
                    for q in range(SH):
                        i = b * SH + q
                        dve.wait_ge(a_ok, i + 1)
                        dve.wait_ge(sq_ok, FREE + i + 1)
                        dve.tensor_tensor_scan(st[U[q]][:, :], st[U[q]][:, :], sq[q % RQ][:, :], 0.0, ALU.mult, ALU.add).then_inc(scan_ok, 1)
                        nxt = ahead(b, q, 2, last)
                        if nxt:
                            step_sizes(*nxt)
                        if q == 17:
                            skip_and_gate(b, 0)
                        if (q + 1) % SHARE:
                            dve.wait_ge(scan_ok, RQ + i + 1)
                            dve.tensor_tensor(st[U[q]][:, :], st[U[q]][:, :], m["CT"][:, ds(b * S, S)], ALU.mult).then_inc(prod_ok, 1)
                    skip_and_gate(b, 1)

                step_sizes(0, 0, 0)
                step_sizes(1, 0, 1)
                with dve.Fori(0, BATCH - 1) as b:
                    batch(b, False)
                batch(BATCH - 1, True)


def phase_qkv_second(c, a, d):
    nc = c.nc
    with ExitStack() as ctx:
        wo = sbuf(nc, ctx, "p6_wo", [P, KD, D])
        wqk = [sbuf(nc, ctx, f"p6_wqk{i}", [P, KD, D]) for i in range(2)]
        wv = sbuf(nc, ctx, "p6_wv", [P, KD, D])
        ln = sbuf(nc, ctx, "p6_ln", [P, 2, KD])
        ys = sbuf(nc, ctx, "p6_ys", [P, 2, KD, CH])
        sums = sbuf(nc, ctx, "p6_sums", [P, 3, TPC, 6])
        stats = sbuf(nc, ctx, "p6_stats", [P, 3, TPC, 2])
        rstd = sbuf(nc, ctx, "p6_rstd", [P, 3, TPC])
        msq = sbuf(nc, ctx, "p6_msq", [P, 2, TPC])
        normed = sbuf(nc, ctx, "p6_normed", [P, TPC * D])
        base = sbuf(nc, ctx, "p6_base", [P, TPC * D])
        aT = sbuf(nc, ctx, "p6_aT", [P, KD, CH])
        hT = sbuf(nc, ctx, "p6_hT", [P, KD, CH])
        rest = sbuf(nc, ctx, "p6_rest", [P, 2, CH])
        parts = [sbuf(nc, ctx, f"p6_parts{i}", [P, 3, 2, CH], BF16) for i in range(2)]
        vx = sbuf(nc, ctx, "p6_vx", [P, TPC, G * HG, HD + 1])
        psO = psum(nc, ctx, "p6_psO", [P, TPC * D])
        psT = psum(nc, ctx, "p6_psT", [P, KD, CH])
        psP = psum(nc, ctx, "p6_psP", [P, 2, CH])
        psV = psum(nc, ctx, "p6_psV", [P, TPC, D])
        w_in, ones_ok, ys_ok, out_ok = (c.sem("p6_" + n) for n in ("w_in", "ones_ok", "ys_ok", "out_ok"))
        summed, stats_ok, ms_ok, rstd_ok, chain = (c.sem("p6_" + n) for n in ("summed", "stats_ok", "ms_ok", "rstd_ok", "chain"))
        added = c.sem("p6_added")
        tick, tick_pool = c.sem("p6_tick"), c.sem("p6_tick_pool")
        turned, aT_ok, hT_ok, v_ok, proj_ok = (c.sem("p6_" + n) for n in ("turned", "aT_ok", "hT_ok", "v_ok", "proj_ok"))
        upper_ok, rest_ok, mid_ok, low_ok, vx_ok, stored = (c.sem("p6_" + n) for n in ("upper_ok", "rest_ok", "mid_ok", "low_ok", "vx_ok", "stored"))
        STORES = 16 * (1 + 4 + 4 + 4)

        with nc.Block() as block:

            @block.sync
            def _(sp):
                for w, src in ((wo, a["wo3"]), (wqk[0], a["wq2"]), (wqk[1], a["wk2"]), (wv, a["wv2"])):
                    sp.dma_start(w[:, :, :], src.rearrange("(k p) n -> p k n", p=P)).then_inc(w_in, 16)
                sp.dma_start(ln[:, 0, :], a["ln1"]).then_inc(w_in, 16)
                sp.dma_start(ln[:, 1, :], a["ln2"]).then_inc(w_in, 16)
                sp.sem_inc(stored, STORES)
                with sp.Fori(0, BATCH) as b:
                    for ch in range(CPB):
                        n = b * CPB + ch
                        sp.wait_ge(hT_ok, n + 1)
                        sp.dma_start(d["h"][ds(n, 1)].rearrange("n p e -> (n p) e"), hT[:, :, :].rearrange("p k t -> p (k t)")).then_inc(stored, 16)
                        sp.wait_ge(vx_ok, n + 1)
                        bg = ds(b * G, G)
                        for g in range(G):
                            sp.dma_start(d["v2"][bg][g, :, ch * TPC:(ch + 1) * TPC, :, :].rearrange("p j h e -> p j (h e)"),
                                         vx[:, :, g * HG:(g + 1) * HG, :].rearrange("p j h e -> p j (h e)")).then_inc(stored, 16)
                        for i in range(2):
                            sp.wait_ge(low_ok, 2 * n + i + 2)
                            for g in range(G):
                                rows = slice(64 * (g % 2), 64 * (g % 2) + 64)
                                sp.dma_start(d["qk2"][i][bg][g, :, :, ch * CH:(ch + 1) * CH].rearrange("e r t -> r e t"),
                                             parts[i][rows, :, g // 2, :]).then_inc(stored, 16)
                sp.wait_ge(stored, STORES * (BATCH * CPB + 1))

            @block.gpsimd
            def _(pool):
                pool.sem_inc(low_ok, 1)

                def copy(n, ch):
                    pool.wait_ge(out_ok, n + 1)
                    pool.tensor_copy(ys[:, ch, :, :].rearrange("p k t -> p (k t)"), c.norm[:, ds(n * KD * CH, KD * CH)]).then_inc(ys_ok, 1)

                def rstd_of(n, k):
                    if k < 2:
                        rows_rstd(pool, stats_ok, 3 * n + k + 1, rstd[:, k, :], stats[:, k, :, 1], EPS, c.power, added, 3 * n + k + 1, rstd_ok, tick_pool)
                    else:
                        rows_rstd(pool, ms_ok, 2 * n + 2, rstd[:, 2, :], msq[:, 1, :], RMS_EPS, c.power, added, 3 * n + 3, rstd_ok, tick_pool)

                def lower(n, i):
                    pool.wait_ge(mid_ok, 2 * n + i + 1)
                    pool.tensor_tensor(parts[i][:, 2, :, :], rest[:, :, :], parts[i][:, 1, :, :], ALU.subtract).then_inc(low_ok, 1)

                def batch(b, last):
                    for ch in range(CPB):
                        n = b * CPB + ch
                        more = not (last and ch == CPB - 1)
                        for k in range(3):
                            if more:
                                rstd_of(n + 1, k)
                            if k > 0:
                                lower(n, k - 1)
                        if not last:
                            copy(n + 2, ch)

                copy(0, 0)
                copy(1, 1)
                for k in range(3):
                    rstd_of(0, k)
                with pool.Fori(0, BATCH - 1) as b:
                    batch(b, False)
                batch(BATCH - 1, True)

            @block.tensor
            def _(pe):
                pe.sem_inc(out_ok, 2)
                pe.sem_inc(turned, 1)
                pe.wait_ge(w_in, 96)

                def out_projection(n, ch):
                    for j in range(TPC):
                        for k in range(KD):
                            last = pe.matmul(psO[:, j * D:(j + 1) * D], ys[:, ch, k, j * P:(j + 1) * P], wo[:, k, :], start=k == 0, stop=k == KD - 1)
                    last.then_inc(out_ok, 1)

                def projections(n):
                    pe.wait_ge(chain, 1 + 4 * n + 4)
                    for j in range(TPC):
                        for k in range(KD):
                            last = pe.transpose(psT[:, k, j * P:(j + 1) * P], base[:, j * D + k * P:j * D + (k + 1) * P], c.ident[:, :])
                    last.then_inc(turned, 1)
                    pe.wait_ge(aT_ok, n + 1)
                    for i in range(2):
                        pe.wait_ge(rest_ok, 2 * n + i + 1)
                        for f in range(2):
                            for k in range(KD):
                                last = pe.matmul(psP[:, f, :], wqk[i][:, k, f * P:(f + 1) * P], aT[:, k, :], start=k == 0, stop=k == KD - 1)
                        last.then_inc(proj_ok, 1)
                        if i == 0:
                            for j in range(TPC):
                                for k in range(KD):
                                    last = pe.matmul(psV[:, j, :], aT[:, k, j * P:(j + 1) * P], wv[:, k, :], start=k == 0, stop=k == KD - 1)
                            last.then_inc(v_ok, 1)

                def batch(b, last):
                    for ch in range(CPB):
                        n = b * CPB + ch
                        if not (last and ch == CPB - 1):
                            pe.wait_ge(ys_ok, n + 2)
                            pe.wait_ge(chain, 1 + 4 * n + 1)
                            out_projection(n + 1, 1 - ch)
                        projections(n)

                pe.wait_ge(ys_ok, 1)
                out_projection(0, 0)
                with pe.Fori(0, BATCH - 1) as b:
                    batch(b, False)
                batch(BATCH - 1, True)

            @block.scalar
            def _(act):
                act.wait_ge(w_in, 96)
                act.wait_ge(ones_ok, 1)
                with act.Fori(0, BATCH) as b:
                    for ch in range(CPB):
                        n = b * CPB + ch
                        act.wait_ge(turned, n + 2)
                        for k in range(KD):
                            last = act.activation(aT[:, k, :], psT[:, k, :], ACT.Copy, scale=ln[:, 0, k:k + 1])
                        last.then_inc(aT_ok, 1)
                        act.wait_ge(stored, STORES * (n + 1))
                        for k in range(KD):
                            last = act.activation(hT[:, k, :], psT[:, k, :], ACT.Copy, scale=ln[:, 1, k:k + 1])
                        last.then_inc(hT_ok, 1)
                        for i in range(2):
                            act.wait_ge(proj_ok, 2 * n + i + 1)
                            act.activation(parts[i][:, 0, :, :], psP[:, :, :], ACT.Copy).then_inc(upper_ok, 1)
                            if i == 0:
                                act.wait_ge(v_ok, n + 1)
                                act.activation(vx[:, :, :, 0:HD], psV[:, :, :].rearrange("p j (h e) -> p j h e", e=HD), ACT.Copy).then_inc(vx_ok, 1)
                            act.wait_ge(rest_ok, 1 + 2 * n + i + 1)
                            act.activation(parts[i][:, 1, :, :], rest[:, :, :], ACT.Copy).then_inc(mid_ok, 1)

            @block.vector
            def _(dve):
                dve.memset(vx[:, :, :, :], 1.0).then_inc(ones_ok, 1)
                dve.sem_inc(chain, 1)
                dve.sem_inc(rest_ok, 1)

                def rows_of(n):
                    return [ds(n * TPC * D + j * D, D) for j in range(TPC)]

                def update(n):
                    dve.wait_ge(out_ok, n + 3)
                    row_stats(dve, [psO[:, j * D:(j + 1) * D] for j in range(TPC)], sums[:, 0], stats[:, 0], summed, 3 * n + 1, stats_ok, tick)
                    dve.wait_ge(rstd_ok, 3 * n + 1)
                    for j in range(TPC):
                        last = dve.tensor_scalar(normed[:, j * D:(j + 1) * D], psO[:, j * D:(j + 1) * D],
                                                 stats[:, 0, j, 0:1], rstd[:, 0, j:j + 1], ALU.subtract, ALU.mult)
                    last.then_inc(chain, 1)
                    rows = c.x[:, ds(n * TPC * D, TPC * D)]
                    dve.wait_ge(chain, 1 + 4 * n + 1)
                    dve.tensor_tensor(rows, rows, normed[:, :], ALU.add).then_inc(chain, 1)

                def normalise(n, meanwhile):
                    wait_alone(dve, chain, 1 + 4 * n + 2, tick)
                    row_stats(dve, [c.x[:, r] for r in rows_of(n)], sums[:, 1], stats[:, 1], summed, 3 * n + 2, stats_ok, tick)
                    meanwhile()
                    dve.wait_ge(rstd_ok, 3 * n + 2)
                    dve.wait_ge(ys_ok, n + 1)
                    for j, r in enumerate(rows_of(n)):
                        last = dve.tensor_scalar(c.norm[:, r], c.x[:, r], stats[:, 1, j, 0:1], rstd[:, 1, j:j + 1], ALU.subtract, ALU.mult)
                    last.then_inc(chain, 1)

                def rms_normalise(n, meanwhile):
                    wait_alone(dve, chain, 1 + 4 * n + 3, tick)
                    row_stats(dve, [c.norm[:, r] for r in rows_of(n)], sums[:, 2], stats[:, 2], summed, 3 * n + 3, stats_ok, tick)
                    dve.wait_ge(stats_ok, 3 * n + 3)
                    dve.tensor_tensor(msq[:, 0, :], stats[:, 2, :, 0], stats[:, 2, :, 0], ALU.mult).then_inc(ms_ok, 1)
                    dve.wait_ge(ms_ok, 2 * n + 1)
                    dve.tensor_tensor(msq[:, 1, :], msq[:, 0, :], stats[:, 2, :, 1], ALU.add).then_inc(ms_ok, 1)
                    meanwhile()
                    dve.wait_ge(rstd_ok, 3 * n + 3)
                    dve.wait_ge(turned, n + 1)
                    for j, r in enumerate(rows_of(n)):
                        last = dve.tensor_scalar(base[:, j * D:(j + 1) * D], c.norm[:, r], rstd[:, 2, j:j + 1], None, ALU.mult)
                    last.then_inc(chain, 1)

                def leftover(n, i):
                    dve.wait_ge(upper_ok, 2 * n + i + 1)
                    dve.wait_ge(low_ok, 2 * n + i + 1)
                    dve.tensor_tensor(rest[:, :, :], psP[:, :, :], parts[i][:, 0, :, :], ALU.subtract).then_inc(rest_ok, 1)

                def batch(b, last):
                    for ch in range(CPB):
                        n = b * CPB + ch
                        more = not (last and ch == CPB - 1)
                        if more:
                            update(n + 1)
                            normalise(n + 1, lambda: leftover(n, 0))
                            rms_normalise(n + 1, lambda: leftover(n, 1))
                        else:
                            leftover(n, 0)
                            leftover(n, 1)

                update(0)
                normalise(0, lambda: None)
                rms_normalise(0, lambda: None)
                with dve.Fori(0, BATCH - 1) as b:
                    batch(b, False)
                batch(BATCH - 1, True)


def phase_mlp(c, a, d, out):
    nc = c.nc
    with ExitStack() as ctx:
        wo = sbuf(nc, ctx, "p8_wo", [P, KD, D])
        wa = sbuf(nc, ctx, "p8_wa", [P, KD, R])
        wb = sbuf(nc, ctx, "p8_wb", [R, F])
        wgu = [sbuf(nc, ctx, f"p8_wgu{i}", [P, KD, F]) for i in range(2)]
        wd = sbuf(nc, ctx, "p8_wd", [P, FT, D])
        at = sbuf(nc, ctx, "p8_at", [P, CPB, TPC * D])
        hT = sbuf(nc, ctx, "p8_hT", [P, CPB, KD, CH])
        aT = sbuf(nc, ctx, "p8_aT", [P, KD, CH])
        oT = sbuf(nc, ctx, "p8_oT", [P, KD, CH])
        mod = sbuf(nc, ctx, "p8_mod", [R, CH])
        g = sbuf(nc, ctx, "p8_g", [R, CH])
        gate = sbuf(nc, ctx, "p8_gate", [P, 2, CH])
        mT = sbuf(nc, ctx, "p8_mT", [P, FT, CH])
        sums = sbuf(nc, ctx, "p8_sums", [P, TPC, 6])
        stats = sbuf(nc, ctx, "p8_stats", [P, TPC, 2])
        rstd = sbuf(nc, ctx, "p8_rstd", [P, TPC])
        y = sbuf(nc, ctx, "p8_y", [P, TPC * D])
        normed = sbuf(nc, ctx, "p8_normed", [P, TPC * D])
        psX = [psum(nc, ctx, f"p8_psX{i}", [P, 2, CH]) for i in range(2)]
        psM = [psum(nc, ctx, f"p8_psM{i}", [P, CH]) for i in range(2)]
        psD = psum(nc, ctx, "p8_psD", [P, TPC * D])
        w_in, h_in, h_used = c.sem("p8_w_in"), [c.sem(f"p8_h_in{i}") for i in range(CPB)], c.sem("p8_h_used")
        at_ok, turned, aT_ok, oproj_ok, oT_ok, low_ok, mod_ok, g_ok = (c.sem("p8_" + n) for n in ("at_ok", "turned", "aT_ok", "oproj_ok", "oT_ok", "low_ok", "mod_ok", "g_ok"))
        gu_ok, silu_ok, m_ok, down_ok = (c.sem("p8_" + n) for n in ("gu_ok", "silu_ok", "m_ok", "down_ok"))
        summed, stats_ok, rstd_ok, chain, stored = (c.sem("p8_" + n) for n in ("summed", "stats_ok", "rstd_ok", "chain", "stored"))
        added, gu_in, wd_in = c.sem("p8_added"), c.sem("p8_gu_in"), c.sem("p8_wd_in")
        tick, tick_pool = c.sem("p8_tick"), c.sem("p8_tick_pool")

        with nc.Block() as block:

            @block.sync
            def _(sp):
                for w, src, landed in ((wo, a["wo4"], w_in), (wa, a["loraA"], w_in), (wgu[0], a["win"], gu_in), (wgu[1], a["wup"], gu_in)):
                    sp.dma_start(w[:, :, :], src.rearrange("(k p) n -> p k n", p=P)).then_inc(landed, 16)
                sp.dma_start(wb[:, :], a["loraB"]).then_inc(gu_in, 16)

                def load(n, ch):
                    sp.dma_start(hT[:, ch, :, :].rearrange("p k t -> p (k t)"), d["h"][ds(n, 1)].rearrange("n p e -> (n p) e")).then_inc(h_in[ch], 16)

                for ch in range(CPB):
                    load(ch, ch)
                sp.dma_start(wd[:, :, :], a["wdown"].rearrange("(k p) n -> p k n", p=P)).then_inc(wd_in, 16)

                def batch(b, last):
                    for ch in range(CPB):
                        n = b * CPB + ch
                        if not last:
                            sp.wait_ge(gu_ok, (n + 1) * FT)
                            load(n + CPB, ch)
                        sp.wait_ge(chain, 3 * n + 4)
                        sp.dma_start(out[ds(b, 1), ch * CH:(ch + 1) * CH, :].rearrange("b (j p) e -> p (b j) e", p=P),
                                     c.x[:, ds(n * TPC * D, TPC * D)].rearrange("p (j e) -> p j e", e=D)).then_inc(stored, 16)

                with sp.Fori(0, BATCH - 1) as b:
                    batch(b, False)
                batch(BATCH - 1, True)
                sp.wait_ge(stored, 16 * BATCH * CPB)

            @block.gpsimd
            def _(pool):
                def copy(n, ch):
                    pool.wait_ge(turned, n + 1)
                    pool.tensor_copy(at[:, ch, :], c.attn[:, ds(n * TPC * D, TPC * D)]).then_inc(at_ok, 1)

                def batch(b, last):
                    for ch in range(CPB):
                        n = b * CPB + ch
                        if not (last and ch == CPB - 1):
                            copy(n + 1, 1 - ch)
                        rows_rstd(pool, stats_ok, n + 1, rstd[:, :], stats[:, :, 1], EPS, c.power, added, n + 1, rstd_ok, tick_pool)

                copy(0, 0)
                with pool.Fori(0, BATCH - 1) as b:
                    batch(b, False)
                batch(BATCH - 1, True)

            @block.tensor
            def _(pe):
                pe.sem_inc(turned, 2)
                pe.wait_ge(w_in, 32)

                def turn(n, ch):
                    pe.wait_ge(at_ok, n + 1)
                    for j in range(TPC):
                        for k in range(KD):
                            last = pe.transpose(psX[0][:, k, j * P:(j + 1) * P], at[:, ch, j * D + k * P:j * D + (k + 1) * P], c.ident[:, :])
                    last.then_inc(turned, 1)

                def project(n):
                    pe.wait_ge(aT_ok, n + 1)
                    for f in range(KD):
                        for k in range(KD):
                            last = pe.matmul(psX[1][:, f, :], wo[:, k, f * P:(f + 1) * P], aT[:, k, :], start=k == 0, stop=k == KD - 1)
                    last.then_inc(oproj_ok, 1)

                def low_rank(n, b, ch):
                    pe.wait_ge(oT_ok, n + 1)
                    pe.wait_ge(h_in[ch], 16 * (b + 1))
                    for ps, src in ((psM[0], oT), (psM[1], hT[:, ch])):
                        for k in range(KD):
                            last = pe.matmul(ps[0:R, :], wa[:, k, :], src[:, k, :], start=k == 0, stop=k == KD - 1)
                    last.then_inc(low_ok, 1)

                def gate_and_up(n, ch):
                    for f in range(FT):
                        if f > 0:
                            pe.wait_ge(m_ok, FT * n + f)
                        for i in range(2):
                            for k in range(KD):
                                last = pe.matmul(psX[f % 2][:, i, :], wgu[i][:, k, f * P:(f + 1) * P], hT[:, ch, k, :], start=k == 0, stop=i == 1 and k == KD - 1)
                            if i == 0:
                                if f == 0:
                                    pe.wait_ge(g_ok, n + 1)
                                pe.matmul(psX[f % 2][:, 0, :], wb[:, f * P:(f + 1) * P], g[:, :], start=False, stop=True)
                        last.then_inc(gu_ok, 1)

                def down(tiles):
                    for j in tiles:
                        for k in range(FT):
                            last = pe.matmul(psD[:, j * D:(j + 1) * D], mT[:, k, j * P:(j + 1) * P], wd[:, k, :], start=k == 0, stop=k == FT - 1)
                    return last

                def batch(b, last):
                    for ch in range(CPB):
                        n = b * CPB + ch
                        nb, nch = (b, 1) if ch == 0 else (b + 1, 0)
                        more = not (last and ch == CPB - 1)
                        if more:
                            pe.wait_ge(m_ok, FT * (n + 1))
                            turn(n + 1, nch)
                        pe.wait_ge(m_ok, 1 + FT * (n + 1))
                        pe.wait_ge(chain, 3 * n + 1)
                        down(range(0, TPC // 2))
                        if more:
                            project(n + 1)
                        down(range(TPC // 2, TPC)).then_inc(down_ok, 1)
                        if more:
                            low_rank(n + 1, nb, nch)
                            gate_and_up(n + 1, nch)

                turn(0, 0)
                project(0)
                low_rank(0, 0, 0)
                pe.wait_ge(gu_in, 48)
                gate_and_up(0, 0)
                pe.wait_ge(wd_in, 16)
                with pe.Fori(0, BATCH - 1) as b:
                    batch(b, False)
                batch(BATCH - 1, True)

            @block.scalar
            def _(act):
                act.preload_act_table_set("silu_and_others")
                with act.Fori(0, BATCH) as b:
                    for ch in range(CPB):
                        n = b * CPB + ch
                        act.wait_ge(turned, n + 3)
                        act.activation(aT[:, :, :], psX[0][:, :, :], ACT.Copy).then_inc(aT_ok, 1)
                        act.wait_ge(oproj_ok, n + 1)
                        act.activation(oT[:, :, :], psX[1][:, :, :], ACT.Copy).then_inc(oT_ok, 1)
                        act.wait_ge(low_ok, n + 1)
                        act.activation(mod[:, :], psM[0][0:R, :], ACT.Tanh).then_inc(mod_ok, 1)
                        for f in range(FT):
                            act.wait_ge(gu_ok, FT * n + f + 1)
                            act.activation(gate[:, f % 2, :], psX[f % 2][:, 0, :], ACT.Silu).then_inc(silu_ok, 1)

            @block.vector
            def _(dve):
                dve.sem_inc(chain, 1)
                dve.sem_inc(m_ok, 1)

                def modulate(n):
                    dve.wait_ge(mod_ok, n + 1)
                    dve.scalar_tensor_tensor(out=g[:, :], in0=mod[:, :], scalar=0.1, in1=psM[1][0:R, :], op0=ALU.mult, op1=ALU.mult).then_inc(g_ok, 1)

                def product(n, f):
                    dve.wait_ge(silu_ok, FT * n + f + 1)
                    dve.tensor_tensor(mT[:, f, :], gate[:, f % 2, :], psX[f % 2][:, 1, :], ALU.mult).then_inc(m_ok, 1)

                def residual(n):
                    dve.wait_ge(down_ok, n + 1)
                    dve.tensor_tensor(y[:, :], psD[:, :], c.norm[:, ds(n * TPC * D, TPC * D)], ALU.add).then_inc(chain, 1)

                def statistics(n):
                    dve.wait_ge(chain, 1 + 3 * n + 1)
                    row_stats(dve, [y[:, j * D:(j + 1) * D] for j in range(TPC)], sums, stats, summed, n + 1, stats_ok, tick)

                def normalise(n):
                    dve.wait_ge(rstd_ok, n + 1)
                    for j in range(TPC):
                        last = dve.tensor_scalar(normed[:, j * D:(j + 1) * D], y[:, j * D:(j + 1) * D],
                                                 stats[:, j, 0:1], rstd[:, j:j + 1], ALU.subtract, ALU.mult)
                    last.then_inc(chain, 1)

                def update(n):
                    rows = c.x[:, ds(n * TPC * D, TPC * D)]
                    dve.wait_ge(chain, 1 + 3 * n + 2)
                    dve.tensor_tensor(rows, rows, normed[:, :], ALU.add).then_inc(chain, 1)

                def batch(b, last):
                    for ch in range(CPB):
                        n = b * CPB + ch
                        more = not (last and ch == CPB - 1)
                        if more:
                            modulate(n + 1)
                        for f in range(FT):
                            if more:
                                product(n + 1, f)
                            if f < 4:
                                (residual, statistics, normalise, update)[f](n)

                modulate(0)
                for f in range(FT):
                    product(0, f)
                with dve.Fori(0, BATCH - 1) as b:
                    batch(b, False)
                batch(BATCH - 1, True)



def sandwich(nc, a, out):
    with ExitStack() as ctx:
        c = Core(nc, ctx)
        c.x = sbuf(nc, ctx, "x", [P, TILES * D])
        c.norm = sbuf(nc, ctx, "norm", [P, TILES * D])
        c.attn = sbuf(nc, ctx, "attn", [P, TILES * D])
        c.ident = sbuf(nc, ctx, "ident_f32", [P, P])
        c.identb = sbuf(nc, ctx, "ident_bf16", [P, P], BF16)
        c.masks = sbuf(nc, ctx, "masks_bf16", [P, 4, P], BF16)
        c.tau = sbuf(nc, ctx, "tau", [P, 1])
        c.itau = sbuf(nc, ctx, "itau", [P, 3])
        c.power = sbuf(nc, ctx, "power", [P, TPC])
        c.xscale = sbuf(nc, ctx, "xscale", [P, 2])

        def dram(name, shape, dt=F32):
            return nc.dram_tensor(name, shape, dt).ap()

        d = dict(
            q1=dram("q1", [2, BATCH, AQ, PADT], F16), k1=dram("k1", [2, BATCH, AK, PADT], F16),
            v1=dram("v1", [BATCH * G, P, TPB + 1, NB + 1]), m1=dram("m1", [G, 2, 2, HG * TPC, P], F16),
            qk2=[dram(n, [BATCH * G, 3, HD * HG, S], BF16) for n in ("q2", "k2")],
            v2=dram("v2", [BATCH * G, P, TPB, HG, HD + 1]), m2=dram("m2", [G, 2, 3, HG * TPC, P], BF16),
            h=dram("h", [BATCH * CPB, P, KD * CH]))

        with ExitStack() as first:
            c.masksf = sbuf(nc, first, "masks_f32", [P, 4, P])
            phase_load(c, a)
            c.end_phase()
        phase_qkv_first(c, a, d)
        c.end_phase()

        def q1_loads(b, g):
            return [((32 * e + NB * w, 32 * e + NB * w + NB),
                     d["q1"][(0, 1, 0)[e], ds(b, 1), g * 32:(g + 1) * 32, w:w + S].rearrange("b (n h) t -> (b n) h t", h=HG))
                    for e in range(3) for w in range(TAPS)]

        def k1_loads(b, g):
            return [((32 * e + NB * w, 32 * e + NB * w + NB),
                     d["k1"][(0, 0, 1)[e], ds(b, 1), g * NB:(g + 1) * NB, w:w + S].rearrange("b n t -> n b t"))
                    for e in range(3) for w in range(TAPS)]

        def v1_load(b, g):
            return d["v1"][ds(b * G + g, 1), :, 1:, :].rearrange("n p k e -> (n p) k e").unsqueeze(2)

        def consts1(Q, K):
            return [(t[96:98, :, :], a["qbias"]) for t in Q] + [(t[96:100, 0, :], a["kbias"]) for t in K]

        phase_attention(c, "a1", F16, q1_loads, k1_loads, v1_load, d["m1"], consts1, True, NB, 2, 2,
                        c.itau[:, 2:3], -60000.0, c.masks[:, 0, :], c.masks[:, 1, :], AQ)
        c.end_phase()
        phase_out_first(c, a)
        c.end_phase()

        with ExitStack() as mid:
            m = dict(Bp=[sbuf(nc, mid, f"Bp{e}", [P, BATCH * S], BF16) for e in range(3)],
                      dp=sbuf(nc, mid, "dp", [3 * SH, BATCH * S], BF16), dm=sbuf(nc, mid, "dm", [SH, CH], BF16),
                      CT=sbuf(nc, mid, "CT", [P, BATCH * S]), xT=c.attn)
            phase_fp8_and_ssm_inputs(c, a, m)
            c.end_phase()
            phase_ssm(c, a, m)
            c.end_phase()
        phase_qkv_second(c, a, d)
        c.end_phase()

        def q2_loads(b, g):
            return [(rows, d["qk2"][0][ds(b * G + g, 1), 0:e].rearrange("b e (n h) t -> (b e n) h t", h=HG))
                    for rows, e in (((0, 48), 3), ((48, 80), 2), ((80, 96), 1))]

        def k2_loads(b, g):
            return [((16 * i, 16 * i + 16), d["qk2"][1][ds(b * G + g, 1), e].rearrange("b (n h) t -> (b n) h t", h=HG))
                    for i, e in enumerate((0, 0, 0, 1, 1, 2))]

        def v2_load(b, g):
            return d["v2"][ds(b * G + g, 1)].rearrange("n p k h e -> (n p) k h e")

        def consts2(Q, K):
            return [(t[96:99, :, :], a["kones"]) for t in K]

        phase_attention(c, "a2", BF16, q2_loads, k2_loads, v2_load, d["m2"], consts2, False, HD, 0, 3,
                        HD ** -0.5, MASKED, c.masks[:, 2, :], c.masks[:, 3, :], D)
        c.end_phase()
        phase_mlp(c, a, d, out)


def shape_constants():
    r = np.arange(S, dtype=np.float32)
    k, q = np.arange(P)[:, None], np.arange(P)[None, :]
    masks = np.stack([np.where(hidden, np.float32(MASKED), np.float32(0))
                      for hidden in (k >= q, k <= q, k > q, k < q)]).astype(np.float32)
    bias = (S * np.sqrt(TAPS * NB) / (r.astype(np.float64) + 1))
    high = bias.astype(np.float16)
    low = (bias - high).astype(np.float16)
    qbias = np.broadcast_to(np.stack([high, low])[:, None, :], (2, HG, S))
    kbias = np.stack([r / S, r / S, np.ones(S), np.ones(S)]).astype(np.float16)
    return dict(ident=np.eye(P, dtype=np.float32), masks=masks, qbias=np.ascontiguousarray(qbias), kbias=kbias)


def kernel(**inputs):
    import concourse.bacc as bacc
    from concourse.bass_utils import run_bass_kernel_spmd

    i = {k: np.asarray(v) for k, v in inputs.items()}

    def heads_last(w, groups, per):
        return w.reshape(groups, per, -1, w.shape[-1]).transpose(0, 2, 1, 3).reshape(w.shape)

    def column(v):
        return v.reshape(KD, P).T

    arrays = dict(
        x=i["L0_attn_hidden_states"], tau=i["L0_attn_tau"].reshape(1),
        wq1=heads_last(i["L0_attn_Wq"], G, HG).T, wk1=i["L0_attn_Wk"].T, wv1=i["L0_attn_Wv"].T, wo1=i["L0_attn_Wo"].T,
        emb0=i["L0_attn_v_emb0"].reshape(P, 1), emb1=i["L0_attn_v_emb1"].reshape(P, 1),
        wf=i["L0_ffn_weight"].T, wx=i["L1_attn_Wx"], wg=i["L1_attn_Wg"], bg=column(i["L1_attn_bg"]),
        wo3=i["L1_attn_Wo"], ssmA=i["L1_attn_A"].T, skip=column(np.repeat(i["L1_attn_Dp"], SHD)),
        ln1=column(i["L1_ffn_ln1_w"]), ln2=column(i["L1_ffn_ln2_w"]),
        wq2=heads_last(i["L1_ffn_Wq"], G, HG).T, wk2=heads_last(i["L1_ffn_Wk"], G, HG).T,
        wv2=i["L1_ffn_Wv"].T, wo4=i["L1_ffn_Wo"].T, loraA=i["L1_ffn_A"], loraB=i["L1_ffn_B"],
        win=i["L1_ffn_W_in_base"].T, wup=i["L1_ffn_W_up_base"].T, wdown=i["L1_ffn_W_down"].T,
        kones=np.ones((3, HG, S), i["L0_ffn_weight"].dtype), **shape_constants())
    nc = bacc.Bacc("TRN2", target_bir_lowering=False, num_devices=1)
    feed, handles = {}, {}
    for name, v in arrays.items():
        v = np.ascontiguousarray(v)
        feed["in_" + name] = v
        handles[name] = nc.dram_tensor("in_" + name, v.shape, mybir.dt.from_np(v.dtype), kind="ExternalInput").ap()
    out = nc.dram_tensor("out", (BATCH, S, D), F32, kind="ExternalOutput").ap()
    sandwich(nc, handles, out)
    result = run_bass_kernel_spmd(nc, [feed], core_ids=[0])
    return result.results[0]["out"]
```
